# Optimizing a Trainium2 kernel written in Bass

```python
import numpy as np
import jax
import jax.numpy as jnp

def _softmax(x, axis=-1):
    return jax.nn.softmax(x, axis=axis)

def _gelu(x):
    return jax.nn.gelu(x, approximate=True)

def _silu(x):
    return jax.nn.silu(x)

def _sigmoid(x):
    return jax.nn.sigmoid(x)

def _layernorm(x, axis=-1, eps=1e-05):
    m = jnp.mean(x, axis=axis, keepdims=True)
    v = jnp.var(x, axis=axis, keepdims=True)
    return (x - m) / jnp.sqrt(v + eps)

def _scatter_add(tgt, idx, src, axis=0):
    return tgt.at[idx].add(src)

def _segment_sum(src, seg, n):
    return jax.ops.segment_sum(src, seg, n)
kernel_name = 'mk_seq_preln_d2_jaxref_r8_7569d6'

def setup_inputs(seed: int=0):
    np.random.seed(seed)
    _w = jnp.asarray

    def _L0_attn_setup():
        import jax, jax.numpy as jnp
        import numpy as np
        BLOCK = 32
        EPS = 1e-06

        def _silu(x):
            return x * jax.nn.sigmoid(x)
        key = jax.random.key(seed)
        k1, k2, k3, k4 = jax.random.split(key, 4)
        embed_dim, hidden_dim = (256, 256)
        b, n, h = (2, 512, 16)
        x = jax.random.normal(k1, (b, n, embed_dim), dtype=jnp.float32)
        slope_rate = jax.random.uniform(k2, (h, 1, 1), dtype=jnp.float32, minval=0.01, maxval=1.0)
        W_qkvu = jax.random.normal(k3, (4 * hidden_dim, embed_dim), dtype=jnp.float32) / np.sqrt(embed_dim)
        W_out = jax.random.normal(k4, (embed_dim, hidden_dim), dtype=jnp.float32) / np.sqrt(hidden_dim)
        return {'x': x, 'slope_rate': slope_rate, 'W_qkvu': W_qkvu, 'W_out': W_out}
    _L0_attn_in = _L0_attn_setup()

    def _L0_ffn_setup():
        import jax, jax.numpy as jnp
        import numpy as np
        HIDDEN = 256
        INTER = 1024
        SCALE = 64.0

        def fwht(x):
            orig_shape = x.shape
            n = orig_shape[-1]
            x = x.reshape(-1, n)
            h = 1
            while h < n:
                x = x.reshape(-1, n // (2 * h), 2, h)
                a, b = (x[:, :, 0, :], x[:, :, 1, :])
                x = jnp.stack([a + b, a - b], axis=2).reshape(-1, n)
                h *= 2
            return (x / jnp.sqrt(jnp.asarray(n, x.dtype))).reshape(orig_shape)
        key = jax.random.key(seed)
        ks = jax.random.split(key, 8)
        inp = jax.random.normal(ks[0], (4, 256, HIDDEN), dtype=jnp.float32)
        SU_ug = jnp.where(jax.random.bernoulli(ks[1], 0.5, (HIDDEN,)), 1.0, -1.0).astype(jnp.float32)
        SU_dp = jnp.where(jax.random.bernoulli(ks[2], 0.5, (INTER,)), 1.0, -1.0).astype(jnp.float32)
        Wscale_ug = jax.random.uniform(ks[3], (2 * INTER,), jnp.float32, 0.5, 1.5)
        Wscale_dp = jax.random.uniform(ks[4], (HIDDEN,), jnp.float32, 0.5, 1.5)
        W_up = jax.random.normal(ks[5], (INTER, HIDDEN), dtype=jnp.float32) * 0.02
        W_gate = jax.random.normal(ks[6], (INTER, HIDDEN), dtype=jnp.float32) * 0.02
        W_down = jax.random.normal(ks[7], (HIDDEN, INTER), dtype=jnp.float32) * 0.02
        return {'input': inp, 'SU_ug': SU_ug, 'SU_dp': SU_dp, 'Wscale_ug': Wscale_ug, 'Wscale_dp': Wscale_dp, 'W_up': W_up, 'W_gate': W_gate, 'W_down': W_down}
    _L0_ffn_in = _L0_ffn_setup()

    def _L1_attn_setup():
        import jax, jax.numpy as jnp
        import numpy as np
        B, S, H = (16, 64, 256)
        NH, NKV = (16, 4)
        HD = H // NH

        def _rope_tables(seq_len, dim, dtype):
            inv_freq = 1.0 / 10000.0 ** (jnp.arange(0, dim, 2, dtype=jnp.float32) / dim)
            t = jnp.arange(seq_len, dtype=jnp.float32)
            freqs = jnp.einsum('i,j->ij', t, inv_freq)
            emb = jnp.concatenate([freqs, freqs], axis=-1)
            cos = jnp.cos(emb)[None, None].astype(dtype)
            sin = jnp.sin(emb)[None, None].astype(dtype)
            return (cos, sin)

        def _rotate_half(x):
            x1, x2 = jnp.split(x, 2, axis=-1)
            return jnp.concatenate([-x2, x1], axis=-1)
        key = jax.random.key(seed)
        kx, kq, kk, kv, ko = jax.random.split(key, 5)
        x = jax.random.normal(kx, (B, S, H), dtype=jnp.float32)
        s = 0.02
        Wq = jax.random.normal(kq, (H, H), dtype=jnp.float32) * s
        Wk = jax.random.normal(kk, (NKV * HD, H), dtype=jnp.float32) * s
        Wv = jax.random.normal(kv, (NKV * HD, H), dtype=jnp.float32) * s
        Wo = jax.random.normal(ko, (H, H), dtype=jnp.float32) * s
        return {'x': x, 'Wq': Wq, 'Wk': Wk, 'Wv': Wv, 'Wo': Wo}
    _L1_attn_in = _L1_attn_setup()

    def _L1_ffn_setup():
        import jax, jax.numpy as jnp
        import numpy as np
        EPS = 1e-05
        ROPE_BASE = 150000.0
        NHEADS = 32
        KVHEADS = 8
        HEAD_DIM = 64
        TOP_K = 4

        def _rms(x, w):
            return x * jax.lax.rsqrt(jnp.mean(x * x, -1, keepdims=True) + EPS) * w

        def _rope(q, k):
            S, hd = (q.shape[1], q.shape[-1])
            half = hd // 2
            inv = 1.0 / ROPE_BASE ** (jnp.arange(half, dtype=jnp.float32) / half)
            ang = jnp.arange(S, dtype=jnp.float32)[:, None] * inv
            cos = jnp.concatenate([jnp.cos(ang), jnp.cos(ang)], -1)[None, :, None, :]
            sin = jnp.concatenate([jnp.sin(ang), jnp.sin(ang)], -1)[None, :, None, :]

            def rot(t):
                t1, t2 = (t[..., :half], t[..., half:])
                return jnp.concatenate([-t2, t1], -1)
            return (q * cos + rot(q) * sin, k * cos + rot(k) * sin)
        key = jax.random.key(seed)
        ks = jax.random.split(key, 12)
        B, S, D, H, E = (1, 128, 256, 256, 16)
        s = 0.02
        return {'x': jax.random.normal(ks[0], (B, S, D), jnp.float32), 'ln_w': jnp.ones((D,), jnp.float32), 'ff_ln_w': jnp.ones((D,), jnp.float32), 'wq': jax.random.normal(ks[1], (D, NHEADS * HEAD_DIM), jnp.float32) * s, 'wk': jax.random.normal(ks[2], (D, KVHEADS * HEAD_DIM), jnp.float32) * s, 'wv': jax.random.normal(ks[3], (D, KVHEADS * HEAD_DIM), jnp.float32) * s, 'wo': jax.random.normal(ks[4], (NHEADS * HEAD_DIM, D), jnp.float32) * s, 'wg': jax.random.normal(ks[5], (D, E), jnp.float32) * s, 'w1': jax.random.normal(ks[6], (E, D, H), jnp.float32) * s, 'w3': jax.random.normal(ks[7], (E, D, H), jnp.float32) * s, 'w2': jax.random.normal(ks[8], (E, H, D), jnp.float32) * s}
    _L1_ffn_in = _L1_ffn_setup()
    _d = {'L0_attn_x': _L0_attn_in['x'], 'L0_attn_slope_rate': _L0_attn_in['slope_rate'], 'L0_attn_W_qkvu': _L0_attn_in['W_qkvu'], 'L0_attn_W_out': _L0_attn_in['W_out'], 'L0_ffn_SU_ug': _L0_ffn_in['SU_ug'], 'L0_ffn_SU_dp': _L0_ffn_in['SU_dp'], 'L0_ffn_Wscale_ug': _L0_ffn_in['Wscale_ug'], 'L0_ffn_Wscale_dp': _L0_ffn_in['Wscale_dp'], 'L0_ffn_W_up': _L0_ffn_in['W_up'], 'L0_ffn_W_gate': _L0_ffn_in['W_gate'], 'L0_ffn_W_down': _L0_ffn_in['W_down'], 'L1_attn_Wq': _L1_attn_in['Wq'], 'L1_attn_Wk': _L1_attn_in['Wk'], 'L1_attn_Wv': _L1_attn_in['Wv'], 'L1_attn_Wo': _L1_attn_in['Wo'], 'L1_ffn_ln_w': _L1_ffn_in['ln_w'], 'L1_ffn_ff_ln_w': _L1_ffn_in['ff_ln_w'], 'L1_ffn_wq': _L1_ffn_in['wq'], 'L1_ffn_wk': _L1_ffn_in['wk'], 'L1_ffn_wv': _L1_ffn_in['wv'], 'L1_ffn_wo': _L1_ffn_in['wo'], 'L1_ffn_wg': _L1_ffn_in['wg'], 'L1_ffn_w1': _L1_ffn_in['w1'], 'L1_ffn_w3': _L1_ffn_in['w3'], 'L1_ffn_w2': _L1_ffn_in['w2']}
    _x0 = _d['L0_attn_x']
    _d['L0_attn_x'] = jax.random.normal(jax.random.fold_in(jax.random.key(seed), 1), (4, 512, 256), dtype=_x0.dtype)
    del _x0
    return _d

def reference(L0_attn_x, L0_attn_slope_rate, L0_attn_W_qkvu, L0_attn_W_out, L0_ffn_SU_ug, L0_ffn_SU_dp, L0_ffn_Wscale_ug, L0_ffn_Wscale_dp, L0_ffn_W_up, L0_ffn_W_gate, L0_ffn_W_down, L1_attn_Wq, L1_attn_Wk, L1_attn_Wv, L1_attn_Wo, L1_ffn_ln_w, L1_ffn_ff_ln_w, L1_ffn_wq, L1_ffn_wk, L1_ffn_wv, L1_ffn_wo, L1_ffn_wg, L1_ffn_w1, L1_ffn_w3, L1_ffn_w2):

    def _L0_attn_ref(x, slope_rate, W_qkvu, W_out):
        import jax, jax.numpy as jnp
        import numpy as np
        BLOCK = 32
        EPS = 1e-06

        def _silu(x):
            return x * jax.nn.sigmoid(x)
        b, n, embed_dim = x.shape
        h = slope_rate.shape[0]
        hidden_dim = W_qkvu.shape[0] // 4
        d = hidden_dim // h
        NB = n // BLOCK
        qkvu = x @ W_qkvu.T
        q, k, v, u = jnp.split(qkvu, 4, axis=-1)

        def to_heads(t):
            return t.reshape(b, n, h, d).transpose(0, 2, 1, 3)
        q = _silu(to_heads(q))
        k = _silu(to_heads(k))
        v = to_heads(v)
        s = slope_rate
        arr = jnp.arange(1, BLOCK + 1, dtype=x.dtype)
        q_decay = jnp.exp(-s * arr[:, None])
        k_decay = jnp.exp(-s * (BLOCK - arr[:, None]))
        idx = arr[:, None] - arr[None, :]
        diag_decay = jnp.exp(jnp.where(idx >= 0, -s * idx, -jnp.inf))
        block_decay = jnp.exp(-s * BLOCK)

        def blk(t):
            return t.reshape(b, h, NB, BLOCK, d).transpose(2, 0, 1, 3, 4)
        qb, kb, vb = (blk(q), blk(k), blk(v))

        def step(kv, inp):
            qi, ki, vi = inp
            qkv_none_diag = jnp.einsum('bhmd,bhde->bhme', qi * q_decay, kv)
            qk = jnp.einsum('bhmd,bhsd->bhms', qi, ki) * diag_decay
            qkv_diag = jnp.einsum('bhms,bhse->bhme', qk, vi)
            kv_new = block_decay * kv + jnp.einsum('bhsd,bhse->bhde', ki * k_decay, vi)
            return (kv_new, qkv_none_diag + qkv_diag)
        kv0 = jnp.zeros((b, h, d, d), dtype=jnp.float32)
        _, outs = jax.lax.scan(step, kv0, (qb, kb, vb))
        o = outs.transpose(1, 2, 0, 3, 4).reshape(b, h, n, d)
        o = o.transpose(0, 2, 1, 3).reshape(b, n, hidden_dim)
        o = o * jax.lax.rsqrt(jnp.mean(o * o, axis=-1, keepdims=True) + EPS)
        o = u * o
        return o @ W_out.T

    def _L0_ffn_ref(input, SU_ug, SU_dp, Wscale_ug, Wscale_dp, W_up, W_gate, W_down):
        import jax, jax.numpy as jnp
        import numpy as np
        HIDDEN = 256
        INTER = 1024
        SCALE = 64.0

        def fwht(x):
            orig_shape = x.shape
            n = orig_shape[-1]
            x = x.reshape(-1, n)
            h = 1
            while h < n:
                x = x.reshape(-1, n // (2 * h), 2, h)
                a, b = (x[:, :, 0, :], x[:, :, 1, :])
                x = jnp.stack([a + b, a - b], axis=2).reshape(-1, n)
                h *= 2
            return (x / jnp.sqrt(jnp.asarray(n, x.dtype))).reshape(orig_shape)
        n = SU_ug.shape[0]
        x = input.reshape(-1, n)
        x = fwht(x * SU_ug) / SCALE
        x_up = x @ W_up.T * (Wscale_ug[:INTER] * SCALE)
        x_gate = x @ W_gate.T * (Wscale_ug[INTER:] * SCALE)
        x = jax.nn.silu(x_gate) * x_up
        x = fwht(x * SU_dp) / SCALE
        x = x @ W_down.T * (Wscale_dp * SCALE)
        return x.reshape(input.shape)

    def _L1_attn_ref(x, Wq, Wk, Wv, Wo):
        import jax, jax.numpy as jnp
        import numpy as np
        B, S, H = (16, 64, 256)
        NH, NKV = (16, 4)
        HD = H // NH

        def _rope_tables(seq_len, dim, dtype):
            inv_freq = 1.0 / 10000.0 ** (jnp.arange(0, dim, 2, dtype=jnp.float32) / dim)
            t = jnp.arange(seq_len, dtype=jnp.float32)
            freqs = jnp.einsum('i,j->ij', t, inv_freq)
            emb = jnp.concatenate([freqs, freqs], axis=-1)
            cos = jnp.cos(emb)[None, None].astype(dtype)
            sin = jnp.sin(emb)[None, None].astype(dtype)
            return (cos, sin)

        def _rotate_half(x):
            x1, x2 = jnp.split(x, 2, axis=-1)
            return jnp.concatenate([-x2, x1], axis=-1)
        b, s, _ = x.shape
        scaling = HD ** (-0.5)
        q = jnp.einsum('bsh,oh->bso', x, Wq).reshape(b, s, NH, HD).transpose(0, 2, 1, 3)
        k = jnp.einsum('bsh,oh->bso', x, Wk).reshape(b, s, NKV, HD).transpose(0, 2, 1, 3)
        v = jnp.einsum('bsh,oh->bso', x, Wv).reshape(b, s, NKV, HD).transpose(0, 2, 1, 3)
        cos, sin = _rope_tables(s, HD, x.dtype)
        q = q * cos + _rotate_half(q) * sin
        k = k * cos + _rotate_half(k) * sin
        rep = NH // NKV
        k = jnp.repeat(k, rep, axis=1)
        v = jnp.repeat(v, rep, axis=1)
        scores = jnp.einsum('bhqd,bhkd->bhqk', q, k) * scaling
        attn = jax.nn.softmax(scores, axis=-1)
        out = jnp.einsum('bhqk,bhkd->bhqd', attn, v)
        out = out.transpose(0, 2, 1, 3).reshape(b, s, H)
        return jnp.einsum('bsh,oh->bso', out, Wo)

    def _L1_ffn_ref(x, ln_w, ff_ln_w, wq, wk, wv, wo, wg, w1, w3, w2):
        import jax, jax.numpy as jnp
        import numpy as np
        EPS = 1e-05
        ROPE_BASE = 150000.0
        NHEADS = 32
        KVHEADS = 8
        HEAD_DIM = 64
        TOP_K = 4

        def _rms(x, w):
            return x * jax.lax.rsqrt(jnp.mean(x * x, -1, keepdims=True) + EPS) * w

        def _rope(q, k):
            S, hd = (q.shape[1], q.shape[-1])
            half = hd // 2
            inv = 1.0 / ROPE_BASE ** (jnp.arange(half, dtype=jnp.float32) / half)
            ang = jnp.arange(S, dtype=jnp.float32)[:, None] * inv
            cos = jnp.concatenate([jnp.cos(ang), jnp.cos(ang)], -1)[None, :, None, :]
            sin = jnp.concatenate([jnp.sin(ang), jnp.sin(ang)], -1)[None, :, None, :]

            def rot(t):
                t1, t2 = (t[..., :half], t[..., half:])
                return jnp.concatenate([-t2, t1], -1)
            return (q * cos + rot(q) * sin, k * cos + rot(k) * sin)
        B, S, D = x.shape
        h = _rms(x, ln_w)
        q = (h @ wq).reshape(B, S, NHEADS, HEAD_DIM)
        k = (h @ wk).reshape(B, S, KVHEADS, HEAD_DIM)
        v = (h @ wv).reshape(B, S, KVHEADS, HEAD_DIM)
        q, k = _rope(q, k)
        g = NHEADS // KVHEADS
        k = jnp.repeat(k, g, axis=2)
        v = jnp.repeat(v, g, axis=2)
        scores = jnp.einsum('bqhd,bkhd->bhqk', q, k) / np.float32(np.sqrt(HEAD_DIM))
        causal = jnp.tril(jnp.ones((S, S), bool))
        scores = jnp.where(causal[None, None], scores, jnp.float32(-1e+30))
        attn = jax.nn.softmax(scores, -1)
        o = jnp.einsum('bhqk,bkhd->bqhd', attn, v).reshape(B, S, NHEADS * HEAD_DIM)
        x = x + o @ wo
        h = _rms(x, ff_ln_w)
        logits = h @ wg
        topv, topi = jax.lax.top_k(logits, TOP_K)
        gate = jax.nn.softmax(topv, -1)
        bidx = jnp.arange(B)[:, None, None]
        sidx = jnp.arange(S)[None, :, None]
        weights = jnp.zeros_like(logits).at[bidx, sidx, topi].set(gate)
        a = jax.nn.silu(jnp.einsum('bsd,edh->bseh', h, w1)) * jnp.einsum('bsd,edh->bseh', h, w3)
        y = jnp.einsum('bseh,ehd->bsed', a, w2)
        moe = jnp.einsum('bsed,bse->bsd', y, weights)
        return x + moe
    x = L0_attn_x
    x = x + _L0_attn_ref(_layernorm(x, axis=-1), L0_attn_slope_rate, L0_attn_W_qkvu, L0_attn_W_out)
    x = x + _L0_ffn_ref(_layernorm(x, axis=-1), L0_ffn_SU_ug, L0_ffn_SU_dp, L0_ffn_Wscale_ug, L0_ffn_Wscale_dp, L0_ffn_W_up, L0_ffn_W_gate, L0_ffn_W_down)
    x = x + _L1_attn_ref(_layernorm(x, axis=-1), L1_attn_Wq, L1_attn_Wk, L1_attn_Wv, L1_attn_Wo)
    x = x + _L1_ffn_ref(_layernorm(x, axis=-1), L1_ffn_ln_w, L1_ffn_ff_ln_w, L1_ffn_wq, L1_ffn_wk, L1_ffn_wv, L1_ffn_wo, L1_ffn_wg, L1_ffn_w1, L1_ffn_w3, L1_ffn_w2)
    return x

_drawn_inputs = setup_inputs


def setup_inputs(seed=0):
    import zlib

    import numpy as np

    out = dict(_drawn_inputs(seed))
    spreads = {'L1_ffn_ln_w': (1.0, 0.6), 'L1_ffn_ff_ln_w': (1.0, 0.6)}
    factors = {'L0_ffn_Wscale_ug': 5.604,
     'L0_ffn_Wscale_dp': 7.725,
     'L1_attn_Wq': 8.0,
     'L1_attn_Wk': 8.0,
     'L1_attn_Wv': 8.0,
     'L1_attn_Wo': 8.0,
     'L1_ffn_wq': 8.0,
     'L1_ffn_wk': 8.0,
     'L1_ffn_wv': 3.958,
     'L1_ffn_wo': 3.933,
     'L1_ffn_wg': 8.0,
     'L1_ffn_w1': 8.0,
     'L1_ffn_w3': 8.0,
     'L1_ffn_w2': 8.0}
    for name, (base, spread) in spreads.items():
        noise = np.random.default_rng([zlib.crc32(name.encode()), seed]).standard_normal(out[name].shape)
        drawn = base * np.exp(spread * noise) if base else spread * noise
        out[name] = jnp.asarray(drawn.astype(out[name].dtype))
    for name, factor in factors.items():
        out[name] = (out[name] * factor).astype(out[name].dtype)
    return out
```

```python
from contextlib import ExitStack

import concourse.bass as bass
from concourse import mybir

ALU = mybir.AluOpType
ACT = mybir.ActivationFunctionType
AX = mybir.AxisListType.X
F32 = mybir.dt.float32
BF16 = mybir.dt.bfloat16

P = 128
D = 256
DC = D // P
B, S = 4, 512
TB = S // P
NT = B * TB
INTER = 1024
IC = INTER // P
H16, HD16 = 16, 16
KV16 = 4
G64, R64, HD64 = 8, 4, 64
E, TOPK, EH = 16, 4, 256
QKV = 384

CONST_COLS = {}
_at = 0
for _name, _n in (("ident", P), ("lag", P), ("ge", P), ("causal", P), ("block", P), ("ramp", P), ("left", 1),
                  ("parity", 2), ("cos16", TB * HD16), ("sin16", TB * HD16), ("cos64", TB * HD64),
                  ("sin64", TB * HD64)):
    CONST_COLS[_name] = (_at, _at + _n)
    _at += _n
NCONST = _at


class Region:

    def __init__(self, tensor):
        self.tensor, self.at = tensor, 0

    def reuse(self):
        self.at = 0

    def take(self, *shape):
        n = 1
        for s in shape:
            n *= s
        v = self.tensor[:, self.at:self.at + n]
        self.at += n
        assert self.at <= self.tensor.shape[1], (self.at, self.tensor.shape)
        dims = "abc"[:len(shape)]
        if len(shape) == 1:
            return v
        return v.rearrange(f"p ({' '.join(dims)}) -> p {' '.join(dims)}", **dict(zip(dims, shape)))


class Count:

    def __init__(self, sem, per_round=0, start=0):
        self.sem, self.per_round, self.n, self.start = sem, per_round, 0, start

    def inc(self, ins):
        ins.then_inc(self.sem, 1)
        self.n += 1

    def wait(self, eng, rnd=0):
        eng.wait_ge(self.sem, rnd * self.per_round + self.n + self.start)


def two_layers(nc, x_in, slope, W_qkvu, W_out0, SU_ug, SU_dp, Wscale_ug, Wscale_dp, W_up, W_gate, W_down,
               Wq1, Wk1, Wv1, Wo1, ln_w, ff_ln_w, wq, wk, wv, wo, wg, w1, w3, w2, consts, out):
    ctx = ExitStack()
    with ctx:
        def sb(name, shape, dt=F32):
            return ctx.enter_context(nc.sbuf_tensor(name, shape, dt))

        def sem(name):
            return ctx.enter_context(nc.semaphore(name))

        bank = [ctx.enter_context(nc.psum_tensor(f"bank{i}", [P, 512], F32)) for i in range(8)]

        x = sb("x", [P, NT, D])
        con = sb("con", [P, NCONST])

        def const(name):
            a, b = CONST_COLS[name]
            return con[:, a:b]

        ident = const("ident")
        wqkvuT = sb("wqkvuT", [P, DC, 4 * D])
        wout0T = sb("wout0T", [P, DC, D])
        wugT = sb("wugT", [P, DC, 2 * INTER])
        wdT = sb("wdT", [P, IC, D])
        wqkv1T = sb("wqkv1T", [P, DC, QKV])
        wo1T = sb("wo1T", [P, DC, D])
        late = Region(sb("late", [P, DC * G64 * QKV + 2 * G64 * D]))
        wgrp = late.take(DC, G64, QKV)
        wo_sb = late.take(2 * G64, D)
        late.reuse()
        wg_sb = sb("wg_sb", [P, DC, E])
        su_ug = sb("su_ug", [P, DC])
        su_dp = sb("su_dp", [P, IC])
        ws_ug = sb("ws_ug", [P, 2 * IC])
        ws_dp = sb("ws_dp", [P, DC])
        lnw = sb("lnw", [P, DC])
        fflnw = sb("fflnw", [P, DC])

        NATB = 15
        wnat = late.take(NATB, D)
        early = Region(sb("early", [P, 40 * D + 10368]))
        wugd = early.take(24, D)
        pong = early.take(16, D)

        st = sb("st", [P, NT, 6])
        mv = sb("mv", [P, NT, 2])
        var = sb("var", [P, NT])
        std = sb("std", [P, NT])
        rstd = sb("rstd", [P, NT])
        xn = sb("xn", [P, NT, D])
        hn = wugT[:].rearrange("p c (t d) -> p (c t) d", d=D)
        xn_st = sb("xn_st", [P, TB, D])
        xnT = sb("xnT", [P, DC, S])

        ld_c, ld_x, ld_w, ld_ug, ld_s, ld_l1, ld_l2 = (sem(n) for n in (
            "ld_c", "ld_x", "ld_w", "ld_ug", "ld_s", "ld_l1", "ld_l2"))
        v_chain = sem("v_chain")
        ln_var, ln_std = sem("ln_var"), sem("ln_std")
        xn_all = sem("xn_all")
        wt_ps = sem("wt_ps")
        wt_sb = [sem("wt_sb_dve"), sem("wt_sb_act")]
        fw_chain, fw_done = sem("fw_chain"), sem("fw_done")
        stored = sem("stored")

        mid = CONST_COLS.get

        slope_b = sb("slope_b", [P, H16])
        nslope_b = sb("nslope_b", [P, H16])
        slope_p = sb("slope_p", [P, DC])
        nslope_p = sb("nslope_p", [P, DC])
        DT = late.take(H16, P)
        QD = early.take(DC, P)
        KD = early.take(H16)
        BD = early.take(DC)
        qT = early.take(DC, S)
        qdT = early.take(DC, S)
        kT = early.take(DC, S)
        kTm = early.take(2, DC, S)
        ks = early.take(2, D)
        kd = early.take(TB, D)
        v0 = early.take(TB, D)
        u0 = early.take(TB, D)
        PT0 = late.take(2, H16, P)
        kvs = early.take(DC, P)
        kvt = ks[:, 1, :].rearrange("p (c e) -> p c e", c=DC)
        ou = early.take(TB, D)
        osq = ks[:, 0, :]
        ouT = kT
        ss = early.take(NT)
        y0 = xn

        def head_of(slot):
            g, r = slot // 4, slot % 4
            return 8 * (r // 2) + 2 * g + r % 2

        dec_exp = sem("dec_exp")
        l0 = {n: sem("l0_" + n) for n in ("stage", "xT_ps", "xT_sb", "qk_ps", "q_sb", "kv_ps", "k_sb", "v_sb", "u_ps",
                                          "u_sb", "kTm", "kd", "s_ps", "pt", "o_ps", "st_ps", "st", "ou", "sq",
                                          "ouT_ps", "ouT_sb", "y_ps", "y_sb", "chain", "qd")}
        rms_in, rms_std = sem("rms_in"), sem("rms_std")

        early.reuse()
        early.take(40, D)
        gsil = early.take(2, S)
        aT = early.take(IC, S)
        f0 = {n: sem("f0_" + n) for n in ("stage", "xT_ps", "xT_sb", "up", "silu", "glu", "y_ps", "y")}

        early.reuse()
        causal = sb("causal", [P, P], BF16)
        ident_h = sb("ident_h", [P, P], BF16)
        t1 = early.take(2, 320)
        t2 = early.take(2, 320)
        qk = early.take(2, 512)
        probs = early.take(3, S)
        probsT = early.take(2, S)
        negmax = early.take(64)
        rowsum = early.take(64)
        rinv = early.take(64)
        on = early.take(2, D)
        onT = early.take(2, DC, P)
        narrow_qT = early.take(2, DC, S)
        narrow_kT = early.take(DC, S)
        narrow_v = early.take(1, TB, KV16 * HD16)
        wide_qT = early.take(2, DC, S)
        wide_kT = early.take(2, S)
        wide_v = early.take(2, TB, HD64)
        par4 = early.take(2)

        class Attention:

            names = ("stage", "xT_ps", "xT_sb", "qkv_ps", "rope", "yb", "qk", "m_ps", "m_sb", "s_ps", "max", "exp", "t_ps",
                     "pt_dve", "pt_act", "pv", "on", "y_ps", "chain")

            def __init__(self, name, heads, hd, causal):
                self.heads, self.hd, self.causal = heads, hd, causal
                self.rows, self.units = TB, TB * heads
                self.sem = {n: sem(f"{name}_{n}") for n in self.names}

            def keys(self, row):
                return row + 1 if self.causal else TB

            def row_of(self, j):
                return j // self.heads

            def events(self, prefetch):
                ev = {}
                for r in range(self.rows):
                    last = (r + 1) * self.heads - 1
                    ev.setdefault(last + 4, []).append(("turn_row", r))
                    ev.setdefault(last + 5, []).append(("project", r))
                if prefetch:
                    n = self.units
                    for slot, e in zip((1, 2, 5, 6, 9, 10, 13, 14), QKV_EVENTS):
                        ev.setdefault(slot, []).append(e)
                return ev

        QKV_EVENTS = (("qkv", 0), ("qkv", 1), ("turn_qk", 0), ("qkv", 2), ("turn_qk", 1), ("qkv", 3), ("turn_qk", 2),
                      ("turn_qk", 3))
        a1 = Attention("a1", H16, HD16, False)
        a2 = Attention("a2", R64, HD64, True)
        SBANK, PTBANK, OBANK, MBANK, YBANK = (0, 1, 2), (3, 4), 5, 6, 7
        A1_EV = 2 * TB
        A2_EV = TB + G64 * 2 * TB - TB
        LAG_T, LAG_PV = 2, 3

        early.reuse()
        hT5 = early.take(DC, B * S)
        w13 = early.take(2, 2 * DC, EH)
        w2s = early.take(2, DC, D)
        gs5 = early.take(2, S)
        aT5 = early.take(4, S).rearrange("p (u c) n -> p u c n", u=2)
        logits = early.take(NT, E)
        gate = early.take(NT, E)
        above = early.take(NT, E)
        ties = early.take(NT, E)
        run_a = early.take(NT, E)
        run_b = early.take(NT, E)
        best = early.take(NT, 8)
        room = sb("room", [P, NT])
        gcol = early.take(2, NT)
        m5 = {n: sem("m5_" + n) for n in ("hT_ps", "hT_sb", "lg_ps", "exp", "shift", "silu", "glu", "up_ps", "y_ps", "acc",
                                          "gcol")}
        ld_e = [sem("ld_e0"), sem("ld_e1")]

        block = ctx.enter_context(nc.Block())

        def start_turns():
            for c in range(DC):
                for blocks, dst in ((range(0, 4), wqkvuT[:, c, 0:512]), (range(4, 8), wqkvuT[:, c, 512:1024]),
                                    (range(8, 10), wout0T[:, c, :]), (range(10, 13), wqkv1T[:, c, :]),
                                    (range(13, 15), wo1T[:, c, :])):
                    yield c, list(blocks), dst

        START = list(start_turns())
        FFN = [(c, list(range(4 * g, 4 * g + 4)), wugT[:, c, 512 * g:512 * g + 512], su_ug[:, c:c + 1])
               for g in range(4) for c in range(DC)]
        FFN += [(k % 2, [16 + k // 2, 20 + k // 2], wdT[:, k, :], su_dp[:, k:k + 1]) for k in range(IC)]

        @block.sync
        def _(sync):
            sync.dma_start(con[:], consts).then_inc(ld_c, 16)
            sync.dma_start(wnat[:, 0:8, :], W_qkvu.rearrange("(n p) d -> p n d", p=P)).then_inc(ld_w, 16)
            xv = x_in.rearrange("b (t p) d -> p (b t) d", p=P)
            for b in range(B):
                sync.dma_start(x[:, TB * b:TB * b + TB, :], xv[:, TB * b:TB * b + TB, :]).then_inc(ld_x, 16)
            sync.dma_start(slope_b[:], slope.rearrange("h a b -> (a b h)").partition_broadcast(P)).then_inc(ld_s, 16)
            for h in range(H16):
                sync.dma_start(slope_p[HD16 * (h % 8):HD16 * (h % 8) + HD16, h // 8:h // 8 + 1],
                               slope[h, :, 0].partition_broadcast(HD16)).then_inc(ld_s, 16)
            sync.dma_start(wnat[:, 8:10, :], W_out0.rearrange("(n p) d -> p n d", p=P)).then_inc(ld_w, 16)
            sync.dma_start(wnat[:, 10:12, :], Wq1.rearrange("(n p) d -> p n d", p=P)).then_inc(ld_w, 16)
            sync.dma_start(wnat[0:64, 12, :], Wk1).then_inc(ld_w, 16)
            sync.dma_start(wnat[64:128, 12, :], Wv1).then_inc(ld_w, 16)
            sync.dma_start(wnat[:, 13:15, :], Wo1.rearrange("(n p) d -> p n d", p=P)).then_inc(ld_w, 16)
            sync.dma_start(wugd[:, 0:8, :], W_up.rearrange("(n p) d -> p n d", p=P)).then_inc(ld_ug, 16)
            sync.dma_start(wugd[:, 8:16, :], W_gate.rearrange("(n p) d -> p n d", p=P)).then_inc(ld_ug, 16)
            sync.dma_start(wugd[:, 16:24, :], W_down.rearrange("(r p) (m d) -> p r m d", p=P, d=D)).then_inc(ld_ug, 16)
            sync.dma_start(ws_ug[:], Wscale_ug.rearrange("(n p) -> p n", p=P), allow_slow_non_contiguous=True).then_inc(ld_ug, 16)
            sync.dma_start(ws_dp[:], Wscale_dp.rearrange("(n p) -> p n", p=P), allow_slow_non_contiguous=True).then_inc(ld_ug, 16)
            sync.dma_start(su_ug[:], SU_ug.rearrange("(n p) -> p n", p=P), allow_slow_non_contiguous=True).then_inc(ld_ug, 16)
            sync.dma_start(su_dp[:], SU_dp.rearrange("(n p) -> p n", p=P), allow_slow_non_contiguous=True).then_inc(ld_ug, 16)
            sync.dma_start(lnw[:], ln_w.rearrange("(n p) -> p n", p=P), allow_slow_non_contiguous=True).then_inc(ld_l1, 16)
            sync.dma_start(fflnw[:], ff_ln_w.rearrange("(n p) -> p n", p=P), allow_slow_non_contiguous=True).then_inc(ld_l1, 16)
            sync.dma_start(wg_sb[:], wg.rearrange("(c p) e -> p c e", p=P)).then_inc(ld_l1, 16)
            sync.wait_ge(rms_in, 1)
            for c in range(DC):
                rows = slice(P * c, P * c + P)
                sync.dma_start(wgrp[:, c, :, 0:256], wq[rows, :].rearrange("p (g n) -> p g n", g=G64)).then_inc(ld_l1, 16)
                sync.dma_start(wgrp[:, c, :, 256:320], wk[rows, :].rearrange("p (g n) -> p g n", g=G64)).then_inc(ld_l1, 16)
                sync.dma_start(wgrp[:, c, :, 320:384], wv[rows, :].rearrange("p (g n) -> p g n", g=G64)).then_inc(ld_l1, 16)
            sync.dma_start(wo_sb[:], wo.rearrange("(k p) d -> p k d", p=P)).then_inc(ld_l1, 16)
            def load_expert(e, half):
                w = lambda a: a[bass.ds(e, 1), :, :].rearrange("e (c p) h -> p (e c) h", p=P)
                sync.dma_start(w13[:, half, 0:DC, :], w(w1)).then_inc(ld_e[half], 16)
                sync.dma_start(w13[:, half, DC:2 * DC, :], w(w3)).then_inc(ld_e[half], 16)
                sync.dma_start(w2s[:, half, :, :], w(w2)).then_inc(ld_e[half], 16)

            sync.wait_ge(ln_var, 6)
            load_expert(0, 0)
            load_expert(1, 1)
            with sync.Fori(1, E // 2) as pair:
                for half in range(2):
                    sync.wait_ge(m5["y_ps"], (pair - 1) * 4 * B + 2 * B * (half + 1))
                    load_expert(pair * 2 + half, half)
            sync.wait_ge(stored, 1)
            ov = out.rearrange("b (t p) d -> p (b t) d", p=P)
            sync.dma_start(ov, x[:]).then_inc(ld_x, 16)
            sync.wait_ge(ld_x, 16 * (B + 1))

        @block.gpsimd
        def _(pool):
            chain = Count(fw_chain)
            pool.wait_ge(ld_ug, 16 * 7)

            def butterflies(a, b, n):
                h, src, dst = 1, a, b
                while h < n:
                    s4 = src.rearrange("p (g two h) -> p g two h", two=2, h=h)
                    d4 = dst.rearrange("p (g two h) -> p g two h", two=2, h=h)
                    chain.inc(nc.gpsimd.tensor_tensor(d4[:, :, 0, :], s4[:, :, 0, :], s4[:, :, 1, :], ALU.add))
                    chain.inc(nc.gpsimd.tensor_tensor(d4[:, :, 1, :], s4[:, :, 0, :], s4[:, :, 1, :], ALU.subtract))
                    chain.wait(pool)
                    src, dst, h = dst, src, 2 * h

            flat = lambda t: t.rearrange("p n d -> p (n d)")
            butterflies(flat(wugd[:, 0:16, :]), flat(pong[:, 0:16, :]), D)
            butterflies(flat(wugd[:, 16:24, :]), flat(pong[:, 0:8, :]), INTER)
            for n in range(16):
                chain.inc(nc.gpsimd.tensor_scalar(wugd[:, n, :], wugd[:, n, :], ws_ug[:, n:n + 1], D ** -0.5,
                                                  ALU.mult, ALU.mult))
            for r in range(DC):
                rows = flat(wugd[:, 16 + 4 * r:20 + 4 * r, :])
                chain.inc(nc.gpsimd.tensor_scalar(rows, rows, ws_dp[:, r:r + 1], INTER ** -0.5, ALU.mult, ALU.mult))
            chain.wait(pool)
            nc.gpsimd.drain().then_inc(fw_done, 1)
            def add_rotary(at, n, t):
                pool.wait_ge(at.sem["rope"], n + 1)
                h = t % 2
                if at is a1:
                    nc.gpsimd.tensor_tensor(qk[:, h, 0:D], t1[:, h, 0:D], t2[:, h, 0:D], ALU.add)
                    heads = lambda a: a[:, h, D:320].rearrange("p (k d) -> p k d", k=KV16).unsqueeze(2).to_broadcast(
                        [P, KV16, H16 // KV16, HD16])
                    nc.gpsimd.tensor_tensor(qk[:, h, D:2 * D].rearrange("p (k r d) -> p k r d", k=KV16, d=HD16),
                                            heads(t1), heads(t2), ALU.add).then_inc(at.sem["qk"], 1)
                else:
                    nc.gpsimd.tensor_tensor(qk[:, h, 0:320], t1[:, h, :], t2[:, h, :], ALU.add)
                    nc.gpsimd.tensor_tensor(qk[:, h, 320:384], t1[:, h, D:320], t2[:, h, D:320],
                                            ALU.add).then_inc(at.sem["qk"], 1)

            with pool.Fori(0, B) as b:
                for t in range(TB):
                    add_rotary(a1, b * TB + t, t)
            with pool.Fori(0, B * G64) as i:
                for t in range(TB):
                    add_rotary(a2, i * TB + t, t)

        vch = Count(v_chain)

        def dve_norm(v, phase, eps, src=x, dst=xn, rms=False):
            for t in range(NT):
                if phase == 0 and t % TB == 0:
                    v.wait_ge(ld_x, 16 * (t // TB + 1))
                vch.inc(nc.vector.bn_stats(st[:, t, :], src[:, t, :]))
            vch.wait(v)
            for t in range(NT):
                vch.inc(nc.vector.bn_aggr(mv[:, t, :], st[:, t, :]))
            vch.wait(v)
            if rms:
                vch.inc(nc.vector.tensor_tensor(std[:], mv[:, :, 0], mv[:, :, 0], ALU.mult))
                vch.wait(v)
                vch.inc(nc.vector.tensor_tensor(var[:], mv[:, :, 1], std[:], ALU.add))
                vch.wait(v)
                nc.vector.tensor_scalar(var[:], var[:], eps, None, ALU.add).then_inc(ln_var, 1)
            else:
                nc.vector.tensor_scalar(var[:], mv[:, :, 1], eps, None, ALU.add).then_inc(ln_var, 1)
            v.wait_ge(ln_std, phase + 1)
            vch.inc(nc.vector.reciprocal(rstd[:], std[:]))
            vch.wait(v)
            for t in range(NT):
                if rms:
                    nc.vector.tensor_scalar(dst[:, t, :], src[:, t, :], rstd[:, t:t + 1], None, ALU.mult).then_inc(xn_all, 1)
                else:
                    nc.vector.tensor_scalar(dst[:, t, :], src[:, t, :], mv[:, t, 0:1], rstd[:, t:t + 1],
                                            ALU.subtract, ALU.mult).then_inc(xn_all, 1)
            v.wait_ge(xn_all, NT * (phase + 1))

        @block.vector
        def _(v):
            v.wait_ge(ld_s, 16 * 17)
            v.wait_ge(ld_c, 16)
            vch.inc(nc.vector.tensor_scalar(nslope_b[:], slope_b[:], -1.0, None, ALU.mult))
            vch.inc(nc.vector.tensor_scalar(nslope_p[:], slope_p[:], -1.0, None, ALU.mult))
            dve_norm(v, 0, 1e-5)
            for n, (c, blocks, dst) in enumerate(START):
                if n % 2 == 0:
                    v.wait_ge(wt_ps, n + 1)
                    nc.vector.tensor_copy(dst, bank[n % 8][:, 0:P * len(blocks)]).then_inc(wt_sb[0], 1)
            v.wait_ge(dec_exp, H16 + 2 * DC + 1)
            a, _b = mid("ge")
            vch.inc(nc.vector.tensor_tensor(DT, DT, con[:, None, a:_b].to_broadcast([P, H16, P]), ALU.mult))
            vch.wait(v)

            ch = Count(l0["chain"], 2)
            with v.Fori(0, B) as b:
                ch.n = 0
                v.wait_ge(l0["xT_ps"], b * DC + 1)
                nc.vector.tensor_copy(xn_st[:], xn[:, bass.ts(b, TB), :]).then_inc(l0["stage"], 1)
                v.wait_ge(l0["q_sb"], b * 4 + 2)
                nc.vector.tensor_tensor(qdT.rearrange("p c (t i) -> p c t i", t=TB),
                                        qT.rearrange("p c (t i) -> p c t i", t=TB),
                                        QD.unsqueeze(2).to_broadcast([P, DC, TB, P]), ALU.mult).then_inc(l0["qd"], 1)
                v.wait_ge(l0["q_sb"], b * 4 + 4)
                par = const("parity")
                for e in range(2):
                    nc.vector.tensor_scalar(kTm[:, e, :, :], kT, par[:, e:e + 1], None, ALU.mult).then_inc(l0["kTm"], 1)
                for t in range(TB):
                    v.wait_ge(l0["u_ps"], b * TB + t + 1)
                    nc.vector.tensor_copy(u0[:, t, :], bank[(7, 1)[t % 2]][:, 0:D]).then_inc(l0["u_sb"], 1)
                    v.wait_ge(l0["k_sb"], b * TB + t + 1)
                    nc.vector.tensor_tensor(kd[:, t, :].rearrange("p (h d) -> p h d", h=H16),
                                            ks[:, t % 2, :].rearrange("p (h d) -> p h d", h=H16),
                                            KD.unsqueeze(2).to_broadcast([P, H16, HD16]),
                                            ALU.mult).then_inc(l0["kd"], 1)

                def decay(t):
                    for g in range(4):
                        v.wait_ge(l0["s_ps"], b * 16 + 4 * t + g + 1)
                        if g == 0 and t >= 2:
                            v.wait_ge(l0["o_ps"], b * TB + t - 1)
                        nc.vector.tensor_tensor(PT0[:, t % 2, 4 * g:4 * g + 4, :],
                                                bank[g][:].rearrange("p (h i) -> p h i", h=4),
                                                DT[:, 4 * g:4 * g + 4, :], ALU.mult).then_inc(l0["pt"], 1)

                decay(0)
                for t in range(TB):
                    if t + 1 < TB:
                        decay(t + 1)
                    v.wait_ge(l0["o_ps"], b * TB + t + 1)
                    nc.vector.tensor_tensor(ou[:, t, :], bank[4 + t % 2][:, 0:D], u0[:, t, :],
                                            ALU.mult).then_inc(l0["ou"], 1)
                    if t < TB - 1:
                        v.wait_ge(l0["st_ps"], b * 3 + t + 1)
                        into = kvs if t == 0 else kvt
                        a, _b = mid("block")
                        kv_ins = nc.vector.tensor_tensor(into[:], bank[6][:, 0:D].rearrange("p (c e) -> p c e", c=DC),
                                                         con[:, None, a:_b].to_broadcast([P, DC, P]), ALU.mult)
                        if t == 0:
                            kv_ins.then_inc(l0["st"], 1)
                        else:
                            ch.inc(kv_ins)
                            ch.wait(v, b)
                            v.wait_ge(l0["st"], b * 5 + 2 * t - 1)
                            for c in range(DC):
                                nc.vector.scalar_tensor_tensor(kvs[:, c, :], kvs[:, c, :], BD[:, c:c + 1], kvt[:, c, :],
                                                               ALU.mult, ALU.add).then_inc(l0["st"], 1)
            l0_chain_check = ch.n
            assert l0_chain_check == 2

            v.wait_ge(l0["sq"], NT + 1)
            v.wait_ge(l0["y_sb"], 2 * B + 1)
            nc.vector.tensor_scalar(ss[:], ss[:], 1.0 / D, 1e-6, ALU.mult, ALU.add).then_inc(rms_in, 1)
            v.wait_ge(rms_std, 1)
            vch.inc(nc.vector.reciprocal(rstd[:], std[:]))
            vch.wait(v)
            for t in range(NT):
                vch.inc(nc.vector.scalar_tensor_tensor(x[:, t, :], y0[:, t, :], rstd[:, t:t + 1], x[:, t, :],
                                                       ALU.mult, ALU.add))
            vch.wait(v)
            for n, (c, blocks, dst, sign) in enumerate(FFN):
                if n % 2 == 0:
                    v.wait_ge(wt_ps, len(START) + n + 1)
                    nc.vector.tensor_scalar(dst, bank[n % 8][:, 0:P * len(blocks)], sign, None, ALU.mult).then_inc(wt_sb[0], 1)
            dve_norm(v, 1, 1e-5)
            v.sem_inc(f0["y"], 1)
            with v.Fori(0, B) as b:
                v.wait_ge(f0["xT_ps"], b * DC + 1)
                nc.vector.tensor_copy(xn_st[:], xn[:, bass.ts(b, TB), :]).then_inc(f0["stage"], 1)
                for k in range(IC):
                    v.wait_ge(f0["silu"], b * IC + k + 1)
                    nc.vector.tensor_tensor(aT[:, k, :], bank[2 + 2 * (k % 2)][:], gsil[:, k % 2, :],
                                            ALU.mult).then_inc(f0["glu"], 1)
                for i in range(2):
                    v.wait_ge(f0["y_ps"], b * 2 + i + 1)
                    rows = x[:, bass.ds(b * TB + 2 * i, 2), :]
                    nc.vector.tensor_tensor(rows, rows, bank[6 + i][:].rearrange("p (t d) -> p t d", t=2),
                                            ALU.add).then_inc(f0["y"], 1)
            v.wait_ge(f0["y"], 2 * B + 1)
            def rope(at, n, t, v_dst):
                v.wait_ge(at.sem["qkv_ps"], n + 1)
                hd, h = at.hd, t % 2
                if t >= 2:
                    v.wait_ge(at.sem["qk"], n - 1)
                src = bank[YBANK][:, 0:320].rearrange("p (h d) -> p h d", d=hd)
                tab = lambda name, lo, hi: con[:, None, mid(name)[0] + t * hd + lo:mid(name)[0] + t * hd + hi].to_broadcast(
                    [P, 320 // hd, hi - lo])
                u1, u2 = (a[:, h, :].rearrange("p (h d) -> p h d", d=hd) for a in (t1, t2))
                name, half = str(hd), hd // 2
                nc.vector.tensor_tensor(u1, src, tab("cos" + name, 0, hd), ALU.mult)
                nc.vector.tensor_tensor(u2[:, :, 0:half], src[:, :, half:hd], tab("sin" + name, 0, half), ALU.mult)
                nc.vector.tensor_tensor(u2[:, :, half:hd], src[:, :, 0:half], tab("sin" + name, half, hd),
                                        ALU.mult).then_inc(at.sem["rope"], 1)
                nc.vector.tensor_copy(v_dst, bank[YBANK][:, 320:384]).then_inc(at.sem["yb"], 1)

            def dve_rows(at, it, b, ev, n_rope, v_dst, res):
                u0_, r0 = it * at.units, it * at.rows
                for j in range(at.units + LAG_PV + 3):
                    if j < at.units:
                        v.wait_ge(at.sem["s_ps"], u0_ + j + 1)
                        nc.vector.tensor_reduce(negmax[:, j:j + 1], bank[SBANK[j % 3]][:, 0:P * at.keys(at.row_of(j))],
                                                AX, ALU.max, negate=True).then_inc(at.sem["max"], 1)
                    e = j - LAG_T
                    if 0 <= e < at.units and e % 2 == 0:
                        v.wait_ge(at.sem["t_ps"], u0_ + e + 1)
                        if e >= 2:
                            v.wait_ge(at.sem["pv"], u0_ + e - 1)
                        n = P * at.keys(at.row_of(e))
                        nc.vector.tensor_copy(probsT[:, 0, 0:n], bank[PTBANK[0]][:, 0:n]).then_inc(at.sem["pt_dve"], 1)
                    e = j - LAG_PV
                    if 0 <= e < at.units and e % at.heads == at.heads - 1:
                        r = at.row_of(e)
                        cols = slice(r * at.heads, (r + 1) * at.heads)
                        v.wait_ge(at.sem["pv"], u0_ + e + 1)
                        nc.vector.reciprocal(rinv[:, cols], rowsum[:, cols]).then_inc(at.sem["chain"], 1)
                        v.wait_ge(at.sem["chain"], r0 + r + 1)
                        nc.vector.tensor_tensor(on[:, r % 2, :].rearrange("p (h d) -> p h d", d=at.hd),
                                                bank[OBANK][:, 0:D].rearrange("p (h d) -> p h d", d=at.hd),
                                                rinv[:, cols].unsqueeze(2).to_broadcast([P, at.heads, at.hd]),
                                                ALU.mult).then_inc(at.sem["on"], 1)
                    for kind, a in ev.get(j, ()):
                        if kind == "project":
                            v.wait_ge(at.sem["y_ps"], r0 + a + 1)
                            rows = res[:, bass.ds(b * TB + a, 1), :]
                            nc.vector.tensor_tensor(rows, rows, bank[YBANK][:, None, 0:D],
                                                    ALU.add).then_inc(at.sem["yb"], 1)
                        elif kind == "qkv":
                            rope(at, n_rope + a, a, v_dst[:, a, :])

            vch.inc(nc.vector.tensor_copy(causal[:], const("causal")))
            vch.inc(nc.vector.tensor_copy(ident_h[:], ident))
            vch.inc(nc.vector.tensor_scalar(par4, const("parity"), HD16 ** -0.5, None, ALU.mult))
            dve_norm(v, 2, 1e-5)
            v.sem_inc(a1.sem["yb"], 1)
            with v.Fori(0, B) as b:
                v.wait_ge(a1.sem["xT_ps"], b * DC + 1)
                nc.vector.tensor_copy(xn_st[:], xn[:, bass.ts(b, TB), :]).then_inc(a1.sem["stage"], 1)
                for t in range(TB):
                    rope(a1, b * TB + t, t, narrow_v[:, 0, t, :])
                dve_rows(a1, b, b, a1.events(False), 0, None, x)
            v.wait_ge(a1.sem["yb"], A1_EV * B + 1)
            dve_norm(v, 3, 1e-5)
            dve_norm(v, 4, 1e-5, xn, hn, rms=True)
            v.sem_inc(a2.sem["yb"], 1)
            with v.Fori(0, B) as b:
                v.wait_ge(a2.sem["xT_ps"], b * DC + 1)
                nc.vector.tensor_copy(xn_st[:], hn[:, bass.ts(b, TB), :]).then_inc(a2.sem["stage"], 1)
                for t in range(TB):
                    rope(a2, b * TB * G64 + t, t, wide_v[:, 0, t, :])

                def group(g, par, prefetch):
                    dve_rows(a2, b * G64 + g, b, a2.events(prefetch), (b * G64 + g + 1) * TB, wide_v[:, 1 - par], xn)

                with v.Fori(0, G64 // 2 - 1) as pair:
                    for par in range(2):
                        group(pair * 2 + par, par, True)
                group(G64 - 2, 0, True)
                group(G64 - 1, 1, False)
            v.wait_ge(a2.sem["yb"], A2_EV * B + 1)
            for t in range(NT):
                vch.inc(nc.vector.tensor_tensor(x[:, t, :], x[:, t, :], xn[:, t, :], ALU.add))
            vch.wait(v)
            dve_norm(v, 5, 1e-5, xn, hn, rms=True)

            def step(ins):
                vch.inc(ins)
                vch.wait(v)

            v.wait_ge(m5["lg_ps"], 1)
            step(nc.vector.tensor_copy(logits, bank[4][:, 0:NT * E].rearrange("p (t e) -> p t e", e=E)))
            for t in range(NT):
                vch.inc(nc.vector.max(best[:, t, :], logits[:, t, :]))
            vch.wait(v)
            wide = lambda col: col.to_broadcast([P, NT, E])
            least = wide(best[:, :, TOPK - 1:TOPK])
            vch.inc(nc.vector.tensor_tensor(above, logits, least, ALU.is_gt))
            vch.inc(nc.vector.tensor_tensor(ties, logits, least, ALU.is_equal))
            step(nc.vector.tensor_tensor(gate, logits, wide(best[:, :, 0:1]), ALU.subtract))
            nc.vector.tensor_reduce(room[:], above, AX, ALU.add).then_inc(m5["shift"], 1)
            v.wait_ge(m5["shift"], 1)
            step(nc.vector.tensor_scalar(room[:], room[:], -1.0, float(TOPK), ALU.mult, ALU.add))
            src, dst = ties, run_a
            for sh in (1, 2, 4, 8):
                vch.inc(nc.vector.tensor_copy(dst[:, :, 0:sh], src[:, :, 0:sh]))
                step(nc.vector.tensor_tensor(dst[:, :, sh:E], src[:, :, sh:E], src[:, :, 0:E - sh], ALU.add))
                src, dst = dst, (run_b if dst is run_a else run_a)
            step(nc.vector.tensor_tensor(dst, src, wide(room[:].unsqueeze(2)), ALU.is_le))
            step(nc.vector.tensor_tensor(dst, dst, ties, ALU.mult))
            step(nc.vector.tensor_tensor(above, above, dst, ALU.add))
            v.wait_ge(m5["exp"], 1)
            step(nc.vector.tensor_tensor(gate, gate, above, ALU.mult))
            step(nc.vector.tensor_reduce(room[:], gate, AX, ALU.add))
            step(nc.vector.reciprocal(room[:], room[:]))
            step(nc.vector.tensor_tensor(gate, gate, wide(room[:].unsqueeze(2)), ALU.mult))

            v.sem_inc(m5["acc"], 17)
            with v.Fori(0, E // 2) as pair:
                for i in range(2 * B + 1):
                    if i < 2 * B:
                        for hc in range(2):
                            v.wait_ge(m5["silu"], pair * 4 * B + 2 * i + hc + 1)
                            nc.vector.tensor_tensor(aT5[:, i % 2, hc, :], bank[2 * hc + 1][:], gs5[:, hc, :],
                                                    ALU.mult).then_inc(m5["glu"], 1)
                    i -= 1
                    if i >= 0:
                        par, b = i // B, i % B
                        if b == 0:
                            nc.vector.tensor_copy(gcol[:, par, :], gate[:, :, bass.ds(pair * 2 + par, 1)].rearrange(
                                "p t e -> p (t e)")).then_inc(m5["gcol"], 1)
                            v.wait_ge(m5["gcol"], pair * 2 + par + 1)
                        v.wait_ge(m5["acc"], pair * 8 * B + TB * i + 1)
                        for t in range(TB):
                            if t % 2 == 0:
                                v.wait_ge(m5["y_ps"], pair * 4 * B + 2 * i + t // 2 + 1)
                            n = TB * b + t
                            nc.vector.scalar_tensor_tensor(
                                x[:, n, :], bank[4 + 2 * (i % 2) + t // 2][:, D * (t % 2):D * (t % 2) + D],
                                gcol[:, par, n:n + 1], x[:, n, :], ALU.mult, ALU.add).then_inc(m5["acc"], 1)
            v.wait_ge(m5["acc"], 17 + NT * E)
            v.drain().then_inc(stored, 1)

        @block.scalar
        def _(act):
            act.wait_ge(ld_c, 16)
            act.wait_ge(v_chain, 2)
            for slot in range(H16):
                h = head_of(slot)
                nc.scalar.activation(DT[:, slot, :], const("lag"), ACT.Exp,
                                     scale=nslope_b[:, h:h + 1]).then_inc(dec_exp, 1)
            for c in range(DC):
                nc.scalar.activation(QD[:, c, :], const("ramp"), ACT.Exp, scale=nslope_p[:, c:c + 1]).then_inc(dec_exp, 1)
                nc.scalar.activation(BD[:, c:c + 1], nslope_p[:, c:c + 1], ACT.Exp, scale=float(P)).then_inc(dec_exp, 1)
            nc.scalar.activation(KD, nslope_b[:], ACT.Exp, scale=const("left")).then_inc(dec_exp, 1)
            act.wait_ge(ln_var, 1)
            nc.scalar.activation(std[:], var[:], ACT.Sqrt).then_inc(ln_std, 1)
            for n, (c, blocks, dst) in enumerate(START):
                if n % 2 == 1:
                    act.wait_ge(wt_ps, n + 1)
                    nc.scalar.activation(dst, bank[n % 8][:, 0:P * len(blocks)], ACT.Copy).then_inc(wt_sb[1], 1)

            def turn_evac(sems, b, scale=None):
                for c in range(DC):
                    act.wait_ge(sems["xT_ps"], b * DC + c + 2)
                    if scale is None:
                        ins = nc.scalar.activation(xnT[:, c, :], bank[c][:], ACT.Copy)
                    else:
                        ins = nc.scalar.activation(xnT[:, c, :], bank[c][:], ACT.Identity, scale=scale[:, c:c + 1])
                    ins.then_inc(sems["xT_sb"], 1)

            act.sem_inc(l0["y_sb"], 1)
            act.sem_inc(l0["sq"], 1)
            with act.Fori(0, B) as b:
                turn_evac(l0, b)
                for m in range(4):
                    act.wait_ge(l0["qk_ps"], b * 4 + m + 1)
                    nc.scalar.activation((qT, kT)[m // 2][:, m % 2, :], bank[2 + m][:], ACT.Silu).then_inc(l0["q_sb"], 1)
                for t in range(TB):
                    act.wait_ge(l0["kv_ps"], b * TB + t + 1)
                    if t >= 2:
                        act.wait_ge(l0["kd"], b * TB + t - 1)
                    kvb = bank[(6, 0)[t % 2]]
                    nc.scalar.activation(ks[:, t % 2, :], kvb[:, 0:D], ACT.Silu).then_inc(l0["k_sb"], 1)
                    nc.scalar.activation(v0[:, t, :], kvb[:, D:2 * D], ACT.Copy).then_inc(l0["v_sb"], 1)
                for t in range(TB):
                    act.wait_ge(l0["ou"], b * TB + t + 1)
                    act.wait_ge(l0["sq"], b * TB + t + 1)
                    nc.scalar.activation(osq, bank[4 + t % 2][:, 0:D], ACT.Square,
                                         accum_out=ss[:, bass.ds(b * TB + t, 1)]).then_inc(l0["sq"], 1)
                for c in range(DC):
                    act.wait_ge(l0["ouT_ps"], b * DC + c + 1)
                    nc.scalar.activation(ouT[:, c, :], bank[6 + c][:], ACT.Copy).then_inc(l0["ouT_sb"], 1)
                for i in range(2):
                    act.wait_ge(l0["y_ps"], b * 2 + i + 1)
                    nc.scalar.activation(y0[:, bass.ds(b * TB + 2 * i, 2), :],
                                         bank[i][:].rearrange("p (t d) -> p t d", t=2), ACT.Copy).then_inc(l0["y_sb"], 1)
            act.wait_ge(rms_in, 1)
            nc.scalar.activation(std[:], ss[:], ACT.Sqrt).then_inc(rms_std, 1)
            for n, (c, blocks, dst, sign) in enumerate(FFN):
                if n % 2 == 1:
                    act.wait_ge(wt_ps, len(START) + n + 1)
                    nc.scalar.activation(dst, bank[n % 8][:, 0:P * len(blocks)], ACT.Identity, scale=sign).then_inc(wt_sb[1], 1)
            act.wait_ge(ln_var, 2)
            nc.scalar.activation(std[:], var[:], ACT.Sqrt).then_inc(ln_std, 1)
            with act.Fori(0, B) as b:
                turn_evac(f0, b)
                for k in range(IC):
                    act.wait_ge(f0["up"], b * IC + k + 1)
                    if k >= 2:
                        act.wait_ge(f0["glu"], b * IC + k - 1)
                    nc.scalar.activation(gsil[:, k % 2, :], bank[3 + 2 * (k % 2)][:], ACT.Silu).then_inc(f0["silu"], 1)
            def turn_qk(at, n, t, par):
                act.wait_ge(at.sem["m_ps"], n + 1)
                m, cols = bank[MBANK], slice(P * t, P * t + P)
                if at is a1:
                    for e in range(2):
                        nc.scalar.activation(narrow_qT[:, e, :, cols], m[:, 0:D].rearrange("p (c i) -> p c i", c=DC),
                                             ACT.Identity, scale=par4[:, e:e + 1])
                    nc.scalar.activation(narrow_kT[:, :, cols], m[:, D:2 * D].rearrange("p (c i) -> p c i", c=DC),
                                         ACT.Copy).then_inc(at.sem["m_sb"], 1)
                else:
                    nc.scalar.activation(wide_qT[:, par, :, cols], m[:, 0:D].rearrange("p (c i) -> p c i", c=DC),
                                         ACT.Copy, scale=HD64 ** -0.5)
                    nc.scalar.activation(wide_kT[:, par, cols], m[:, D:D + P], ACT.Copy).then_inc(at.sem["m_sb"], 1)

            def act_rows(at, it, ev, n_m, par):
                u0_ = it * at.units
                for j in range(at.units + LAG_PV + 3):
                    if j < at.units:
                        n = P * at.keys(at.row_of(j))
                        act.wait_ge(at.sem["max"], u0_ + j + 1)
                        if j >= 3:
                            act.wait_ge(at.sem["t_ps"], u0_ + j - 2)
                        nc.scalar.activation(probs[:, j % 3, 0:n], bank[SBANK[j % 3]][:, 0:n], ACT.Exp,
                                             bias=negmax[:, j:j + 1], accum_out=rowsum[:, j:j + 1]).then_inc(at.sem["exp"], 1)
                    e = j - LAG_T
                    if 0 <= e < at.units and e % 2 == 1:
                        act.wait_ge(at.sem["t_ps"], u0_ + e + 1)
                        if e >= 2:
                            act.wait_ge(at.sem["pv"], u0_ + e - 1)
                        n = P * at.keys(at.row_of(e))
                        nc.scalar.activation(probsT[:, 1, 0:n], bank[PTBANK[1]][:, 0:n], ACT.Copy).then_inc(at.sem["pt_act"], 1)
                    for kind, a in ev.get(j, ()):
                        if kind == "turn_row":
                            act.wait_ge(at.sem["m_ps"], n_m + 1)
                            nc.scalar.activation(onT[:, a % 2, :, :], bank[MBANK][:, 0:D].rearrange("p (c i) -> p c i", c=DC),
                                                 ACT.Copy).then_inc(at.sem["m_sb"], 1)
                            n_m = n_m + 1
                        elif kind == "turn_qk":
                            turn_qk(at, n_m, a, 1 - par)
                            n_m = n_m + 1

            act.wait_ge(ln_var, 3)
            nc.scalar.activation(std[:], var[:], ACT.Sqrt).then_inc(ln_std, 1)
            act.sem_inc(a1.sem["m_sb"], 1)
            with act.Fori(0, B) as b:
                turn_evac(a1.sem, b)
                for t in range(TB):
                    turn_qk(a1, b * A1_EV + t, t, 0)
                act_rows(a1, b, a1.events(False), b * A1_EV + TB, 0)
            for n in (4, 5):
                act.wait_ge(ln_var, n)
                nc.scalar.activation(std[:], var[:], ACT.Sqrt).then_inc(ln_std, 1)
            act.wait_ge(ld_l1, 16 * 10)
            act.sem_inc(a2.sem["m_sb"], 1)
            with act.Fori(0, B) as b:
                turn_evac(a2.sem, b, lnw)
                for t in range(TB):
                    turn_qk(a2, b * A2_EV + t, t, 0)

                def group(g, par, prefetch):
                    act_rows(a2, b * G64 + g, a2.events(prefetch), b * A2_EV + TB + g * 2 * TB, par)

                with act.Fori(0, G64 // 2 - 1) as pair:
                    for par in range(2):
                        group(pair * 2 + par, par, True)
                group(G64 - 2, 0, True)
                group(G64 - 1, 1, False)
            act.wait_ge(ln_var, 6)
            nc.scalar.activation(std[:], var[:], ACT.Sqrt).then_inc(ln_std, 1)
            for b in range(B):
                for c in range(DC):
                    act.wait_ge(m5["hT_ps"], DC * b + c + 1)
                    nc.scalar.activation(hT5[:, c, S * b:S * b + S], bank[2 * (b % 2) + c][:], ACT.Identity,
                                         scale=fflnw[:, c:c + 1]).then_inc(m5["hT_sb"], 1)
            act.wait_ge(m5["shift"], 1)
            nc.scalar.activation(gate, gate, ACT.Exp).then_inc(m5["exp"], 1)
            with act.Fori(0, E // 2) as pair:
                for i in range(2 * B):
                    for hc in range(2):
                        act.wait_ge(m5["up_ps"], pair * 4 * B + 2 * i + hc + 1)
                        if i >= 1:
                            act.wait_ge(m5["glu"], pair * 4 * B + 2 * i + hc - 1)
                        nc.scalar.activation(gs5[:, hc, :], bank[2 * hc][:], ACT.Silu).then_inc(m5["silu"], 1)
        @block.tensor
        def _(pe):
            pe.wait_ge(ld_c, 16)

            def turn_weights(src, turns, n0):
                for n, (c, blocks, *_rest) in enumerate(turns):
                    if n >= 8:
                        pe.wait_ge(wt_sb[n % 2], (n0 + n - 8) // 2 + 1)
                    for i, blk in enumerate(blocks):
                        ins = nc.tensor.transpose(bank[n % 8][:, P * i:P * i + P], src[:, blk, P * c:P * c + P], ident)
                    ins.then_inc(wt_ps, 1)

            pe.wait_ge(ld_w, 16 * 6)
            turn_weights(wnat, START, 0)
            for half in wt_sb:
                pe.wait_ge(half, len(START) // 2)

            def turn_x(sems, b):
                pe.wait_ge(sems["stage"], b + 1)
                for c in range(DC):
                    for t in range(TB):
                        ins = nc.tensor.transpose(bank[c][:, P * t:P * t + P], xn_st[:, t, P * c:P * c + P], ident)
                    ins.then_inc(sems["xT_ps"], 1)
                pe.wait_ge(sems["xT_sb"], b * DC + DC)

            pe.sem_inc(l0["xT_ps"], 1)
            with pe.Fori(0, B) as b:
                pe.wait_ge(l0["y_sb"], b * 2 + 1)
                turn_x(l0, b)
                for m in range(4):
                    for c in range(DC):
                        ins = nc.tensor.matmul(bank[2 + m][:], wqkvuT[:, c, P * m:P * m + P], xnT[:, c, :],
                                               start=(c == 0), stop=(c == DC - 1))
                    ins.then_inc(l0["qk_ps"], 1)
                for t in range(TB):
                    if t >= 2:
                        pe.wait_ge(l0["v_sb"], b * TB + t - 1)
                        pe.wait_ge(l0["u_sb"], b * TB + t - 1)
                    for c in range(DC):
                        ins = nc.tensor.matmul(bank[(6, 0)[t % 2]][:], xnT[:, c, P * t:P * t + P],
                                               wqkvuT[:, c, D:3 * D], start=(c == 0), stop=(c == DC - 1))
                    ins.then_inc(l0["kv_ps"], 1)
                    for c in range(DC):
                        ins = nc.tensor.matmul(bank[(7, 1)[t % 2]][:, 0:D], xnT[:, c, P * t:P * t + P],
                                               wqkvuT[:, c, 3 * D:4 * D], start=(c == 0), stop=(c == DC - 1))
                    ins.then_inc(l0["u_ps"], 1)

                def scores(t):
                    for r in range(4):
                        for g in range(4):
                            if r == 0 and t >= 1:
                                pe.wait_ge(l0["pt"], b * 16 + 4 * (t - 1) + g + 1)
                            c, odd = r // 2, r % 2
                            rows = slice(32 * g, 32 * g + 32)
                            ins = nc.tensor.matmul(bank[g][:, P * r:P * r + P], kTm[rows, odd, c, P * t:P * t + P],
                                                   qT[rows, c, P * t:P * t + P], start=True, stop=True)
                            if r == 3:
                                ins.then_inc(l0["s_ps"], 1)

                pe.wait_ge(l0["kTm"], b * 2 + 2)
                pe.wait_ge(l0["v_sb"], b * TB + TB)
                pe.wait_ge(l0["u_sb"], b * TB + TB)
                scores(0)
                for t in range(TB):
                    if t < TB - 1:
                        pe.wait_ge(l0["kd"], b * TB + t + 1)
                        if t >= 1:
                            pe.wait_ge(l0["st"], b * 5 + 2 * t - 1)
                        for c in range(DC):
                            ins = nc.tensor.matmul(bank[6][:, P * c:P * c + P], kd[:, t, P * c:P * c + P],
                                                   v0[:, t, P * c:P * c + P], start=True, stop=True)
                        ins.then_inc(l0["st_ps"], 1)
                    if t + 1 < TB:
                        scores(t + 1)
                    pe.wait_ge(l0["pt"], b * 16 + 4 * t + 4)
                    if t >= 2:
                        pe.wait_ge(l0["sq"], b * TB + t)
                    o = bank[4 + t % 2]
                    for slot in range(H16):
                        h = head_of(slot)
                        cols = slice(HD16 * h, HD16 * h + HD16)
                        ins = nc.tensor.matmul(o[:, cols], PT0[:, t % 2, slot, :], v0[:, t, cols], start=(slot == 0),
                                               stop=(t == 0 and slot == H16 - 1), skip_group_check=True)
                    if t >= 1:
                        pe.wait_ge(l0["st"], b * 5 + 2 * t - 1)
                        pe.wait_ge(l0["qd"], b + 1)
                        for c in range(DC):
                            ins = nc.tensor.matmul(o[:, P * c:P * c + P], qdT[:, c, P * t:P * t + P], kvs[:, c, :],
                                                   start=False, stop=(c == DC - 1), skip_group_check=True)
                    ins.then_inc(l0["o_ps"], 1)
                pe.wait_ge(l0["ou"], b * TB + TB)
                for c in range(DC):
                    for t in range(TB):
                        ins = nc.tensor.transpose(bank[6 + c][:, P * t:P * t + P], ou[:, t, P * c:P * c + P], ident)
                    ins.then_inc(l0["ouT_ps"], 1)
                pe.wait_ge(l0["ouT_sb"], b * DC + DC)
                for t in range(TB):
                    for c in range(DC):
                        ins = nc.tensor.matmul(bank[t // 2][:, D * (t % 2):D * (t % 2) + D], ouT[:, c, P * t:P * t + P],
                                               wout0T[:, c, :], start=(c == 0), stop=(c == DC - 1))
                    if t % 2:
                        ins.then_inc(l0["y_ps"], 1)
            pe.wait_ge(l0["y_sb"], 2 * B + 1)
            pe.wait_ge(l0["sq"], NT + 1)
            pe.wait_ge(fw_done, 1)
            turn_weights(wugd, FFN, len(START))
            for half in wt_sb:
                pe.wait_ge(half, (len(START) + len(FFN)) // 2)
            pe.sem_inc(f0["xT_ps"], 1)
            with pe.Fori(0, B) as b:
                turn_x(f0, b)
                for k in range(IC):
                    if k >= 2:
                        pe.wait_ge(f0["glu"], b * IC + k - 1)
                    for j in range(2):
                        for c in range(DC):
                            ins = nc.tensor.matmul(bank[2 + 2 * (k % 2) + j][:],
                                                   wugT[:, c, INTER * j + P * k:INTER * j + P * k + P], xnT[:, c, :],
                                                   start=(c == 0), stop=(c == DC - 1))
                    ins.then_inc(f0["up"], 1)
                pe.wait_ge(f0["glu"], b * IC + IC)
                pe.wait_ge(f0["y"], b * 2 + 1)
                for t in range(TB):
                    for k in range(IC):
                        ins = nc.tensor.matmul(bank[6 + t // 2][:, D * (t % 2):D * (t % 2) + D], aT[:, k, P * t:P * t + P],
                                               wdT[:, k, :], start=(k == 0), stop=(k == IC - 1))
                    if t % 2:
                        ins.then_inc(f0["y_ps"], 1)
            def project_qkv(at, n_qkv, n_y, t, w):
                pe.wait_ge(at.sem["yb"], n_y + 1)
                for c in range(DC):
                    ins = nc.tensor.matmul(bank[YBANK][:, 0:QKV], xnT[:, c, P * t:P * t + P], w(c),
                                           start=(c == 0), stop=(c == DC - 1))
                ins.then_inc(at.sem["qkv_ps"], 1)

            def turn_qk(at, n_qkv, n_m, t):
                pe.wait_ge(at.sem["qk"], n_qkv + 1)
                pe.wait_ge(at.sem["m_sb"], n_m + 1)
                for c in range(4 if at is a1 else 3):
                    ins = nc.tensor.transpose(bank[MBANK][:, P * c:P * c + P], qk[:, t % 2, P * c:P * c + P], ident)
                ins.then_inc(at.sem["m_ps"], 1)

            def pe_rows(at, it, ev, n_m, n_y, n_qkv, par, w_next, w_out):
                u0_, r0 = it * at.units, it * at.rows
                pe.wait_ge(at.sem["m_sb"], n_m + 1)
                pe.wait_ge(at.sem["yb"], n_y + 1)
                turned = {}
                for j in range(at.units + LAG_PV + 3):
                    if j < at.units:
                        r, h, sbank = at.row_of(j), j % at.heads, bank[SBANK[j % 3]]
                        n = P * at.keys(r)
                        qcols = slice(P * r, P * r + P)
                        if j >= 3:
                            pe.wait_ge(at.sem["exp"], u0_ + j - 2)
                        if at is a1:
                            c, hh = h // 8, h % 8
                            rows = slice(32 * (hh // 2), 32 * (hh // 2) + 32)
                            ins = nc.tensor.matmul(sbank[:, 0:n], narrow_qT[rows, hh % 2, c, qcols], narrow_kT[rows, c, 0:n],
                                                   start=True, stop=True)
                        else:
                            rows = slice(HD64 * (h % 2), HD64 * (h % 2) + HD64)
                            nc.tensor.matmul(sbank[:, 0:n], wide_qT[rows, par, h // 2, qcols], wide_kT[rows, par, 0:n],
                                             start=True, stop=False)
                            ins = nc.tensor.matmul(sbank[:, n - P:n], ident_h[:], causal[:], start=False, stop=True)
                        ins.then_inc(at.sem["s_ps"], 1)
                    e = j - LAG_T
                    if 0 <= e < at.units:
                        pe.wait_ge(at.sem["exp"], u0_ + e + 1)
                        if e >= 2:
                            pe.wait_ge(at.sem[("pt_dve", "pt_act")[e % 2]], it * (at.units // 2) + e // 2)
                        for k in range(at.keys(at.row_of(e))):
                            ins = nc.tensor.transpose(bank[PTBANK[e % 2]][:, P * k:P * k + P],
                                                      probs[:, e % 3, P * k:P * k + P], ident)
                        ins.then_inc(at.sem["t_ps"], 1)
                    e = j - LAG_PV
                    if 0 <= e < at.units:
                        r, h = at.row_of(e), e % at.heads
                        pe.wait_ge(at.sem[("pt_dve", "pt_act")[e % 2]], it * (at.units // 2) + e // 2 + 1)
                        if h == 0 and r >= 1:
                            pe.wait_ge(at.sem["on"], r0 + r)
                        for k in range(at.keys(r)):
                            v = narrow_v[:, 0, k, HD16 * (h // 4):HD16 * (h // 4) + HD16] if at is a1 else wide_v[:, par, k, :]
                            ins = nc.tensor.matmul(bank[OBANK][:, at.hd * h:at.hd * h + at.hd],
                                                   probsT[:, e % 2, P * k:P * k + P], v,
                                                   start=(k == 0), stop=(k == at.keys(r) - 1))
                        ins.then_inc(at.sem["pv"], 1)
                    for kind, a in ev.get(j, ()):
                        if kind == "turn_row":
                            pe.wait_ge(at.sem["on"], r0 + a + 1)
                            pe.wait_ge(at.sem["m_sb"], n_m + 1)
                            for c in range(DC):
                                ins = nc.tensor.transpose(bank[MBANK][:, P * c:P * c + P], on[:, a % 2, P * c:P * c + P], ident)
                            ins.then_inc(at.sem["m_ps"], 1)
                            n_m = n_m + 1
                            turned[a] = n_m
                        elif kind == "project":
                            pe.wait_ge(at.sem["m_sb"], turned[a] + 1)
                            pe.wait_ge(at.sem["yb"], n_y + 1)
                            for c in range(DC):
                                ins = nc.tensor.matmul(bank[YBANK][:, 0:D], onT[:, a % 2, c, :], w_out(c),
                                                       start=(c == 0), stop=(c == DC - 1))
                            ins.then_inc(at.sem["y_ps"], 1)
                            n_y = n_y + 1
                        elif kind == "qkv":
                            project_qkv(at, n_qkv + a, n_y, a, w_next)
                            n_y = n_y + 1
                        else:
                            turn_qk(at, n_qkv + a, n_m, a)
                            n_m = n_m + 1

            def first_qkv(at, b, n_m, n_y, n_qkv, w):
                turn_x(at.sem, b)
                for kind, t in QKV_EVENTS:
                    if kind == "qkv":
                        project_qkv(at, n_qkv + t, n_y + t, t, w)
                    else:
                        turn_qk(at, n_qkv + t, n_m + t, t)

            pe.wait_ge(f0["y"], 2 * B + 1)
            pe.sem_inc(a1.sem["xT_ps"], 1)
            with pe.Fori(0, B) as b:
                first_qkv(a1, b, b * A1_EV, b * A1_EV, b * TB, lambda c: wqkv1T[:, c, :])
                pe_rows(a1, b, a1.events(False), b * A1_EV + TB, b * A1_EV + TB, 0, 0, None, lambda c: wo1T[:, c, :])
            pe.wait_ge(ld_l1, 16 * 10)
            pe.sem_inc(a2.sem["xT_ps"], 1)
            with pe.Fori(0, B) as b:
                first_qkv(a2, b, b * A2_EV, b * A2_EV, b * TB * G64, lambda c: wgrp[:, c, 0, :])

                def group(g, par, prefetch):
                    n_ev = b * A2_EV + TB + g * 2 * TB
                    pe_rows(a2, b * G64 + g, a2.events(prefetch), n_ev, n_ev, (b * G64 + g + 1) * TB, par,
                            lambda c: wgrp[:, c, bass.ds(g + 1, 1), :].rearrange("p a n -> p (a n)"),
                            lambda c: wo_sb[:, bass.ds(g * 2 + c, 1), :].rearrange("p a n -> p (a n)"))

                with pe.Fori(0, G64 // 2 - 1) as pair:
                    for par in range(2):
                        group(pair * 2 + par, par, True)
                group(G64 - 2, 0, True)
                group(G64 - 1, 1, False)
            for b in range(B):
                pe.wait_ge(xn_all, 5 * NT + TB * b + TB)
                if b >= 2:
                    pe.wait_ge(m5["hT_sb"], DC * (b - 1))
                for c in range(DC):
                    for t in range(TB):
                        ins = nc.tensor.transpose(bank[2 * (b % 2) + c][:, P * t:P * t + P],
                                                  hn[:, TB * b + t, P * c:P * c + P], ident)
                    ins.then_inc(m5["hT_ps"], 1)
            pe.wait_ge(m5["hT_sb"], DC * B)
            for t in range(NT):
                for c in range(DC):
                    ins = nc.tensor.matmul(bank[4][:, E * t:E * t + E], hT5[:, c, P * t:P * t + P], wg_sb[:, c, :],
                                           start=(c == 0), stop=(c == DC - 1))
            ins.then_inc(m5["lg_ps"], 1)
            pe.wait_ge(m5["exp"], 1)
            with pe.Fori(0, E // 2) as pair:
                for i in range(2 * B + 1):
                    if i < 2 * B:
                        par, b = i // B, i % B
                        if b == 0:
                            pe.wait_ge(ld_e[par], pair * 48 + 48)
                        for hc in range(2):
                            if i >= 1:
                                pe.wait_ge(m5["glu"], pair * 4 * B + 2 * i + hc - 1)
                            for j in range(2):
                                for c in range(DC):
                                    ins = nc.tensor.matmul(bank[2 * hc + j][:], w13[:, par, DC * j + c, P * hc:P * hc + P],
                                                           hT5[:, c, S * b:S * b + S], start=(c == 0), stop=(c == DC - 1))
                            ins.then_inc(m5["up_ps"], 1)
                    i -= 1
                    if i >= 0:
                        par = i // B
                        pe.wait_ge(m5["glu"], pair * 4 * B + 2 * i + 2)
                        pe.wait_ge(m5["acc"], pair * 8 * B + TB * i + 17 - 2 * TB)
                        for t in range(TB):
                            for hc in range(2):
                                ins = nc.tensor.matmul(bank[4 + 2 * (i % 2) + t // 2][:, D * (t % 2):D * (t % 2) + D],
                                                       aT5[:, i % 2, hc, P * t:P * t + P], w2s[:, par, hc, :],
                                                       start=(hc == 0), stop=(hc == 1))
                            if t % 2:
                                ins.then_inc(m5["y_ps"], 1)

_INS = ["L0_attn_x", "L0_attn_slope_rate", "L0_attn_W_qkvu", "L0_attn_W_out", "L0_ffn_SU_ug", "L0_ffn_SU_dp",
        "L0_ffn_Wscale_ug", "L0_ffn_Wscale_dp", "L0_ffn_W_up", "L0_ffn_W_gate", "L0_ffn_W_down", "L1_attn_Wq",
        "L1_attn_Wk", "L1_attn_Wv", "L1_attn_Wo", "L1_ffn_ln_w", "L1_ffn_ff_ln_w", "L1_ffn_wq", "L1_ffn_wk",
        "L1_ffn_wv", "L1_ffn_wo", "L1_ffn_wg", "L1_ffn_w1", "L1_ffn_w3", "L1_ffn_w2"]
_OUTS = [((B, S, D), "float32")]


def shape_constants(np):
    f = np.float32
    c = np.zeros((P, NCONST), f)

    def put(name, a):
        lo, hi = CONST_COLS[name]
        c[:, lo:hi] = np.asarray(a, f).reshape(P, hi - lo)

    p, i = np.arange(P)[:, None], np.arange(P)[None, :]
    put("ident", p == i)
    put("lag", np.maximum(i - p, 0))
    put("ge", i >= p)
    put("causal", np.where(i <= p, 0.0, -1e30))
    put("block", p // HD16 == i // HD16)
    put("ramp", np.broadcast_to(i + 1, (P, P)))
    put("left", P - 1 - np.arange(P))
    put("parity", np.stack([(p[:, 0] // HD16) % 2 == 0, (p[:, 0] // HD16) % 2 == 1], 1))
    for name, hd, inv in (
            ("16", HD16, f(1.0) / f(10000.0) ** (np.arange(0, HD16, 2, dtype=f) / f(HD16))),
            ("64", HD64, f(1.0) / f(150000.0) ** (np.arange(HD64 // 2, dtype=f) / f(HD64 // 2)))):
        ang = (np.arange(S, dtype=f)[:, None] * inv.astype(f)[None, :]).astype(f)
        tiles = lambda a: a.reshape(TB, P, hd).transpose(1, 0, 2)
        put("cos" + name, tiles(np.concatenate([np.cos(ang), np.cos(ang)], 1)))
        put("sin" + name, tiles(np.concatenate([-np.sin(ang), np.sin(ang)], 1)))
    return c


def kernel(**inputs):
    import numpy as _np
    import concourse.bacc as _bacc
    from concourse import mybir as _mybir
    from concourse.bass_utils import run_bass_kernel_spmd as _run

    nc = _bacc.Bacc("TRN2", target_bir_lowering=False, num_devices=1)
    arrays, args = {}, []
    for name in _INS + ["consts"]:
        a = _np.ascontiguousarray(shape_constants(_np) if name == "consts" else inputs[name])
        arrays[f"in_{name}_dram"] = a
        args.append(nc.dram_tensor(f"in_{name}_dram", a.shape, _mybir.dt.from_np(a.dtype), kind="ExternalInput").ap())
    for i, (shape, dtype) in enumerate(_OUTS):
        dt = _mybir.dt.from_np(_np.dtype(dtype))
        args.append(nc.dram_tensor(f"out_{i}_dram", shape, dt, kind="ExternalOutput").ap())
    two_layers(nc, *args)
    r = _run(nc, [arrays], core_ids=[0])
    return r.results[0]["out_0_dram"]
```

```python
from contextlib import ExitStack

import concourse.bass as bass
from concourse import mybir

ALU = mybir.AluOpType
ACT = mybir.ActivationFunctionType
AX = mybir.AxisListType.X
F32 = mybir.dt.float32
F32R = mybir.dt.float32r
BF16 = mybir.dt.bfloat16

P = 128
D = 256
DC = D // P
B, S = 4, 512
TB = S // P
NT = B * TB
INTER = 1024
IC = INTER // P
H16, HD16 = 16, 16
KV16 = 4
G64, R64, HD64 = 8, 4, 64
E, TOPK, EH = 16, 4, 256
QKV = 384

CONST_COLS = {}
_at = 0
for _name, _n in (("ident", P), ("lag", P), ("ge", P), ("causal", P), ("block", P), ("ramp", P), ("left", 1),
                  ("parity", 2), ("cos16", TB * HD16), ("sin16", TB * HD16), ("cos64", TB * HD64),
                  ("sin64", TB * HD64)):
    CONST_COLS[_name] = (_at, _at + _n)
    _at += _n
NCONST = _at


class Region:

    def __init__(self, tensor):
        self.tensor, self.at = tensor, 0

    def reuse(self):
        self.at = 0

    def take(self, *shape):
        n = 1
        for s in shape:
            n *= s
        v = self.tensor[:, self.at:self.at + n]
        self.at += n
        assert self.at <= self.tensor.shape[1], (self.at, self.tensor.shape)
        dims = "abc"[:len(shape)]
        if len(shape) == 1:
            return v
        return v.rearrange(f"p ({' '.join(dims)}) -> p {' '.join(dims)}", **dict(zip(dims, shape)))


class Count:

    def __init__(self, sem, per_round=0, start=0):
        self.sem, self.per_round, self.n, self.start = sem, per_round, 0, start

    def inc(self, ins):
        ins.then_inc(self.sem, 1)
        self.n += 1

    def wait(self, eng, rnd=0):
        eng.wait_ge(self.sem, rnd * self.per_round + self.n + self.start)


def two_layers(nc, x_in, slope, W_qkvu, W_out0, SU_ug, SU_dp, Wscale_ug, Wscale_dp, W_up, W_gate, W_down,
               Wq1, Wk1, Wv1, Wo1, ln_w, ff_ln_w, wq, wk, wv, wo, wg, w1, w3, w2, consts, out):
    ctx = ExitStack()
    with ctx:
        def sb(name, shape, dt=F32):
            return ctx.enter_context(nc.sbuf_tensor(name, shape, dt))

        def sem(name):
            return ctx.enter_context(nc.semaphore(name))

        bank = [ctx.enter_context(nc.psum_tensor(f"bank{i}", [P, 512], F32)) for i in range(8)]

        x = sb("x", [P, NT, D])
        con = sb("con", [P, NCONST])

        def const(name):
            a, b = CONST_COLS[name]
            return con[:, a:b]

        ident = const("ident")
        wqkvuT = sb("wqkvuT", [P, DC, 4 * D])
        wout0T = sb("wout0T", [P, DC, D])
        wugT = sb("wugT", [P, DC, 2 * INTER])
        wdT = sb("wdT", [P, IC, D])
        wqkv1T = sb("wqkv1T", [P, DC, QKV])
        late = Region(sb("late", [P, DC * G64 * QKV + 2 * G64 * D]))
        wgrp = late.take(DC, G64, QKV)
        wo_sb = late.take(2 * G64, D)
        late.reuse()
        wg_sb = sb("wg_sb", [P, DC, E])
        su_ug = sb("su_ug", [P, DC])
        su_dp = sb("su_dp", [P, IC])
        ws_ug = sb("ws_ug", [P, 2 * IC])
        ws_dp = sb("ws_dp", [P, DC])
        lnw = sb("lnw", [P, DC])
        fflnw = sb("fflnw", [P, DC])

        NATB = 15
        wnat = late.take(NATB, D)
        causal = sb("causal", [P, P], BF16)
        ident_h = sb("ident_h", [P, P], BF16)
        room = sb("room", [P, NT])
        gcol = sb("gcol", [P, 2, NT])
        wo1p = sb("wo1p", [P, 4, D])

        st = sb("st", [P, NT, 6])
        mv = sb("mv", [P, NT, 2])
        var = sb("var", [P, NT])
        std = sb("std", [P, NT])
        rstd = sb("rstd", [P, NT])
        xn = sb("xn", [P, NT, D])
        hn = wugT[:].rearrange("p c (t d) -> p (c t) d", d=D)
        xn_st = sb("xn_st", [P, TB, D])
        xnT = sb("xnT", [P, DC, S])

        ld_c, ld_x, ld_w, ld_ug, ld_s, ld_l1, ld_l2 = (sem(n) for n in (
            "ld_c", "ld_x", "ld_w", "ld_ug", "ld_s", "ld_l1", "ld_l2"))
        v_chain = sem("v_chain")
        ln_var, ln_std = sem("ln_var"), sem("ln_std")
        xn_all = sem("xn_all")
        wt_ps = sem("wt_ps")
        wt_sb = [sem("wt_sb_dve"), sem("wt_sb_act")]
        wo_spread = sem("wo_spread")
        fw_chain, fw_done = sem("fw_chain"), sem("fw_done")
        stored = sem("stored")

        mid = CONST_COLS.get

        slope_b = sb("slope_b", [P, H16])
        nslope_b = sb("nslope_b", [P, H16])
        slope_p = sb("slope_p", [P, DC])
        nslope_p = sb("nslope_p", [P, DC])
        first = ctx.enter_context(ExitStack())
        early = Region(first.enter_context(nc.sbuf_tensor("early", [P, 32 * D + 10368], F32)))
        wugd = early.take(24, D)
        pong = early.take(8, D)
        DT = late.take(H16, P)
        QD = early.take(DC, P)
        KD = early.take(H16)
        BD = early.take(DC)
        qT = early.take(DC, S)
        qdT = early.take(DC, S)
        kT = early.take(DC, S)
        kTm = early.take(2, DC, S)
        ks = early.take(2, D)
        kd = early.take(TB, D)
        v0 = early.take(TB, D)
        u0 = early.take(TB, D)
        PT0 = late.take(2, H16, P)
        kvs = early.take(DC, P)
        kvt = ks[:, 1, :].rearrange("p (c e) -> p c e", c=DC)
        ou = early.take(TB, D)
        osq = ks[:, 0, :]
        ouT = kT
        ss = early.take(NT)
        y0 = xn

        def head_of(slot):
            g, r = slot // 4, slot % 4
            return 8 * (r // 2) + 2 * g + r % 2

        dec_exp = sem("dec_exp")
        l0 = {n: sem("l0_" + n) for n in ("stage", "xT_ps", "xT_sb", "qk_ps", "q_sb", "kv_ps", "k_sb", "v_sb", "u_ps",
                                          "u_sb", "kTm", "kd", "s_ps", "pt", "o_ps", "st_ps", "st", "ou", "sq",
                                          "ouT_ps", "ouT_sb", "y_ps", "y_sb", "chain", "qd")}
        rms_in, rms_std = sem("rms_in"), sem("rms_std")

        early.reuse()
        early.take(32, D)
        gsil = early.take(2, S)
        aT = early.take(IC, S)
        f0 = {n: sem("f0_" + n) for n in ("stage", "xT_ps", "xT_sb", "up", "silu", "glu", "y_ps", "y")}

        first.close()
        second = ctx.enter_context(ExitStack())
        qf = second.enter_context(nc.sbuf_tensor("qf", [P, H16 * S], F32R))
        kf = second.enter_context(nc.sbuf_tensor("kf", [P, KV16 * S], F32R))
        region = Region(second.enter_context(nc.sbuf_tensor("attn", [P, 10080], F32)))
        probsT = region.take(3, S)
        negmax, rowsum, rinv = const("lag")[:, 0:64], const("lag")[:, 64:128], const("ge")[:, 0:64]
        onT = region.take(2, S)
        t1 = region.take(2, 320)
        t2 = region.take(2, 320)
        shared = region.at
        narrow_x = region.take(2, (H16 + KV16) * P)
        narrow_v = region.take(TB, KV16, 32)
        narrow_q = qf[:].rearrange("p (h n) -> p h n", h=H16)
        narrow_k = kf[:].rearrange("p (h n) -> p h n", h=KV16)
        region.at = shared
        wide_x = region.take(2, (R64 + 2) * P)
        wide_v = region.take(2, TB, HD64)
        wide_probs = region.take(8, S)
        wide_q = qf[:, 0:2 * R64 * S].rearrange("p (u h n) -> p u h n", u=2, h=R64)
        wide_k = kf[:].rearrange("p (u h n) -> p u h n", u=2, h=2)
        more_probs = wdT[:].rearrange("p k d -> p (k d)").rearrange("p (u n) -> p u n", n=S)
        narrow_probs = wugT[:].rearrange("p c n -> p (c n)").rearrange("p (u n) -> p u n", n=S)

        class Attention:

            names = ("stage", "xT_ps", "xT_sb", "qkv_ps", "rope", "yb", "sum", "hi", "qk", "m_ps", "m_sb", "m_sbd", "s_ps",
                     "max", "exp", "inv", "norm", "t_ps", "pt_dve", "pt_act", "pv", "o_sb", "y_ps")

            def __init__(self, name, quads, hd, causal, probs):
                self.quads, self.hd, self.causal, self.probs = quads, hd, causal, probs
                self.units = 4 * len(quads)
                self.per_row = len(quads) // TB
                self.steps = [(q, k) for q, (r, _g) in enumerate(quads) for k in range(self.keys(r))]
                self.sem = {n: sem(f"{name}_{n}") for n in self.names}

            def keys(self, row):
                return row + 1 if self.causal else TB

            def row_of(self, unit):
                return self.quads[unit // 4][0]

            def last_step(self, quad):
                return max(n for n, (q, _k) in enumerate(self.steps) if q == quad)

            def prob(self, unit):
                slot = unit % 12
                return self.probs[:, slot, :] if slot < 8 else more_probs[:, slot - 8, :]

            def order(self, extra):
                ops, turned, done, due, slot = [], 0, 0, [], 0

                def values():
                    nonlocal done
                    ops.append(("values", done))
                    q = self.steps[done][0]
                    if done == self.last_step(q) and (q + 1) % self.per_row == 0:
                        due.append((slot + 1, q // self.per_row))
                    done += 1

                while done < len(self.steps) or due:
                    if slot < self.units:
                        ops.append(("scores", slot))
                    ops += extra.get(slot, [])
                    while due and due[0][0] <= slot:
                        ops.append(("project", due.pop(0)[1]))
                    if turned < len(self.steps) and 4 * self.steps[turned][0] + 3 + LAG <= slot:
                        ops.append(("turn", turned))
                        turned += 1
                        if turned - done > 2:
                            values()
                    elif done < turned:
                        values()
                    slot += 1
                return ops

        FIRST_QKV = (("qkv", 0), ("qkv", 1), ("split", 0), ("split", 1), ("turn_q", 0), ("turn_k", 0), ("qkv", 2),
                     ("turn_q", 1), ("turn_k", 1), ("qkv", 3), ("split", 2), ("split", 3), ("turn_q", 2), ("turn_k", 2),
                     ("turn_q", 3), ("turn_k", 3))
        NEXT_QKV = {0: [("qkv", 0)], 2: [("qkv", 1)], 4: [("split", 0)], 5: [("split", 1), ("turn_q", 0)], 6: [("turn_k", 0)],
                    7: [("turn_q", 1)], 8: [("turn_k", 1)], 9: [("qkv", 2)], 11: [("qkv", 3)], 13: [("split", 2)],
                    14: [("split", 3), ("turn_q", 2)], 15: [("turn_k", 2)], 16: [("turn_q", 3)], 17: [("turn_k", 3)]}
        LAG = 3
        a1 = Attention("a1", [(r, g) for r in range(TB) for g in range(KV16)], HD16, False, narrow_probs)
        a2 = Attention("a2", [(r, 0) for r in reversed(range(TB))], HD64, True, wide_probs)
        SBANK, PTBANK, OBANK, MBANK, YBANK = (0, 1, 2), (3, 4), 5, 6, 7
        A1_Y = 2 * TB
        A2_Y = TB + G64 * 2 * TB - TB
        A2_M = 2 * TB * G64

        second.close()
        early = Region(sb("experts", [P, 18560]))
        hT5 = early.take(DC, B * S)
        w13 = early.take(2, 2 * DC, EH)
        w2s = early.take(2, DC, D)
        gs5 = early.take(2, S)
        aT5 = early.take(4, S).rearrange("p (u c) n -> p u c n", u=2)
        logits = early.take(NT, E)
        gate = early.take(NT, E)
        above = early.take(NT, E)
        ties = early.take(NT, E)
        run_a = early.take(NT, E)
        run_b = early.take(NT, E)
        best = early.take(NT, 8)
        m5 = {n: sem("m5_" + n) for n in ("hT_ps", "hT_sb", "lg_ps", "exp", "shift", "silu", "glu", "up_ps", "y_ps", "acc",
                                          "gcol")}
        ld_e = [sem("ld_e0"), sem("ld_e1")]

        block = ctx.enter_context(nc.Block())

        def parts(at, t):
            h, q, k = t % 2, t1[:, t % 2, 0:D], t1[:, t % 2, D:320]
            if at is a1:
                qx = narrow_x[:, h, 0:H16 * P].rearrange("p (h z) -> p h z", z=P)
                kx = narrow_x[:, h, H16 * P:].rearrange("p (h f w d) -> p h f w d", h=KV16, w=2, d=HD16)
                qd = lambda w: qx[:, :, 32 * w:32 * w + 32].rearrange("p h (f d) -> p h f d", d=HD16)
                kd_ = lambda w: kx[:, :, :, w, :]
                wide = lambda a, n, f: a.rearrange("p (h d) -> p h d", h=n).unsqueeze(2).to_broadcast([P, n, f, HD16])
                return ((qd, qd(0), wide(q, H16, 2)), (kd_, kd_(0), wide(k, KV16, 4)))
            qx = wide_x[:, h, 0:R64 * P].rearrange("p (h w d) -> p h w d", h=R64, w=2)
            kx = wide_x[:, h, R64 * P:].rearrange("p (w f d) -> p w f d", w=2, f=2)
            return ((lambda w: qx[:, :, w, :], qx[:, :, 0, :], q.rearrange("p (h d) -> p h d", h=R64)),
                    (lambda w: kx[:, w, :, :], kx[:, 0, :, :], k.unsqueeze(1).to_broadcast([P, 2, HD64])))

        def start_turns():
            for c in range(DC):
                for blocks, dst in ((range(0, 4), wqkvuT[:, c, 0:512]), (range(4, 8), wqkvuT[:, c, 512:1024]),
                                    (range(8, 10), wout0T[:, c, :]), (range(10, 13), wqkv1T[:, c, :])):
                    yield wnat, c, list(blocks), dst
            for i in range(4):
                yield wo_nat, 0, [i, 4 + i], wo1p[:, i, :]

        wo_nat = xn_st[:].rearrange("p t d -> p (t d)").rearrange("p (n q) -> p n q", q=P)
        START = list(start_turns())
        FFN = [(wugd, c, list(range(4 * g, 4 * g + 4)), wugT[:, c, 512 * g:512 * g + 512], su_ug[:, c:c + 1])
               for g in range(4) for c in range(DC)]
        FFN += [(wugd, k % 2, [16 + k // 2, 20 + k // 2], wdT[:, k, :], su_dp[:, k:k + 1]) for k in range(IC)]

        @block.sync
        def _(sync):
            sync.dma_start(con[:], consts).then_inc(ld_c, 16)
            sync.dma_start(wnat[:, 0:8, :], W_qkvu.rearrange("(n p) d -> p n d", p=P)).then_inc(ld_w, 16)
            xv = x_in.rearrange("b (t p) d -> p (b t) d", p=P)
            for b in range(B):
                sync.dma_start(x[:, TB * b:TB * b + TB, :], xv[:, TB * b:TB * b + TB, :]).then_inc(ld_x, 16)
            sync.dma_start(slope_b[:], slope.rearrange("h a b -> (a b h)").partition_broadcast(P)).then_inc(ld_s, 16)
            for h in range(H16):
                sync.dma_start(slope_p[HD16 * (h % 8):HD16 * (h % 8) + HD16, h // 8:h // 8 + 1],
                               slope[h, :, 0].partition_broadcast(HD16)).then_inc(ld_s, 16)
            sync.dma_start(wnat[:, 8:10, :], W_out0.rearrange("(n p) d -> p n d", p=P)).then_inc(ld_w, 16)
            sync.dma_start(wnat[:, 10:12, :], Wq1.rearrange("(n p) d -> p n d", p=P)).then_inc(ld_w, 16)
            sync.dma_start(wnat[0:64, 12, :], Wk1).then_inc(ld_w, 16)
            sync.dma_start(wnat[64:128, 12, :], Wv1).then_inc(ld_w, 16)
            sync.dma_start(wnat[:, 13:15, :], Wo1.rearrange("(n p) d -> p n d", p=P)).then_inc(ld_w, 16)
            sync.dma_start(wugd[:, 0:8, :], W_up.rearrange("(n p) d -> p n d", p=P)).then_inc(ld_ug, 16)
            sync.dma_start(wugd[:, 8:16, :], W_gate.rearrange("(n p) d -> p n d", p=P)).then_inc(ld_ug, 16)
            sync.dma_start(wugd[:, 16:24, :], W_down.rearrange("(r p) (m d) -> p r m d", p=P, d=D)).then_inc(ld_ug, 16)
            sync.dma_start(ws_ug[:], Wscale_ug.rearrange("(n p) -> p n", p=P), allow_slow_non_contiguous=True).then_inc(ld_ug, 16)
            sync.dma_start(ws_dp[:], Wscale_dp.rearrange("(n p) -> p n", p=P), allow_slow_non_contiguous=True).then_inc(ld_ug, 16)
            sync.dma_start(su_ug[:], SU_ug.rearrange("(n p) -> p n", p=P), allow_slow_non_contiguous=True).then_inc(ld_ug, 16)
            sync.dma_start(su_dp[:], SU_dp.rearrange("(n p) -> p n", p=P), allow_slow_non_contiguous=True).then_inc(ld_ug, 16)
            sync.dma_start(lnw[:], ln_w.rearrange("(n p) -> p n", p=P), allow_slow_non_contiguous=True).then_inc(ld_l1, 16)
            sync.dma_start(fflnw[:], ff_ln_w.rearrange("(n p) -> p n", p=P), allow_slow_non_contiguous=True).then_inc(ld_l1, 16)
            sync.dma_start(wg_sb[:], wg.rearrange("(c p) e -> p c e", p=P)).then_inc(ld_l1, 16)
            sync.wait_ge(rms_in, 1)
            for c in range(DC):
                rows = slice(P * c, P * c + P)
                sync.dma_start(wgrp[:, c, :, 0:256], wq[rows, :].rearrange("p (g n) -> p g n", g=G64)).then_inc(ld_l1, 16)
                sync.dma_start(wgrp[:, c, :, 256:320], wk[rows, :].rearrange("p (g n) -> p g n", g=G64)).then_inc(ld_l1, 16)
                sync.dma_start(wgrp[:, c, :, 320:384], wv[rows, :].rearrange("p (g n) -> p g n", g=G64)).then_inc(ld_l1, 16)
            sync.dma_start(wo_sb[:], wo.rearrange("(k p) d -> p k d", p=P)).then_inc(ld_l1, 16)
            def load_expert(e, half):
                w = lambda a: a[bass.ds(e, 1), :, :].rearrange("e (c p) h -> p (e c) h", p=P)
                sync.dma_start(w13[:, half, 0:DC, :], w(w1)).then_inc(ld_e[half], 16)
                sync.dma_start(w13[:, half, DC:2 * DC, :], w(w3)).then_inc(ld_e[half], 16)
                sync.dma_start(w2s[:, half, :, :], w(w2)).then_inc(ld_e[half], 16)

            sync.wait_ge(ln_var, 6)
            load_expert(0, 0)
            load_expert(1, 1)
            with sync.Fori(1, E // 2) as pair:
                for half in range(2):
                    sync.wait_ge(m5["y_ps"], (pair - 1) * 4 * B + 2 * B * (half + 1))
                    load_expert(pair * 2 + half, half)
            sync.wait_ge(stored, 1)
            ov = out.rearrange("b (t p) d -> p (b t) d", p=P)
            sync.dma_start(ov, x[:]).then_inc(ld_x, 16)
            sync.wait_ge(ld_x, 16 * (B + 1))

        @block.gpsimd
        def _(pool):
            chain = Count(fw_chain)
            pool.wait_ge(ld_ug, 16 * 7)

            def butterflies(a, b, n):
                h, src, dst = 1, a, b
                while h < n:
                    s4 = src.rearrange("p (g two h) -> p g two h", two=2, h=h)
                    d4 = dst.rearrange("p (g two h) -> p g two h", two=2, h=h)
                    chain.inc(nc.gpsimd.tensor_tensor(d4[:, :, 0, :], s4[:, :, 0, :], s4[:, :, 1, :], ALU.add))
                    chain.inc(nc.gpsimd.tensor_tensor(d4[:, :, 1, :], s4[:, :, 0, :], s4[:, :, 1, :], ALU.subtract))
                    chain.wait(pool)
                    src, dst, h = dst, src, 2 * h

            flat = lambda t: t.rearrange("p n d -> p (n d)")
            for blk, n in ((0, D), (8, D), (16, INTER)):
                butterflies(flat(wugd[:, blk:blk + 8, :]), flat(pong), n)
            for n in range(16):
                chain.inc(nc.gpsimd.tensor_scalar(wugd[:, n, :], wugd[:, n, :], ws_ug[:, n:n + 1], D ** -0.5,
                                                  ALU.mult, ALU.mult))
            for r in range(DC):
                rows = flat(wugd[:, 16 + 4 * r:20 + 4 * r, :])
                chain.inc(nc.gpsimd.tensor_scalar(rows, rows, ws_dp[:, r:r + 1], INTER ** -0.5, ALU.mult, ALU.mult))
            chain.wait(pool)
            nc.gpsimd.drain().then_inc(fw_done, 1)
            def add_rotary(at, n, t):
                pool.wait_ge(at.sem["rope"], n + 1)
                nc.gpsimd.tensor_tensor(t1[:, t % 2, :], t1[:, t % 2, :], t2[:, t % 2, :], ALU.add).then_inc(at.sem["sum"], 1)

            def pool_round(at, it, extra, n_qkv):
                for kind, a in at.order(extra):
                    if kind == "scores":
                        pool.wait_ge(at.sem["inv"], it * at.units + a + 1)
                        n = P * at.keys(at.row_of(a))
                        p = at.prob(a)[:, 0:n]
                        nc.gpsimd.tensor_tensor(p, p, rinv[:, a:a + 1].to_broadcast([P, n]), ALU.mult).then_inc(at.sem["norm"], 1)
                    elif kind == "qkv":
                        add_rotary(at, n_qkv + a, a)

            with pool.Fori(0, B) as b:
                for t in range(TB):
                    add_rotary(a1, b * TB + t, t)
                pool_round(a1, b, {}, 0)
            with pool.Fori(0, B) as b:
                for t in range(TB):
                    add_rotary(a2, b * TB * G64 + t, t)
                with pool.Fori(0, G64 - 1) as g:
                    pool_round(a2, b * G64 + g, NEXT_QKV, (b * G64 + g + 1) * TB)
                pool_round(a2, b * G64 + G64 - 1, {}, 0)

        vch = Count(v_chain)

        def dve_norm(v, phase, eps, src=x, dst=xn, rms=False):
            for t in range(NT):
                if phase == 0 and t % TB == 0:
                    v.wait_ge(ld_x, 16 * (t // TB + 1))
                vch.inc(nc.vector.bn_stats(st[:, t, :], src[:, t, :]))
            vch.wait(v)
            for t in range(NT):
                vch.inc(nc.vector.bn_aggr(mv[:, t, :], st[:, t, :]))
            vch.wait(v)
            if rms:
                vch.inc(nc.vector.tensor_tensor(std[:], mv[:, :, 0], mv[:, :, 0], ALU.mult))
                vch.wait(v)
                vch.inc(nc.vector.tensor_tensor(var[:], mv[:, :, 1], std[:], ALU.add))
                vch.wait(v)
                nc.vector.tensor_scalar(var[:], var[:], eps, None, ALU.add).then_inc(ln_var, 1)
            else:
                nc.vector.tensor_scalar(var[:], mv[:, :, 1], eps, None, ALU.add).then_inc(ln_var, 1)
            v.wait_ge(ln_std, phase + 1)
            vch.inc(nc.vector.reciprocal(rstd[:], std[:]))
            vch.wait(v)
            for t in range(NT):
                if rms:
                    nc.vector.tensor_scalar(dst[:, t, :], src[:, t, :], rstd[:, t:t + 1], None, ALU.mult).then_inc(xn_all, 1)
                else:
                    nc.vector.tensor_scalar(dst[:, t, :], src[:, t, :], mv[:, t, 0:1], rstd[:, t:t + 1],
                                            ALU.subtract, ALU.mult).then_inc(xn_all, 1)
            v.wait_ge(xn_all, NT * (phase + 1))

        @block.vector
        def _(v):
            v.wait_ge(ld_s, 16 * 17)
            v.wait_ge(ld_c, 16)
            vch.inc(nc.vector.tensor_scalar(nslope_b[:], slope_b[:], -1.0, None, ALU.mult))
            vch.inc(nc.vector.tensor_scalar(nslope_p[:], slope_p[:], -1.0, None, ALU.mult))
            v.wait_ge(ld_w, 16 * 6)
            vch.inc(nc.vector.memset(wo_nat, 0.0))
            vch.wait(v)
            for blk in range(DC):
                ins = nc.vector.tensor_copy(
                    wo_nat[:, 4 * blk:4 * blk + 4, :].rearrange("p i (g d) -> p i g d", d=32)[:, :, :, 0:HD16],
                    wnat[:, 13 + blk, :].rearrange("p (g i d) -> p i g d", g=KV16, d=HD16))
            ins.then_inc(wo_spread, 1)
            dve_norm(v, 0, 1e-5)
            for n, (_src, c, blocks, dst) in enumerate(START):
                if n % 2 == 0:
                    v.wait_ge(wt_ps, n + 1)
                    nc.vector.tensor_copy(dst, bank[n % 8][:, 0:P * len(blocks)]).then_inc(wt_sb[0], 1)
            v.wait_ge(dec_exp, H16 + 2 * DC + 1)
            a, _b = mid("ge")
            vch.inc(nc.vector.tensor_tensor(DT, DT, con[:, None, a:_b].to_broadcast([P, H16, P]), ALU.mult))
            vch.wait(v)

            v.wait_ge(wt_ps, len(START))
            ch = Count(l0["chain"], 2)
            with v.Fori(0, B) as b:
                ch.n = 0
                v.wait_ge(l0["xT_ps"], b * DC + 1)
                nc.vector.tensor_copy(xn_st[:], xn[:, bass.ts(b, TB), :]).then_inc(l0["stage"], 1)
                v.wait_ge(l0["q_sb"], b * 4 + 2)
                nc.vector.tensor_tensor(qdT.rearrange("p c (t i) -> p c t i", t=TB),
                                        qT.rearrange("p c (t i) -> p c t i", t=TB),
                                        QD.unsqueeze(2).to_broadcast([P, DC, TB, P]), ALU.mult).then_inc(l0["qd"], 1)
                v.wait_ge(l0["q_sb"], b * 4 + 4)
                par = const("parity")
                for e in range(2):
                    nc.vector.tensor_scalar(kTm[:, e, :, :], kT, par[:, e:e + 1], None, ALU.mult).then_inc(l0["kTm"], 1)
                for t in range(TB):
                    v.wait_ge(l0["u_ps"], b * TB + t + 1)
                    nc.vector.tensor_copy(u0[:, t, :], bank[(7, 1)[t % 2]][:, 0:D]).then_inc(l0["u_sb"], 1)
                    v.wait_ge(l0["k_sb"], b * TB + t + 1)
                    nc.vector.tensor_tensor(kd[:, t, :].rearrange("p (h d) -> p h d", h=H16),
                                            ks[:, t % 2, :].rearrange("p (h d) -> p h d", h=H16),
                                            KD.unsqueeze(2).to_broadcast([P, H16, HD16]),
                                            ALU.mult).then_inc(l0["kd"], 1)

                def decay(t):
                    for g in range(4):
                        v.wait_ge(l0["s_ps"], b * 16 + 4 * t + g + 1)
                        if g == 0 and t >= 2:
                            v.wait_ge(l0["o_ps"], b * TB + t - 1)
                        nc.vector.tensor_tensor(PT0[:, t % 2, 4 * g:4 * g + 4, :],
                                                bank[g][:].rearrange("p (h i) -> p h i", h=4),
                                                DT[:, 4 * g:4 * g + 4, :], ALU.mult).then_inc(l0["pt"], 1)

                decay(0)
                for t in range(TB):
                    if t + 1 < TB:
                        decay(t + 1)
                    v.wait_ge(l0["o_ps"], b * TB + t + 1)
                    nc.vector.tensor_tensor(ou[:, t, :], bank[4 + t % 2][:, 0:D], u0[:, t, :],
                                            ALU.mult).then_inc(l0["ou"], 1)
                    if t < TB - 1:
                        v.wait_ge(l0["st_ps"], b * 3 + t + 1)
                        into = kvs if t == 0 else kvt
                        a, _b = mid("block")
                        kv_ins = nc.vector.tensor_tensor(into[:], bank[6][:, 0:D].rearrange("p (c e) -> p c e", c=DC),
                                                         con[:, None, a:_b].to_broadcast([P, DC, P]), ALU.mult)
                        if t == 0:
                            kv_ins.then_inc(l0["st"], 1)
                        else:
                            ch.inc(kv_ins)
                            ch.wait(v, b)
                            v.wait_ge(l0["st"], b * 5 + 2 * t - 1)
                            for c in range(DC):
                                nc.vector.scalar_tensor_tensor(kvs[:, c, :], kvs[:, c, :], BD[:, c:c + 1], kvt[:, c, :],
                                                               ALU.mult, ALU.add).then_inc(l0["st"], 1)
            l0_chain_check = ch.n
            assert l0_chain_check == 2

            v.wait_ge(l0["sq"], NT + 1)
            v.wait_ge(l0["y_sb"], 2 * B + 1)
            nc.vector.tensor_scalar(ss[:], ss[:], 1.0 / D, 1e-6, ALU.mult, ALU.add).then_inc(rms_in, 1)
            v.wait_ge(rms_std, 1)
            vch.inc(nc.vector.reciprocal(rstd[:], std[:]))
            vch.wait(v)
            for t in range(NT):
                vch.inc(nc.vector.scalar_tensor_tensor(x[:, t, :], y0[:, t, :], rstd[:, t:t + 1], x[:, t, :],
                                                       ALU.mult, ALU.add))
            vch.wait(v)
            for n, (_src, c, blocks, dst, sign) in enumerate(FFN):
                if n % 2 == 0:
                    v.wait_ge(wt_ps, len(START) + n + 1)
                    nc.vector.tensor_scalar(dst, bank[n % 8][:, 0:P * len(blocks)], sign, None, ALU.mult).then_inc(wt_sb[0], 1)
            dve_norm(v, 1, 1e-5)
            v.sem_inc(f0["y"], 1)
            with v.Fori(0, B) as b:
                v.wait_ge(f0["xT_ps"], b * DC + 1)
                nc.vector.tensor_copy(xn_st[:], xn[:, bass.ts(b, TB), :]).then_inc(f0["stage"], 1)
                for k in range(IC):
                    v.wait_ge(f0["silu"], b * IC + k + 1)
                    nc.vector.tensor_tensor(aT[:, k, :], bank[2 + 2 * (k % 2)][:], gsil[:, k % 2, :],
                                            ALU.mult).then_inc(f0["glu"], 1)
                for i in range(2):
                    v.wait_ge(f0["y_ps"], b * 2 + i + 1)
                    rows = x[:, bass.ds(b * TB + 2 * i, 2), :]
                    nc.vector.tensor_tensor(rows, rows, bank[6 + i][:].rearrange("p (t d) -> p t d", t=2),
                                            ALU.add).then_inc(f0["y"], 1)
            v.wait_ge(f0["y"], 2 * B + 1)
            def rope(at, n, t, v_dst):
                v.wait_ge(at.sem["qkv_ps"], n + 1)
                hd, h = at.hd, t % 2
                src = bank[YBANK][:, 0:320].rearrange("p (h d) -> p h d", d=hd)
                tab = lambda name, lo, hi: con[:, None, mid(name)[0] + t * hd + lo:mid(name)[0] + t * hd + hi].to_broadcast(
                    [P, 320 // hd, hi - lo])
                u1, u2 = (a[:, h, :].rearrange("p (h d) -> p h d", d=hd) for a in (t1, t2))
                name, half = str(hd), hd // 2
                nc.vector.tensor_tensor(u1, src, tab("cos" + name, 0, hd), ALU.mult)
                nc.vector.tensor_tensor(u2[:, :, 0:half], src[:, :, half:hd], tab("sin" + name, 0, half), ALU.mult)
                nc.vector.tensor_tensor(u2[:, :, half:hd], src[:, :, 0:half], tab("sin" + name, half, hd),
                                        ALU.mult).then_inc(at.sem["rope"], 1)
                vp = bank[YBANK][:, 320:384]
                nc.vector.tensor_copy(v_dst, vp.rearrange("p (g d) -> p g d", g=KV16) if at is a1 else vp).then_inc(at.sem["yb"], 1)

            def split_low(at, n, t):
                v.wait_ge(at.sem["hi"], n + 1)
                for dst, high, whole in parts(at, t):
                    ins = nc.vector.tensor_tensor(dst(1).bitcast(F32R), whole, high, ALU.subtract)
                ins.then_inc(at.sem["qk"], 1)

            def dve_round(at, it, b, extra, n_qkv, v_dst, res):

                def invert(m):
                    v.wait_ge(at.sem["exp"], it * at.units + m + 1)
                    nc.vector.reciprocal(rinv[:, m:m + 1], rowsum[:, m:m + 1]).then_inc(at.sem["inv"], 1)

                for kind, a in at.order(extra):
                    if kind == "scores":
                        v.wait_ge(at.sem["s_ps"], it * at.units + a + 1)
                        nc.vector.tensor_reduce(negmax[:, a:a + 1], bank[SBANK[a % 3]][:, 0:P * at.keys(at.row_of(a))],
                                                AX, ALU.max, negate=True).then_inc(at.sem["max"], 1)
                        if a >= 2:
                            invert(a - 2)
                        if a == at.units - 1:
                            invert(a - 1)
                            invert(a)
                    elif kind == "turn" and a % 2 == 0:
                        n0 = it * len(at.steps)
                        v.wait_ge(at.sem["t_ps"], n0 + a + 1)
                        if a >= 3:
                            v.wait_ge(at.sem["pv"], n0 + a - 2)
                        nc.vector.tensor_copy(probsT[:, a % 3, :], bank[PTBANK[0]][:]).then_inc(at.sem["pt_dve"], 1)
                    elif kind == "project":
                        r = at.quads[a * at.per_row][0]
                        v.wait_ge(at.sem["y_ps"], it * TB + a + 1)
                        rows = res[:, bass.ds(b * TB + r, 1), :]
                        nc.vector.tensor_tensor(rows, rows, bank[YBANK][:, None, 0:D], ALU.add).then_inc(at.sem["yb"], 1)
                    elif kind == "qkv":
                        rope(at, n_qkv + a, a, v_dst(a))
                    elif kind == "split":
                        split_low(at, n_qkv + a, a)

            def narrow_turned(n, t):
                for i in (1, 3):
                    v.wait_ge(a1.sem["m_ps"], (n + t) * 5 + i + 1)
                    nc.vector.tensor_scalar(narrow_q[:, 4 * i:4 * i + 4, P * t:P * t + P],
                                            bank[i][:].rearrange("p (h n) -> p h n", h=4), HD16 ** -0.5, None,
                                            ALU.mult).then_inc(a1.sem["m_sbd"], 1)

            vch.inc(nc.vector.tensor_copy(causal[:], const("causal")))
            vch.inc(nc.vector.tensor_copy(ident_h[:], ident))
            vch.inc(nc.vector.memset(narrow_x, 0.0))
            vch.inc(nc.vector.memset(narrow_v, 0.0))
            dve_norm(v, 2, 1e-5)
            v.sem_inc(a1.sem["yb"], 1)
            with v.Fori(0, B) as b:
                v.wait_ge(a1.sem["xT_ps"], b * DC + 1)
                nc.vector.tensor_copy(xn_st[:], xn[:, bass.ts(b, TB), :]).then_inc(a1.sem["stage"], 1)
                for kind, t in FIRST_QKV:
                    if kind == "qkv":
                        rope(a1, b * TB + t, t, narrow_v[:, t, :, 0:HD16])
                    elif kind == "split":
                        split_low(a1, b * TB + t, t)
                    elif kind == "turn_q":
                        narrow_turned(b * TB, t)
                dve_round(a1, b, b, {}, 0, None, x)
            v.wait_ge(a1.sem["yb"], A1_Y * B + 1)
            dve_norm(v, 3, 1e-5)
            dve_norm(v, 4, 1e-5, xn, hn, rms=True)
            v.sem_inc(a2.sem["yb"], 1)
            with v.Fori(0, B) as b:
                v.wait_ge(a2.sem["xT_ps"], b * DC + 1)
                nc.vector.tensor_copy(xn_st[:], hn[:, bass.ts(b, TB), :]).then_inc(a2.sem["stage"], 1)
                for kind, t in FIRST_QKV:
                    if kind == "qkv":
                        rope(a2, b * TB * G64 + t, t, wide_v[:, 0, t, :])
                    elif kind == "split":
                        split_low(a2, b * TB * G64 + t, t)

                def group(g, par, extra):
                    dve_round(a2, b * G64 + g, b, extra, (b * G64 + g + 1) * TB, lambda t: wide_v[:, 1 - par, t, :], xn)

                with v.Fori(0, G64 // 2 - 1) as pair:
                    for par in range(2):
                        group(pair * 2 + par, par, NEXT_QKV)
                group(G64 - 2, 0, NEXT_QKV)
                group(G64 - 1, 1, {})
            v.wait_ge(a2.sem["yb"], A2_Y * B + 1)
            for t in range(NT):
                vch.inc(nc.vector.tensor_tensor(x[:, t, :], x[:, t, :], xn[:, t, :], ALU.add))
            vch.wait(v)
            dve_norm(v, 5, 1e-5, xn, hn, rms=True)

            def step(ins):
                vch.inc(ins)
                vch.wait(v)

            v.wait_ge(m5["lg_ps"], 1)
            step(nc.vector.tensor_copy(logits, bank[4][:, 0:NT * E].rearrange("p (t e) -> p t e", e=E)))
            for t in range(NT):
                vch.inc(nc.vector.max(best[:, t, :], logits[:, t, :]))
            vch.wait(v)
            wide = lambda col: col.to_broadcast([P, NT, E])
            least = wide(best[:, :, TOPK - 1:TOPK])
            vch.inc(nc.vector.tensor_tensor(above, logits, least, ALU.is_gt))
            vch.inc(nc.vector.tensor_tensor(ties, logits, least, ALU.is_equal))
            step(nc.vector.tensor_tensor(gate, logits, wide(best[:, :, 0:1]), ALU.subtract))
            nc.vector.tensor_reduce(room[:], above, AX, ALU.add).then_inc(m5["shift"], 1)
            v.wait_ge(m5["shift"], 1)
            step(nc.vector.tensor_scalar(room[:], room[:], -1.0, float(TOPK), ALU.mult, ALU.add))
            src, dst = ties, run_a
            for sh in (1, 2, 4, 8):
                vch.inc(nc.vector.tensor_copy(dst[:, :, 0:sh], src[:, :, 0:sh]))
                step(nc.vector.tensor_tensor(dst[:, :, sh:E], src[:, :, sh:E], src[:, :, 0:E - sh], ALU.add))
                src, dst = dst, (run_b if dst is run_a else run_a)
            step(nc.vector.tensor_tensor(dst, src, wide(room[:].unsqueeze(2)), ALU.is_le))
            step(nc.vector.tensor_tensor(dst, dst, ties, ALU.mult))
            step(nc.vector.tensor_tensor(above, above, dst, ALU.add))
            v.wait_ge(m5["exp"], 1)
            step(nc.vector.tensor_tensor(gate, gate, above, ALU.mult))
            step(nc.vector.tensor_reduce(room[:], gate, AX, ALU.add))
            step(nc.vector.reciprocal(room[:], room[:]))
            step(nc.vector.tensor_tensor(gate, gate, wide(room[:].unsqueeze(2)), ALU.mult))

            v.sem_inc(m5["acc"], 17)
            with v.Fori(0, E // 2) as pair:
                for i in range(2 * B + 1):
                    if i < 2 * B:
                        for hc in range(2):
                            v.wait_ge(m5["silu"], pair * 4 * B + 2 * i + hc + 1)
                            nc.vector.tensor_tensor(aT5[:, i % 2, hc, :], bank[2 * hc + 1][:], gs5[:, hc, :],
                                                    ALU.mult).then_inc(m5["glu"], 1)
                    i -= 1
                    if i >= 0:
                        par, b = i // B, i % B
                        if b == 0:
                            nc.vector.tensor_copy(gcol[:, par, :], gate[:, :, bass.ds(pair * 2 + par, 1)].rearrange(
                                "p t e -> p (t e)")).then_inc(m5["gcol"], 1)
                            v.wait_ge(m5["gcol"], pair * 2 + par + 1)
                        v.wait_ge(m5["acc"], pair * 8 * B + TB * i + 1)
                        for t in range(TB):
                            if t % 2 == 0:
                                v.wait_ge(m5["y_ps"], pair * 4 * B + 2 * i + t // 2 + 1)
                            n = TB * b + t
                            nc.vector.scalar_tensor_tensor(
                                x[:, n, :], bank[4 + 2 * (i % 2) + t // 2][:, D * (t % 2):D * (t % 2) + D],
                                gcol[:, par, n:n + 1], x[:, n, :], ALU.mult, ALU.add).then_inc(m5["acc"], 1)
            v.wait_ge(m5["acc"], 17 + NT * E)
            v.drain().then_inc(stored, 1)

        @block.scalar
        def _(act):
            act.wait_ge(ld_c, 16)
            act.wait_ge(v_chain, 2)
            for slot in range(H16):
                h = head_of(slot)
                nc.scalar.activation(DT[:, slot, :], const("lag"), ACT.Exp,
                                     scale=nslope_b[:, h:h + 1]).then_inc(dec_exp, 1)
            for c in range(DC):
                nc.scalar.activation(QD[:, c, :], const("ramp"), ACT.Exp, scale=nslope_p[:, c:c + 1]).then_inc(dec_exp, 1)
                nc.scalar.activation(BD[:, c:c + 1], nslope_p[:, c:c + 1], ACT.Exp, scale=float(P)).then_inc(dec_exp, 1)
            nc.scalar.activation(KD, nslope_b[:], ACT.Exp, scale=const("left")).then_inc(dec_exp, 1)
            act.wait_ge(ln_var, 1)
            nc.scalar.activation(std[:], var[:], ACT.Sqrt).then_inc(ln_std, 1)
            for n, (_src, c, blocks, dst) in enumerate(START):
                if n % 2 == 1:
                    act.wait_ge(wt_ps, n + 1)
                    nc.scalar.activation(dst, bank[n % 8][:, 0:P * len(blocks)], ACT.Copy).then_inc(wt_sb[1], 1)

            def turn_evac(sems, b, scale=None):
                for c in range(DC):
                    act.wait_ge(sems["xT_ps"], b * DC + c + 2)
                    if scale is None:
                        ins = nc.scalar.activation(xnT[:, c, :], bank[c][:], ACT.Copy)
                    else:
                        ins = nc.scalar.activation(xnT[:, c, :], bank[c][:], ACT.Identity, scale=scale[:, c:c + 1])
                    ins.then_inc(sems["xT_sb"], 1)

            act.sem_inc(l0["y_sb"], 1)
            act.sem_inc(l0["sq"], 1)
            with act.Fori(0, B) as b:
                turn_evac(l0, b)
                for m in range(4):
                    act.wait_ge(l0["qk_ps"], b * 4 + m + 1)
                    nc.scalar.activation((qT, kT)[m // 2][:, m % 2, :], bank[2 + m][:], ACT.Silu).then_inc(l0["q_sb"], 1)
                for t in range(TB):
                    act.wait_ge(l0["kv_ps"], b * TB + t + 1)
                    if t >= 2:
                        act.wait_ge(l0["kd"], b * TB + t - 1)
                    kvb = bank[(6, 0)[t % 2]]
                    nc.scalar.activation(ks[:, t % 2, :], kvb[:, 0:D], ACT.Silu).then_inc(l0["k_sb"], 1)
                    nc.scalar.activation(v0[:, t, :], kvb[:, D:2 * D], ACT.Copy).then_inc(l0["v_sb"], 1)
                for t in range(TB):
                    act.wait_ge(l0["ou"], b * TB + t + 1)
                    act.wait_ge(l0["sq"], b * TB + t + 1)
                    nc.scalar.activation(osq, bank[4 + t % 2][:, 0:D], ACT.Square,
                                         accum_out=ss[:, bass.ds(b * TB + t, 1)]).then_inc(l0["sq"], 1)
                for c in range(DC):
                    act.wait_ge(l0["ouT_ps"], b * DC + c + 1)
                    nc.scalar.activation(ouT[:, c, :], bank[6 + c][:], ACT.Copy).then_inc(l0["ouT_sb"], 1)
                for i in range(2):
                    act.wait_ge(l0["y_ps"], b * 2 + i + 1)
                    nc.scalar.activation(y0[:, bass.ds(b * TB + 2 * i, 2), :],
                                         bank[i][:].rearrange("p (t d) -> p t d", t=2), ACT.Copy).then_inc(l0["y_sb"], 1)
            act.wait_ge(rms_in, 1)
            nc.scalar.activation(std[:], ss[:], ACT.Sqrt).then_inc(rms_std, 1)
            for n, (_src, c, blocks, dst, sign) in enumerate(FFN):
                if n % 2 == 1:
                    act.wait_ge(wt_ps, len(START) + n + 1)
                    nc.scalar.activation(dst, bank[n % 8][:, 0:P * len(blocks)], ACT.Identity, scale=sign).then_inc(wt_sb[1], 1)
            act.wait_ge(ln_var, 2)
            nc.scalar.activation(std[:], var[:], ACT.Sqrt).then_inc(ln_std, 1)
            with act.Fori(0, B) as b:
                turn_evac(f0, b)
                for k in range(IC):
                    act.wait_ge(f0["up"], b * IC + k + 1)
                    if k >= 2:
                        act.wait_ge(f0["glu"], b * IC + k - 1)
                    nc.scalar.activation(gsil[:, k % 2, :], bank[3 + 2 * (k % 2)][:], ACT.Silu).then_inc(f0["silu"], 1)
            def split_high(at, n, t):
                act.wait_ge(at.sem["sum"], n + 1)
                for dst, _high, whole in parts(at, t):
                    ins = nc.scalar.activation(dst(0).bitcast(F32R), whole, ACT.Copy)
                ins.then_inc(at.sem["hi"], 1)

            def narrow_turned(n, t):
                cols = slice(P * t, P * t + P)
                for i in (0, 2, 4):
                    act.wait_ge(a1.sem["m_ps"], (n + t) * 5 + i + 1)
                    dst = narrow_k[:, :, cols] if i == 4 else narrow_q[:, 4 * i:4 * i + 4, cols]
                    nc.scalar.activation(dst, bank[i][:].rearrange("p (h n) -> p h n", h=4), ACT.Copy,
                                         scale=1.0 if i == 4 else HD16 ** -0.5).then_inc(a1.sem["m_sb"], 1)

            def wide_turned(kind, n_m, t, par):
                act.wait_ge(a2.sem["m_ps"], n_m + 1)
                cols = slice(P * t, P * t + P)
                if kind == "turn_q":
                    ins = nc.scalar.activation(wide_q[:, par, :, cols], bank[MBANK][:].rearrange("p (h n) -> p h n", h=R64),
                                               ACT.Copy, scale=HD64 ** -0.5)
                else:
                    ins = nc.scalar.activation(wide_k[:, par, :, cols],
                                               bank[MBANK][:, 0:2 * P].rearrange("p (h n) -> p h n", h=2), ACT.Copy)
                ins.then_inc(a2.sem["m_sb"], 1)

            def act_round(at, it, extra, n_qkv, n_m, par):
                n0 = it * len(at.steps)

                def exponentials(m):
                    n = P * at.keys(at.row_of(m))
                    act.wait_ge(at.sem["max"], it * at.units + m + 1)
                    if m >= 12:
                        act.wait_ge(at.sem["t_ps"], n0 + at.last_step(m // 4 - 3) + 1)
                    nc.scalar.activation(at.prob(m)[:, 0:n], bank[SBANK[m % 3]][:, 0:n], ACT.Exp, bias=negmax[:, m:m + 1],
                                         accum_out=rowsum[:, m:m + 1]).then_inc(at.sem["exp"], 1)

                held = None
                for kind, a in at.order(extra):
                    if kind == "scores":
                        if held is not None:
                            exponentials(held)
                        held = a
                    elif kind == "turn" and a % 2 == 1:
                        act.wait_ge(at.sem["t_ps"], n0 + a + 1)
                        if a >= 3:
                            act.wait_ge(at.sem["pv"], n0 + a - 2)
                        nc.scalar.activation(probsT[:, a % 3, :], bank[PTBANK[1]][:], ACT.Copy).then_inc(at.sem["pt_act"], 1)
                    if kind in ("turn", "values") and held is not None:
                        exponentials(held)
                        held = None
                    if kind == "values":
                        q = at.steps[a][0]
                        if a == at.last_step(q) and (q + 1) % at.per_row == 0:
                            i = q // at.per_row
                            act.wait_ge(at.sem["pv"], n0 + a + 1)
                            if i >= 2:
                                act.wait_ge(at.sem["y_ps"], it * TB + i - 1)
                            n = S if at is a1 else D
                            nc.scalar.activation(onT[:, i % 2, 0:n], bank[OBANK][:, 0:n], ACT.Copy).then_inc(at.sem["o_sb"], 1)
                    elif kind == "split":
                        split_high(at, n_qkv + a, a)
                    elif kind in ("turn_q", "turn_k"):
                        wide_turned(kind, n_m, a, 1 - par)
                        n_m = n_m + 1

            act.wait_ge(ln_var, 3)
            nc.scalar.activation(std[:], var[:], ACT.Sqrt).then_inc(ln_std, 1)
            with act.Fori(0, B) as b:
                turn_evac(a1.sem, b)
                for kind, t in FIRST_QKV:
                    if kind == "split":
                        split_high(a1, b * TB + t, t)
                    elif kind == "turn_q":
                        narrow_turned(b * TB, t)
                act_round(a1, b, {}, 0, 0, 0)
            for n in (4, 5):
                act.wait_ge(ln_var, n)
                nc.scalar.activation(std[:], var[:], ACT.Sqrt).then_inc(ln_std, 1)
            act.wait_ge(ld_l1, 16 * 10)
            act.sem_inc(a2.sem["m_sb"], 1)
            with act.Fori(0, B) as b:
                turn_evac(a2.sem, b, lnw)
                n_m = b * A2_M
                for kind, t in FIRST_QKV:
                    if kind == "split":
                        split_high(a2, b * TB * G64 + t, t)
                    elif kind in ("turn_q", "turn_k"):
                        wide_turned(kind, n_m, t, 0)
                        n_m = n_m + 1

                def group(g, par, extra):
                    act_round(a2, b * G64 + g, extra, (b * G64 + g + 1) * TB, b * A2_M + (g + 1) * 2 * TB, par)

                with act.Fori(0, G64 // 2 - 1) as pair:
                    for par in range(2):
                        group(pair * 2 + par, par, NEXT_QKV)
                group(G64 - 2, 0, NEXT_QKV)
                group(G64 - 1, 1, {})
            act.wait_ge(ln_var, 6)
            nc.scalar.activation(std[:], var[:], ACT.Sqrt).then_inc(ln_std, 1)
            for b in range(B):
                for c in range(DC):
                    act.wait_ge(m5["hT_ps"], DC * b + c + 1)
                    nc.scalar.activation(hT5[:, c, S * b:S * b + S], bank[2 * (b % 2) + c][:], ACT.Identity,
                                         scale=fflnw[:, c:c + 1]).then_inc(m5["hT_sb"], 1)
            act.wait_ge(m5["shift"], 1)
            nc.scalar.activation(gate, gate, ACT.Exp).then_inc(m5["exp"], 1)
            with act.Fori(0, E // 2) as pair:
                for i in range(2 * B):
                    for hc in range(2):
                        act.wait_ge(m5["up_ps"], pair * 4 * B + 2 * i + hc + 1)
                        if i >= 1:
                            act.wait_ge(m5["glu"], pair * 4 * B + 2 * i + hc - 1)
                        nc.scalar.activation(gs5[:, hc, :], bank[2 * hc][:], ACT.Silu).then_inc(m5["silu"], 1)
        @block.tensor
        def _(pe):
            pe.wait_ge(ld_c, 16)

            def turn_weights(turns, n0):
                for n, (src, c, blocks, *_rest) in enumerate(turns):
                    if n >= 8:
                        pe.wait_ge(wt_sb[n % 2], (n0 + n - 8) // 2 + 1)
                    for i, blk in enumerate(blocks):
                        ins = nc.tensor.transpose(bank[n % 8][:, P * i:P * i + P], src[:, blk, P * c:P * c + P], ident)
                    ins.then_inc(wt_ps, 1)

            pe.wait_ge(ld_w, 16 * 6)
            pe.wait_ge(wo_spread, 1)
            turn_weights(START, 0)
            for half in wt_sb:
                pe.wait_ge(half, len(START) // 2)

            def turn_x(sems, b):
                pe.wait_ge(sems["stage"], b + 1)
                for c in range(DC):
                    for t in range(TB):
                        ins = nc.tensor.transpose(bank[c][:, P * t:P * t + P], xn_st[:, t, P * c:P * c + P], ident)
                    ins.then_inc(sems["xT_ps"], 1)
                pe.wait_ge(sems["xT_sb"], b * DC + DC)

            pe.sem_inc(l0["xT_ps"], 1)
            with pe.Fori(0, B) as b:
                pe.wait_ge(l0["y_sb"], b * 2 + 1)
                turn_x(l0, b)
                for m in range(4):
                    for c in range(DC):
                        ins = nc.tensor.matmul(bank[2 + m][:], wqkvuT[:, c, P * m:P * m + P], xnT[:, c, :],
                                               start=(c == 0), stop=(c == DC - 1))
                    ins.then_inc(l0["qk_ps"], 1)
                for t in range(TB):
                    if t >= 2:
                        pe.wait_ge(l0["v_sb"], b * TB + t - 1)
                        pe.wait_ge(l0["u_sb"], b * TB + t - 1)
                    for c in range(DC):
                        ins = nc.tensor.matmul(bank[(6, 0)[t % 2]][:], xnT[:, c, P * t:P * t + P],
                                               wqkvuT[:, c, D:3 * D], start=(c == 0), stop=(c == DC - 1))
                    ins.then_inc(l0["kv_ps"], 1)
                    for c in range(DC):
                        ins = nc.tensor.matmul(bank[(7, 1)[t % 2]][:, 0:D], xnT[:, c, P * t:P * t + P],
                                               wqkvuT[:, c, 3 * D:4 * D], start=(c == 0), stop=(c == DC - 1))
                    ins.then_inc(l0["u_ps"], 1)

                def scores(t):
                    for r in range(4):
                        for g in range(4):
                            if r == 0 and t >= 1:
                                pe.wait_ge(l0["pt"], b * 16 + 4 * (t - 1) + g + 1)
                            c, odd = r // 2, r % 2
                            rows = slice(32 * g, 32 * g + 32)
                            ins = nc.tensor.matmul(bank[g][:, P * r:P * r + P], kTm[rows, odd, c, P * t:P * t + P],
                                                   qT[rows, c, P * t:P * t + P], start=True, stop=True)
                            if r == 3:
                                ins.then_inc(l0["s_ps"], 1)

                pe.wait_ge(l0["kTm"], b * 2 + 2)
                pe.wait_ge(l0["v_sb"], b * TB + TB)
                pe.wait_ge(l0["u_sb"], b * TB + TB)
                scores(0)
                for t in range(TB):
                    if t < TB - 1:
                        pe.wait_ge(l0["kd"], b * TB + t + 1)
                        if t >= 1:
                            pe.wait_ge(l0["st"], b * 5 + 2 * t - 1)
                        for c in range(DC):
                            ins = nc.tensor.matmul(bank[6][:, P * c:P * c + P], kd[:, t, P * c:P * c + P],
                                                   v0[:, t, P * c:P * c + P], start=True, stop=True)
                        ins.then_inc(l0["st_ps"], 1)
                    if t + 1 < TB:
                        scores(t + 1)
                    pe.wait_ge(l0["pt"], b * 16 + 4 * t + 4)
                    if t >= 2:
                        pe.wait_ge(l0["sq"], b * TB + t)
                    o = bank[4 + t % 2]
                    for slot in range(H16):
                        h = head_of(slot)
                        cols = slice(HD16 * h, HD16 * h + HD16)
                        ins = nc.tensor.matmul(o[:, cols], PT0[:, t % 2, slot, :], v0[:, t, cols], start=(slot == 0),
                                               stop=(t == 0 and slot == H16 - 1), skip_group_check=True)
                    if t >= 1:
                        pe.wait_ge(l0["st"], b * 5 + 2 * t - 1)
                        pe.wait_ge(l0["qd"], b + 1)
                        for c in range(DC):
                            ins = nc.tensor.matmul(o[:, P * c:P * c + P], qdT[:, c, P * t:P * t + P], kvs[:, c, :],
                                                   start=False, stop=(c == DC - 1), skip_group_check=True)
                    ins.then_inc(l0["o_ps"], 1)
                pe.wait_ge(l0["ou"], b * TB + TB)
                for c in range(DC):
                    for t in range(TB):
                        ins = nc.tensor.transpose(bank[6 + c][:, P * t:P * t + P], ou[:, t, P * c:P * c + P], ident)
                    ins.then_inc(l0["ouT_ps"], 1)
                pe.wait_ge(l0["ouT_sb"], b * DC + DC)
                for t in range(TB):
                    for c in range(DC):
                        ins = nc.tensor.matmul(bank[t // 2][:, D * (t % 2):D * (t % 2) + D], ouT[:, c, P * t:P * t + P],
                                               wout0T[:, c, :], start=(c == 0), stop=(c == DC - 1))
                    if t % 2:
                        ins.then_inc(l0["y_ps"], 1)
            pe.wait_ge(l0["y_sb"], 2 * B + 1)
            pe.wait_ge(l0["sq"], NT + 1)
            pe.wait_ge(fw_done, 1)
            turn_weights(FFN, len(START))
            for half in wt_sb:
                pe.wait_ge(half, (len(START) + len(FFN)) // 2)
            pe.sem_inc(f0["xT_ps"], 1)
            with pe.Fori(0, B) as b:
                turn_x(f0, b)
                for k in range(IC):
                    if k >= 2:
                        pe.wait_ge(f0["glu"], b * IC + k - 1)
                    for j in range(2):
                        for c in range(DC):
                            ins = nc.tensor.matmul(bank[2 + 2 * (k % 2) + j][:],
                                                   wugT[:, c, INTER * j + P * k:INTER * j + P * k + P], xnT[:, c, :],
                                                   start=(c == 0), stop=(c == DC - 1))
                    ins.then_inc(f0["up"], 1)
                pe.wait_ge(f0["glu"], b * IC + IC)
                pe.wait_ge(f0["y"], b * 2 + 1)
                for t in range(TB):
                    for k in range(IC):
                        ins = nc.tensor.matmul(bank[6 + t // 2][:, D * (t % 2):D * (t % 2) + D], aT[:, k, P * t:P * t + P],
                                               wdT[:, k, :], start=(k == 0), stop=(k == IC - 1))
                    if t % 2:
                        ins.then_inc(f0["y_ps"], 1)
            def project_qkv(at, n_y, t, w):
                pe.wait_ge(at.sem["yb"], n_y + 1)
                for c in range(DC):
                    ins = nc.tensor.matmul(bank[YBANK][:, 0:QKV], xnT[:, c, P * t:P * t + P], w(c),
                                           start=(c == 0), stop=(c == DC - 1))
                ins.then_inc(at.sem["qkv_ps"], 1)

            def wide_turn(kind, n_qkv, n_m, t):
                pe.wait_ge(a2.sem["qk"], n_qkv + 1)
                pe.wait_ge(a2.sem["m_sb"], n_m + 1)
                for i in range(R64) if kind == "turn_q" else range(2):
                    z = P * (i if kind == "turn_q" else R64 + i)
                    ins = nc.tensor.transpose(bank[MBANK][:, P * i:P * i + P], wide_x[:, t % 2, z:z + P], ident)
                ins.then_inc(a2.sem["m_ps"], 1)

            def narrow_turn(n, t):
                pe.wait_ge(a1.sem["qk"], n + t + 1)
                for i in range(5):
                    if t >= 1:
                        e = (n + t - 1) * (3, 2)[i % 2] + i // 2 + 1
                        pe.wait_ge(a1.sem[("m_sb", "m_sbd")[i % 2]], e)
                    for h in range(4):
                        z = P * (4 * i + h)
                        ins = nc.tensor.transpose(bank[i][:, P * h:P * h + P], narrow_x[:, t % 2, z:z + P], ident)
                    ins.then_inc(a1.sem["m_ps"], 1)

            def pe_round(at, it, extra, n_m, n_y, n_qkv, par, w_next, w_out):
                n0 = it * len(at.steps)
                pe.wait_ge(at.sem["yb"], n_y + 1)
                for kind, a in at.order(extra):
                    if kind == "scores":
                        q, i, sbank = a // 4, a % 4, bank[SBANK[a % 3]]
                        r, g = at.quads[q]
                        n = P * at.keys(r)
                        qcols = slice(P * r, P * r + P)
                        if a >= 3:
                            pe.wait_ge(at.sem["exp"], it * at.units + a - 2)
                        if at is a1:
                            ins = nc.tensor.matmul(sbank[:], narrow_q[:, 4 * g + i, qcols], narrow_k[:, g, :],
                                                   start=True, stop=True)
                        else:
                            for w in range(2):
                                nc.tensor.matmul(sbank[:, 0:n], wide_q[:, par, i, qcols], wide_k[:, par, w, 0:n],
                                                 start=(w == 0), stop=False)
                            ins = nc.tensor.matmul(sbank[:, n - P:n], ident_h[:], causal[:], start=False, stop=True)
                        ins.then_inc(at.sem["s_ps"], 1)
                    elif kind == "turn":
                        q, k = at.steps[a]
                        pe.wait_ge(at.sem["norm"], it * at.units + 4 * q + 4)
                        if a >= 2:
                            pe.wait_ge(at.sem[("pt_dve", "pt_act")[a % 2]], it * (len(at.steps) // 2) + a // 2)
                        for i in range(4):
                            ins = nc.tensor.transpose(bank[PTBANK[a % 2]][:, P * i:P * i + P],
                                                      at.prob(4 * q + i)[:, P * k:P * k + P], ident)
                        ins.then_inc(at.sem["t_ps"], 1)
                    elif kind == "values":
                        q, k = at.steps[a]
                        r, g = at.quads[q]
                        pe.wait_ge(at.sem[("pt_dve", "pt_act")[a % 2]], it * (len(at.steps) // 2) + a // 2 + 1)
                        if q >= at.per_row and k == 0:
                            pe.wait_ge(at.sem["o_sb"], it * TB + q // at.per_row)
                        flags = dict(start=(k == 0), stop=(k == at.keys(r) - 1))
                        if at is a1:
                            ins = nc.tensor.matmul(bank[OBANK][32 * g:32 * g + 32, :], narrow_v[:, k, g, :],
                                                   probsT[:, a % 3, :], **flags)
                        else:
                            for e in range(2):
                                ins = nc.tensor.matmul(bank[OBANK][HD64 * e:HD64 * e + HD64, 0:D], wide_v[:, par, k, :],
                                                       probsT[:, a % 3, :].rearrange("p (c e n) -> p e c n", e=2, n=P)[:, e],
                                                       **flags)
                        ins.then_inc(at.sem["pv"], 1)
                    elif kind == "project":
                        pe.wait_ge(at.sem["o_sb"], it * TB + a + 1)
                        pe.wait_ge(at.sem["yb"], n_y + 1)
                        chunks = 4 if at is a1 else DC
                        for c in range(chunks):
                            ins = nc.tensor.matmul(bank[YBANK][:, 0:D], onT[:, a % 2, P * c:P * c + P], w_out(c),
                                                   start=(c == 0), stop=(c == chunks - 1))
                        ins.then_inc(at.sem["y_ps"], 1)
                        n_y = n_y + 1
                    elif kind == "qkv":
                        project_qkv(at, n_y, a, w_next)
                        n_y = n_y + 1
                    elif kind in ("turn_q", "turn_k"):
                        wide_turn(kind, n_qkv + a, n_m, a)
                        n_m = n_m + 1

            pe.wait_ge(f0["y"], 2 * B + 1)
            pe.sem_inc(a1.sem["xT_ps"], 1)
            with pe.Fori(0, B) as b:
                turn_x(a1.sem, b)
                for kind, t in FIRST_QKV:
                    if kind == "qkv":
                        project_qkv(a1, b * A1_Y + t, t, lambda c: wqkv1T[:, c, :])
                    elif kind == "turn_q":
                        narrow_turn(b * TB, t)
                pe.wait_ge(a1.sem["m_sb"], (b + 1) * 3 * TB)
                pe.wait_ge(a1.sem["m_sbd"], (b + 1) * 2 * TB)
                pe_round(a1, b, {}, 0, b * A1_Y + TB, 0, 0, None, lambda c: wo1p[:, c, :])
            pe.wait_ge(ld_l1, 16 * 10)
            pe.sem_inc(a2.sem["xT_ps"], 1)
            with pe.Fori(0, B) as b:
                turn_x(a2.sem, b)
                n_m, n_y = b * A2_M, b * A2_Y
                for kind, t in FIRST_QKV:
                    if kind == "qkv":
                        project_qkv(a2, n_y, t, lambda c: wgrp[:, c, 0, :])
                        n_y = n_y + 1
                    elif kind in ("turn_q", "turn_k"):
                        wide_turn(kind, b * TB * G64 + t, n_m, t)
                        n_m = n_m + 1

                def group(g, par, extra):
                    n_m = b * A2_M + (g + 1) * 2 * TB
                    pe.wait_ge(a2.sem["m_sb"], n_m + 1)
                    pe_round(a2, b * G64 + g, extra, n_m, b * A2_Y + TB + g * 2 * TB, (b * G64 + g + 1) * TB, par,
                             lambda c: wgrp[:, c, bass.ds(g + 1, 1), :].rearrange("p a n -> p (a n)"),
                             lambda c: wo_sb[:, bass.ds(g * 2 + c, 1), :].rearrange("p a n -> p (a n)"))

                with pe.Fori(0, G64 // 2 - 1) as pair:
                    for par in range(2):
                        group(pair * 2 + par, par, NEXT_QKV)
                group(G64 - 2, 0, NEXT_QKV)
                group(G64 - 1, 1, {})
            for b in range(B):
                pe.wait_ge(xn_all, 5 * NT + TB * b + TB)
                if b >= 2:
                    pe.wait_ge(m5["hT_sb"], DC * (b - 1))
                for c in range(DC):
                    for t in range(TB):
                        ins = nc.tensor.transpose(bank[2 * (b % 2) + c][:, P * t:P * t + P],
                                                  hn[:, TB * b + t, P * c:P * c + P], ident)
                    ins.then_inc(m5["hT_ps"], 1)
            pe.wait_ge(m5["hT_sb"], DC * B)
            for t in range(NT):
                for c in range(DC):
                    ins = nc.tensor.matmul(bank[4][:, E * t:E * t + E], hT5[:, c, P * t:P * t + P], wg_sb[:, c, :],
                                           start=(c == 0), stop=(c == DC - 1))
            ins.then_inc(m5["lg_ps"], 1)
            pe.wait_ge(m5["exp"], 1)
            with pe.Fori(0, E // 2) as pair:
                for i in range(2 * B + 1):
                    if i < 2 * B:
                        par, b = i // B, i % B
                        if b == 0:
                            pe.wait_ge(ld_e[par], pair * 48 + 48)
                        for hc in range(2):
                            if i >= 1:
                                pe.wait_ge(m5["glu"], pair * 4 * B + 2 * i + hc - 1)
                            for j in range(2):
                                for c in range(DC):
                                    ins = nc.tensor.matmul(bank[2 * hc + j][:], w13[:, par, DC * j + c, P * hc:P * hc + P],
                                                           hT5[:, c, S * b:S * b + S], start=(c == 0), stop=(c == DC - 1))
                            ins.then_inc(m5["up_ps"], 1)
                    i -= 1
                    if i >= 0:
                        par = i // B
                        pe.wait_ge(m5["glu"], pair * 4 * B + 2 * i + 2)
                        pe.wait_ge(m5["acc"], pair * 8 * B + TB * i + 17 - 2 * TB)
                        for t in range(TB):
                            for hc in range(2):
                                ins = nc.tensor.matmul(bank[4 + 2 * (i % 2) + t // 2][:, D * (t % 2):D * (t % 2) + D],
                                                       aT5[:, i % 2, hc, P * t:P * t + P], w2s[:, par, hc, :],
                                                       start=(hc == 0), stop=(hc == 1))
                            if t % 2:
                                ins.then_inc(m5["y_ps"], 1)

_INS = ["L0_attn_x", "L0_attn_slope_rate", "L0_attn_W_qkvu", "L0_attn_W_out", "L0_ffn_SU_ug", "L0_ffn_SU_dp",
        "L0_ffn_Wscale_ug", "L0_ffn_Wscale_dp", "L0_ffn_W_up", "L0_ffn_W_gate", "L0_ffn_W_down", "L1_attn_Wq",
        "L1_attn_Wk", "L1_attn_Wv", "L1_attn_Wo", "L1_ffn_ln_w", "L1_ffn_ff_ln_w", "L1_ffn_wq", "L1_ffn_wk",
        "L1_ffn_wv", "L1_ffn_wo", "L1_ffn_wg", "L1_ffn_w1", "L1_ffn_w3", "L1_ffn_w2"]
_OUTS = [((B, S, D), "float32")]


def shape_constants(np):
    f = np.float32
    c = np.zeros((P, NCONST), f)

    def put(name, a):
        lo, hi = CONST_COLS[name]
        c[:, lo:hi] = np.asarray(a, f).reshape(P, hi - lo)

    p, i = np.arange(P)[:, None], np.arange(P)[None, :]
    put("ident", p == i)
    put("lag", np.maximum(i - p, 0))
    put("ge", i >= p)
    put("causal", np.where(i <= p, 0.0, -1e30))
    put("block", p // HD16 == i // HD16)
    put("ramp", np.broadcast_to(i + 1, (P, P)))
    put("left", P - 1 - np.arange(P))
    put("parity", np.stack([(p[:, 0] // HD16) % 2 == 0, (p[:, 0] // HD16) % 2 == 1], 1))
    for name, hd, inv in (
            ("16", HD16, f(1.0) / f(10000.0) ** (np.arange(0, HD16, 2, dtype=f) / f(HD16))),
            ("64", HD64, f(1.0) / f(150000.0) ** (np.arange(HD64 // 2, dtype=f) / f(HD64 // 2)))):
        ang = (np.arange(S, dtype=f)[:, None] * inv.astype(f)[None, :]).astype(f)
        tiles = lambda a: a.reshape(TB, P, hd).transpose(1, 0, 2)
        put("cos" + name, tiles(np.concatenate([np.cos(ang), np.cos(ang)], 1)))
        put("sin" + name, tiles(np.concatenate([-np.sin(ang), np.sin(ang)], 1)))
    return c


def kernel(**inputs):
    import numpy as _np
    import concourse.bacc as _bacc
    from concourse import mybir as _mybir
    from concourse.bass_utils import run_bass_kernel_spmd as _run

    nc = _bacc.Bacc("TRN2", target_bir_lowering=False, num_devices=1)
    arrays, args = {}, []
    for name in _INS + ["consts"]:
        a = _np.ascontiguousarray(shape_constants(_np) if name == "consts" else inputs[name])
        arrays[f"in_{name}_dram"] = a
        args.append(nc.dram_tensor(f"in_{name}_dram", a.shape, _mybir.dt.from_np(a.dtype), kind="ExternalInput").ap())
    for i, (shape, dtype) in enumerate(_OUTS):
        dt = _mybir.dt.from_np(_np.dtype(dtype))
        args.append(nc.dram_tensor(f"out_{i}_dram", shape, dt, kind="ExternalOutput").ap())
    two_layers(nc, *args)
    r = _run(nc, [arrays], core_ids=[0])
    return r.results[0]["out_0_dram"]
```

```python
from contextlib import ExitStack

import concourse.bass as bass
from concourse import mybir

ALU = mybir.AluOpType
ACT = mybir.ActivationFunctionType
AX = mybir.AxisListType.X
F32 = mybir.dt.float32
F32R = mybir.dt.float32r
BF16 = mybir.dt.bfloat16

P = 128
D = 256
DC = D // P
B, S = 4, 512
TB = S // P
NT = B * TB
INTER = 1024
IC = INTER // P
H16, HD16 = 16, 16
KV16 = 4
G64, R64, HD64 = 8, 4, 64
E, TOPK, EH = 16, 4, 256
QKV = 384

CONST_COLS = {}
_at = 0
for _name, _n in (("ident", P), ("lag", P), ("ge", P), ("causal", P), ("block", P), ("ramp", P), ("left", 1),
                  ("parity", 2), ("cos16", TB * HD16), ("sin16", TB * HD16), ("cos64", TB * HD64),
                  ("sin64", TB * HD64)):
    CONST_COLS[_name] = (_at, _at + _n)
    _at += _n
NCONST = _at


class Region:

    def __init__(self, tensor):
        self.tensor, self.at = tensor, 0

    def reuse(self):
        self.at = 0

    def take(self, *shape):
        n = 1
        for s in shape:
            n *= s
        v = self.tensor[:, self.at:self.at + n]
        self.at += n
        assert self.at <= self.tensor.shape[1], (self.at, self.tensor.shape)
        dims = "abc"[:len(shape)]
        if len(shape) == 1:
            return v
        return v.rearrange(f"p ({' '.join(dims)}) -> p {' '.join(dims)}", **dict(zip(dims, shape)))


class Count:

    def __init__(self, sem, per_round=0, start=0):
        self.sem, self.per_round, self.n, self.start = sem, per_round, 0, start

    def inc(self, ins):
        ins.then_inc(self.sem, 1)
        self.n += 1

    def wait(self, eng, rnd=0):
        eng.wait_ge(self.sem, rnd * self.per_round + self.n + self.start)


def two_layers(nc, x_in, slope, W_qkvu, W_out0, SU_ug, SU_dp, Wscale_ug, Wscale_dp, W_up, W_gate, W_down,
               Wq1, Wk1, Wv1, Wo1, ln_w, ff_ln_w, wq, wk, wv, wo, wg, w1, w3, w2, consts, out):
    ctx = ExitStack()
    with ctx:
        def sb(name, shape, dt=F32):
            return ctx.enter_context(nc.sbuf_tensor(name, shape, dt))

        def sem(name):
            return ctx.enter_context(nc.semaphore(name))

        bank = [ctx.enter_context(nc.psum_tensor(f"bank{i}", [P, 512], F32)) for i in range(8)]

        x = sb("x", [P, NT, D])
        con = sb("con", [P, NCONST])

        def const(name):
            a, b = CONST_COLS[name]
            return con[:, a:b]

        ident = const("ident")
        wugT = sb("wugT", [P, DC, 2 * INTER])
        wdT = sb("wdT", [P, IC, D])
        wqkv1T = sb("wqkv1T", [P, DC, QKV])
        late = Region(sb("late", [P, DC * G64 * QKV + 2 * G64 * D]))
        wgrp = late.take(DC, G64, QKV)
        wo_sb = late.take(2 * G64, D)
        late.reuse()
        wg_sb = sb("wg_sb", [P, DC, E])
        su_ug = sb("su_ug", [P, DC])
        su_dp = sb("su_dp", [P, IC])
        ws_ug = sb("ws_ug", [P, 2 * IC])
        ws_dp = sb("ws_dp", [P, DC])
        lnw = sb("lnw", [P, DC])
        fflnw = sb("fflnw", [P, DC])

        NATB = 15
        wnat = late.take(NATB, D)
        causal = sb("causal", [P, P], BF16)
        ident_h = sb("ident_h", [P, P], BF16)
        ident_r = sb("ident_r", [P, P], F32R)
        room = sb("room", [P, NT])
        gcol = sb("gcol", [P, 2, NT])
        wo1p = sb("wo1p", [P, 4, D])

        st = sb("st", [P, NT, 6])
        mv = sb("mv", [P, NT, 2])
        var = sb("var", [P, NT])
        std = sb("std", [P, NT])
        rstd = sb("rstd", [P, NT])
        xn = sb("xn", [P, NT, D])
        hn = wugT[:].rearrange("p c (t d) -> p (c t) d", d=D)
        xnT = sb("xnT", [P, DC, S])

        ld_x = [sem(f"ld_x{b}") for b in range(B)]
        out_done = sem("out_done")
        ld_c, ld_w, ld_ug, ld_s, ld_l1 = (sem(n) for n in ("ld_c", "ld_w", "ld_ug", "ld_s", "ld_l1"))
        v_chain = sem("v_chain")
        ln_var, ln_std = sem("ln_var"), sem("ln_std")
        xn_all = sem("xn_all")
        wt_ps = sem("wt_ps")
        wt_sb = [sem("wt_sb_dve"), sem("wt_sb_act")]
        wo_spread = sem("wo_spread")
        slopes = sem("slopes")
        x_sum = sem("x_sum")
        fw_chain, fw_done = sem("fw_chain"), sem("fw_done")
        stored = sem("stored")

        mid = CONST_COLS.get

        first = ctx.enter_context(ExitStack())
        slope_b, nslope_b, slope_p, nslope_p = (first.enter_context(nc.sbuf_tensor(n, [P, cols], F32)) for n, cols in (
            ("slope_b", H16), ("nslope_b", H16), ("slope_p", DC), ("nslope_p", DC)))
        wqkvuT = first.enter_context(nc.sbuf_tensor("wqkvuT", [P, DC, 4 * D], F32))
        wout0T = first.enter_context(nc.sbuf_tensor("wout0T", [P, DC, D], F32))
        xn_st = first.enter_context(nc.sbuf_tensor("xn_st", [P, TB, D], F32))
        early = Region(first.enter_context(nc.sbuf_tensor("early", [P, 32 * D + 10368], F32)))
        wugd = early.take(24, D)
        pong = early.take(8, D)
        DT = late.take(H16, P)
        QD = early.take(DC, P)
        KD = early.take(H16)
        BD = early.take(DC)
        qT = early.take(DC, S)
        qdT = early.take(DC, S)
        kT = early.take(DC, S)
        kTm = early.take(2, DC, S)
        ks = early.take(2, D)
        kd = early.take(TB, D)
        v0 = early.take(TB, D)
        u0 = early.take(TB, D)
        PT0 = late.take(2, H16, P)
        kvs = early.take(DC, P)
        kvt = ks[:, 1, :].rearrange("p (c e) -> p c e", c=DC)
        ou = early.take(TB, D)
        osq = ks[:, 0, :]
        ouT = kT
        ss = early.take(NT)
        y0 = xn

        def head_of(slot):
            g, r = slot // 4, slot % 4
            return 8 * (r // 2) + 2 * g + r % 2

        dec_exp = sem("dec_exp")
        l0 = {n: sem("l0_" + n) for n in ("stage", "xT_ps", "xT_sb", "qk_ps", "q_sb", "kv_ps", "k_sb", "v_sb", "u_ps",
                                          "u_sb", "kTm", "kd", "s_ps", "pt", "o_ps", "st_ps", "st", "ou", "sq",
                                          "ouT_ps", "ouT_sb", "y_ps", "y_sb", "chain", "qd")}
        rms_in, rms_std = sem("rms_in"), sem("rms_std")

        early.reuse()
        early.take(32, D)
        gsil = early.take(2, S)
        aT = early.take(IC, S)
        f0 = {n: sem("f0_" + n) for n in ("stage", "xT_ps", "xT_sb", "up", "silu", "glu", "y_ps", "y")}

        first.close()

        def operands(name, n):
            return second.enter_context(nc.sbuf_tensor(name, [P, n], F32R))[:]

        cols = lambda name: slice(*CONST_COLS[name])
        negmax, rowsum, rinv = con[:, cols("lag")][:, 0:64], con[:, cols("lag")][:, 64:128], con[:, cols("ge")][:, 0:64]
        v_next = con[:, CONST_COLS["block"][0]:CONST_COLS["ramp"][1]]
        v_next = v_next.rearrange("p (t g d) -> p t g d", t=TB, g=KV16)
        more_probs = wdT[:].rearrange("p k d -> p (k d)").rearrange("p (u n) -> p u n", n=S)
        most_probs = wugT[:].rearrange("p c n -> p (c n)").rearrange("p (u n) -> p u n", n=S)

        def shared_buffers(n_turned):
            return region.take(n_turned, S), region.take(S), region.take(2, 320), region.take(2, 320), region.take(4, S)

        second = ctx.enter_context(ExitStack())
        narrow_q = operands("narrow_q", H16 * S).rearrange("p (h n) -> p h n", h=H16)
        narrow_k = operands("narrow_k", 2 * KV16 * S).rearrange("p (h n) -> p h n", h=2 * KV16)
        region = Region(second.enter_context(nc.sbuf_tensor("attn1", [P, 4 * S + 512 + 1280 + 4 * S + 512], F32)))
        narrow_bufs = shared_buffers(4)
        narrow_x = operands("narrow_x", 2 * (H16 + KV16) * P).rearrange("p (u n) -> p u n", u=2)
        narrow_v = region.take(TB, KV16, 32)
        narrow_xT = wo_sb.rearrange("p k d -> p (k d)").rearrange("p (c n) -> p c n", c=DC)

        second.close()
        second = ctx.enter_context(ExitStack())
        wide_q = operands("wide_q", 2 * R64 * S).rearrange("p (u h n) -> p u h n", u=2, h=R64)
        wide_k = operands("wide_k", 4 * S).rearrange("p (u h n) -> p u h n", u=2, h=2)
        region = Region(second.enter_context(nc.sbuf_tensor("attn2", [P, 5 * S + 512 + 1280 + 4 * S + 512 + DC * B * S], F32)))
        wide_bufs = shared_buffers(5)
        wide_x = operands("wide_x", 2 * (R64 + 2) * P).rearrange("p (u n) -> p u n", u=2)
        wide_v = region.take(2, TB, HD64)
        wide_xT = region.take(DC, B * S)

        class Attention:

            names = ("xT_ps", "xT_dve", "xT_act", "stage", "qkv_ps", "rope", "yb", "sum", "hi", "qk", "m_ps", "m_sb", "s_ps",
                     "max", "exp", "inv", "norm", "t_ps", "pt_dve", "pt_act", "v", "pv", "o_sb", "y_ps")

            def __init__(self, name, quads, hd, causal, bufs, n_turned, pieces, lag, behind, rest, prepare, late):
                self.behind = behind
                self.rest = rest
                self.lag = lag
                self.quads, self.hd, self.causal, self.n_turned, self.pieces = quads, hd, causal, n_turned, pieces
                self.probsT, self.onT, self.t1, self.t2, self.probs = bufs
                self.onT = self.onT.rearrange("p (u n) -> p u n", u=2 if causal else 1)
                self.prepare, self.late = prepare, late
                self.units = 4 * len(quads)
                self.per_row = len(quads) // TB
                self.steps = [(q, k) for q, (r, _g) in enumerate(quads) for k in range(self.keys(r))]
                self.sem = {n: sem(f"{name}_{n}") for n in self.names}
                self.turns = TB * pieces
                rounds = self.stream(4)
                assert rounds[1] == rounds[2] and len(rounds) == 5
                self.windows = {"first": [op for op in rounds[0] if (op[0], op[2]) not in sum(late.values(), [])],
                                "steady": rounds[2], "last": [op for op in rounds[3] if op[1] <= 0], "drain": rounds[4]}
                uses = lambda w: sum(op[0] in ("qkv", "project") for op in self.windows[w])
                self.y_uses = {"first": TB, "steady": TB + uses("first") - uses("steady"), "per_round": uses("steady")}

            def keys(self, row):
                return row + 1 if self.causal else TB

            def row_of(self, unit):
                return self.quads[unit // 4][0]

            def last_step(self, quad):
                return max(n for n, (q, _k) in enumerate(self.steps) if q == quad)

            def prob(self, unit):
                slot = unit % RING
                return most_probs[:, slot, :] if slot < 8 else more_probs[:, slot - 8, :] if slot < 12 else self.probs[:, slot - 12, :]

            def sbank(self, unit):
                return SBANK[1 if unit == self.units - 1 else unit % 3]

            def units_in_use(self, unit):
                return 1 if unit in (1, self.units - 1) else 2

            def y_before(self, window, it):
                return TB if window == "first" else it * self.y_uses["per_round"] + self.y_uses["steady"]

            def stream(self, n_rounds):
                out, turned, done, due, slot, total = [], 0, 0, [], 0, n_rounds * len(self.steps)

                def add(kind, rnd, a):
                    out[-1].append((kind, rnd - min(slot // self.units, n_rounds), a))

                def values():
                    nonlocal done
                    rnd, n = divmod(done, len(self.steps))
                    if n == 0 and not self.causal:
                        add("fresh_v", rnd, 0)
                    add("values", rnd, n)
                    q = self.steps[n][0]
                    if n == self.last_step(q) and (q + 1) % self.per_row == 0:
                        due.append((slot + self.rest, rnd, q // self.per_row))
                    done += 1

                while done < total or due:
                    rnd, u = divmod(slot, self.units)
                    if u == 0 and rnd <= n_rounds:
                        out.append([])
                    if rnd < n_rounds:
                        add("scores", rnd, u)
                        for kind, a in self.late.get(u, []):
                            add(kind, rnd, a)
                        for kind, a in self.prepare.get(u, []):
                            add(kind, rnd + 1, a)
                    while due and due[0][0] <= slot:
                        add("project", *due.pop(0)[1:])
                    if turned < total:
                        rnd, n = divmod(turned, len(self.steps))
                        ready = rnd * self.units + 4 * self.steps[n][0] + 3 + self.lag <= slot
                    if turned < total and ready:
                        add("turn", rnd, n)
                        turned += 1
                        if turned - done > 2:
                            values()
                    elif done < turned:
                        values()
                    slot += 1
                return out

        RING = 16
        NARROW_NEXT = {2: [("stage", 0)]}
        for t, (qkv_at, split_at, turn_at) in enumerate(((12, 16, 20), (28, 32, 35), (42, 46, 48), (50, 59, 62))):
            ops = [(qkv_at, ("qkv", t)), (split_at, ("split", t))]
            for i in range(5 if t < TB - 1 else 1):
                ops.append((turn_at + 3 * i, ("turn_qk", 5 * t + i)))
            for at_slot, op in ops:
                NARROW_NEXT.setdefault(at_slot, []).append(op)
        NARROW_LATE = {3 * i: [("turn_qk", 15 + i)] for i in range(1, 5)}
        WIDE_NEXT = {0: [("stage", 0)], 4: [("qkv", 0)], 6: [("split", 0), ("qkv", 1)], 7: [("turn_qk", 0)],
                     8: [("turn_qk", 1), ("split", 1), ("qkv", 2)], 9: [("turn_qk", 2)],
                     10: [("turn_qk", 3), ("split", 2), ("qkv", 3)], 11: [("turn_qk", 4)], 12: [("turn_qk", 5), ("split", 3)],
                     13: [("turn_qk", 6)], 14: [("turn_qk", 7)]}

        def prologue(pieces):
            ops = [("stage", 0, 0)]
            for t in range(TB + 1):
                if t < TB:
                    ops.append(("qkv", 0, t))
                if t >= 1:
                    ops.append(("split", 0, t - 1))
                    ops += [("turn_qk", 0, pieces * (t - 1) + i) for i in range(pieces)]
            return ops

        def reached(n):
            return not isinstance(n, int) or n > 0

        a1 = Attention("a1", [(r, g) for r in range(TB) for g in range(KV16)], HD16, False, narrow_bufs, 4, 5, 4, 2, 9, NARROW_NEXT,
                       NARROW_LATE)
        a2 = Attention("a2", [(r, 0) for r in reversed(range(TB))], HD64, True, wide_bufs, 5, 2, 4, 2, 5, WIDE_NEXT, {})
        SBANK, PTBANK, OBANK, MBANK, YBANK = (0, 1, 2), (3, 4), 5, 6, 7
        ROUNDS = B * G64
        assert B & (B - 1) == 0 and G64 & (G64 - 1) == 0

        def sequence_of(n):
            return (n >> (G64.bit_length() - 1)) & (B - 1)

        def group_of(n):
            return n & (G64 - 1)

        second.close()
        late.reuse()
        hT5 = late.take(DC, B * S)
        raw = late.take(2, 3 * DC, D)

        h_hi, h_lo = (sb(n, [P, DC, B * S], F32R) for n in ("h_hi", "h_lo"))
        w_hi, w_lo = (sb(n, [P, 2, 3 * DC, D], F32R) for n in ("w_hi", "w_lo"))
        a_hi, a_lo = (sb(n, [P, 2, DC, S], F32R) for n in ("a_hi", "a_lo"))
        early = Region(sb("experts", [P, 4 * S + 6 * NT * E + 8 * NT]))
        gs5 = early.take(2, S)
        glu = early.take(2, S)
        logits = early.take(NT, E)
        gate = early.take(NT, E)
        above = early.take(NT, E)
        ties = early.take(NT, E)
        run_a = early.take(NT, E)
        run_b = early.take(NT, E)
        best = early.take(NT, 8)
        m5 = {n: sem("m5_" + n) for n in ("hT_ps", "hT_sb", "lg_ps", "exp", "shift", "silu", "glu", "up_ps", "y_ps", "acc",
                                          "gcol", "h_hi", "h_lo", "w_hi", "w_lo", "a_hi", "a_lo")}
        ld_e = [sem("ld_e0"), sem("ld_e1")]

        block = ctx.enter_context(nc.Block())

        def parts(at, t):
            h, q, k = t % 2, at.t1[:, t % 2, 0:D], at.t1[:, t % 2, D:320]
            if at is a1:
                qx = narrow_x[:, h, 0:H16 * P].rearrange("p (h z) -> p h z", z=P)
                kx = narrow_x[:, h, H16 * P:].rearrange("p (h f w d) -> p h f w d", h=KV16, w=2, d=HD16)
                qd = lambda w: qx[:, :, 32 * w:32 * w + 32].rearrange("p h (f d) -> p h f d", d=HD16)
                kd_ = lambda w: kx[:, :, :, w, :]
                wide = lambda a, n, f: a.rearrange("p (h d) -> p h d", h=n).unsqueeze(2).to_broadcast([P, n, f, HD16])
                return ((qd, qd(0), wide(q, H16, 2)), (kd_, kd_(0), wide(k, KV16, 4)))
            qx = wide_x[:, h, 0:R64 * P].rearrange("p (h w d) -> p h w d", h=R64, w=2)
            kx = wide_x[:, h, R64 * P:].rearrange("p (w f d) -> p w f d", w=2, f=2)
            return ((lambda w: qx[:, :, w, :], qx[:, :, 0, :], q.rearrange("p (h d) -> p h d", h=R64)),
                    (lambda w: kx[:, w, :, :], kx[:, 0, :, :], k.unsqueeze(1).to_broadcast([P, 2, HD64])))

        def start_turns():
            for c in range(DC):
                for blocks, dst in ((range(0, 4), wqkvuT[:, c, 0:512]), (range(4, 8), wqkvuT[:, c, 512:1024]),
                                    (range(8, 10), wout0T[:, c, :]), (range(10, 13), wqkv1T[:, c, :])):
                    yield wnat, c, list(blocks), dst
            for i in range(4):
                yield wo_nat, 0, [i, 4 + i], wo1p[:, i, :]

        wo_nat = xn_st[:].rearrange("p t d -> p (t d)").rearrange("p (n q) -> p n q", q=P)
        START = list(start_turns())
        FFN = [(wugd, c, list(range(4 * g, 4 * g + 4)), wugT[:, c, 512 * g:512 * g + 512], su_ug[:, c:c + 1])
               for g in range(4) for c in range(DC)]
        FFN += [(wugd, k % 2, [16 + k // 2, 20 + k // 2], wdT[:, k, :], su_dp[:, k:k + 1]) for k in range(IC)]

        @block.sync
        def _(sync):
            sync.dma_start(con[:], consts).then_inc(ld_c, 16)
            sync.dma_start(wnat[:, 0:8, :], W_qkvu.rearrange("(n p) d -> p n d", p=P)).then_inc(ld_w, 16)
            xv = x_in.rearrange("b (t p) d -> p (b t) d", p=P)
            for b in range(B):
                sync.dma_start(x[:, TB * b:TB * b + TB, :], xv[:, TB * b:TB * b + TB, :]).then_inc(ld_x[b], 16)
            sync.dma_start(slope_b[:], slope.rearrange("h a b -> (a b h)").partition_broadcast(P)).then_inc(ld_s, 16)
            for h in range(H16):
                sync.dma_start(slope_p[HD16 * (h % 8):HD16 * (h % 8) + HD16, h // 8:h // 8 + 1],
                               slope[h, :, 0].partition_broadcast(HD16)).then_inc(ld_s, 16)
            sync.dma_start(wnat[:, 8:10, :], W_out0.rearrange("(n p) d -> p n d", p=P)).then_inc(ld_w, 16)
            sync.dma_start(wnat[:, 10:12, :], Wq1.rearrange("(n p) d -> p n d", p=P)).then_inc(ld_w, 16)
            sync.dma_start(wnat[0:64, 12, :], Wk1).then_inc(ld_w, 16)
            sync.dma_start(wnat[64:128, 12, :], Wv1).then_inc(ld_w, 16)
            sync.dma_start(wnat[:, 13:15, :], Wo1.rearrange("(n p) d -> p n d", p=P)).then_inc(ld_w, 16)
            sync.dma_start(wugd[:, 0:8, :], W_up.rearrange("(n p) d -> p n d", p=P)).then_inc(ld_ug, 16)
            sync.dma_start(wugd[:, 8:16, :], W_gate.rearrange("(n p) d -> p n d", p=P)).then_inc(ld_ug, 16)
            sync.dma_start(wugd[:, 16:24, :], W_down.rearrange("(r p) (m d) -> p r m d", p=P, d=D)).then_inc(ld_ug, 16)
            sync.dma_start(ws_ug[:], Wscale_ug.rearrange("(n p) -> p n", p=P), allow_slow_non_contiguous=True).then_inc(ld_ug, 16)
            sync.dma_start(ws_dp[:], Wscale_dp.rearrange("(n p) -> p n", p=P), allow_slow_non_contiguous=True).then_inc(ld_ug, 16)
            sync.dma_start(su_ug[:], SU_ug.rearrange("(n p) -> p n", p=P), allow_slow_non_contiguous=True).then_inc(ld_ug, 16)
            sync.dma_start(su_dp[:], SU_dp.rearrange("(n p) -> p n", p=P), allow_slow_non_contiguous=True).then_inc(ld_ug, 16)
            sync.dma_start(lnw[:], ln_w.rearrange("(n p) -> p n", p=P), allow_slow_non_contiguous=True).then_inc(ld_l1, 16)
            sync.dma_start(fflnw[:], ff_ln_w.rearrange("(n p) -> p n", p=P), allow_slow_non_contiguous=True).then_inc(ld_l1, 16)
            sync.dma_start(wg_sb[:], wg.rearrange("(c p) e -> p c e", p=P)).then_inc(ld_l1, 16)
            sync.wait_ge(rms_in, 1)
            for c in range(DC):
                rows = slice(P * c, P * c + P)
                sync.dma_start(wgrp[:, c, :, 0:256], wq[rows, :].rearrange("p (g n) -> p g n", g=G64)).then_inc(ld_l1, 16)
                sync.dma_start(wgrp[:, c, :, 256:320], wk[rows, :].rearrange("p (g n) -> p g n", g=G64)).then_inc(ld_l1, 16)
                sync.dma_start(wgrp[:, c, :, 320:384], wv[rows, :].rearrange("p (g n) -> p g n", g=G64)).then_inc(ld_l1, 16)
            sync.wait_ge(a1.sem["qkv_ps"], B * TB)
            sync.dma_start(wo_sb[:], wo.rearrange("(k p) d -> p k d", p=P)).then_inc(ld_l1, 16)

            def load_expert(e, half):
                w = lambda a: a[bass.ds(e, 1), :, :].rearrange("e (c p) h -> p (e c) h", p=P)
                for i, a in enumerate((w1, w3, w2)):
                    sync.dma_start(raw[:, half, DC * i:DC * i + DC, :], w(a)).then_inc(ld_e[half], 16)

            sync.wait_ge(ln_var, 6)
            load_expert(0, 0)
            load_expert(1, 1)
            with sync.Fori(1, E // 2) as pair:
                for half in range(2):
                    sync.wait_ge(m5["w_lo"], pair * 2 + half - 1)
                    load_expert(pair * 2 + half, half)
            sync.wait_ge(stored, 1)
            ov = out.rearrange("b (t p) d -> p (b t) d", p=P)
            sync.dma_start(ov, x[:]).then_inc(out_done, 16)
            sync.wait_ge(out_done, 16)

        @block.gpsimd
        def _(pool):
            chain = Count(fw_chain)
            pool.wait_ge(ld_ug, 16 * 7)

            def butterflies(a, b, n):
                h, src, dst = 1, a, b
                while h < n:
                    s4 = src.rearrange("p (g two h) -> p g two h", two=2, h=h)
                    d4 = dst.rearrange("p (g two h) -> p g two h", two=2, h=h)
                    chain.inc(nc.gpsimd.tensor_tensor(d4[:, :, 0, :], s4[:, :, 0, :], s4[:, :, 1, :], ALU.add))
                    chain.inc(nc.gpsimd.tensor_tensor(d4[:, :, 1, :], s4[:, :, 0, :], s4[:, :, 1, :], ALU.subtract))
                    chain.wait(pool)
                    src, dst, h = dst, src, 2 * h

            flat = lambda t: t.rearrange("p n d -> p (n d)")
            for blk, n in ((0, D), (8, D), (16, INTER)):
                butterflies(flat(wugd[:, blk:blk + 8, :]), flat(pong), n)
            for n in range(16):
                chain.inc(nc.gpsimd.tensor_scalar(wugd[:, n, :], wugd[:, n, :], ws_ug[:, n:n + 1], D ** -0.5,
                                                  ALU.mult, ALU.mult))
            for r in range(DC):
                rows = flat(wugd[:, 16 + 4 * r:20 + 4 * r, :])
                chain.inc(nc.gpsimd.tensor_scalar(rows, rows, ws_dp[:, r:r + 1], INTER ** -0.5, ALU.mult, ALU.mult))
            chain.wait(pool)
            nc.gpsimd.drain().then_inc(fw_done, 1)
            def pool_work(at, ops, it):

                def normalise(rnd, m):
                    pool.wait_ge(at.sem["inv"], rnd * at.units + m + 1)
                    n = P * at.keys(at.row_of(m))
                    p = at.prob(m)[:, 0:n]
                    nc.gpsimd.tensor_tensor(p, p, rinv[:, m:m + 1].to_broadcast([P, n]), ALU.mult).then_inc(at.sem["norm"], 1)

                for kind, d, a in ops:
                    n = it + d
                    if kind == "scores":
                        if a >= at.behind:
                            normalise(n, a - at.behind)
                        elif reached(n):
                            normalise(n - 1, at.units + a - at.behind)
                    elif kind == "qkv":
                        pool.wait_ge(at.sem["rope"], n * TB + a + 1)
                        nc.gpsimd.tensor_tensor(at.t1[:, a % 2, :], at.t1[:, a % 2, :], at.t2[:, a % 2, :],
                                                ALU.add).then_inc(at.sem["sum"], 1)
                if ops is at.windows["drain"]:
                    for m in range(at.units - at.behind, at.units):
                        normalise(it - 1, m)

            pool_work(a1, prologue(5), 0)
            pool_work(a1, a1.windows["first"], 0)
            with pool.Fori(1, B - 1) as b:
                pool_work(a1, a1.windows["steady"], b)
            pool_work(a1, a1.windows["last"], B - 1)
            pool_work(a1, a1.windows["drain"], B)
            pool_work(a2, prologue(2), 0)
            pool_work(a2, a2.windows["first"], 0)
            with pool.Fori(1, ROUNDS - 1) as rnd:
                pool_work(a2, a2.windows["steady"], rnd)
            pool_work(a2, a2.windows["last"], ROUNDS - 1)
            pool_work(a2, a2.windows["drain"], ROUNDS)
            def rest(dst, whole, high, signal):
                nc.gpsimd.tensor_tensor(dst, whole, high, ALU.subtract).then_inc(m5[signal], 1)

            def weights_rest(e, half):
                pool.wait_ge(m5["w_hi"], e + 1)
                rest(w_lo[:, half], raw[:, half], w_hi[:, half], "w_lo")

            weights_rest(0, 0)
            for b in range(B):
                for c in range(DC):
                    pool.wait_ge(m5["h_hi"], DC * b + c + 1)
                    cols = slice(S * b, S * b + S)
                    rest(h_lo[:, c, cols], hT5[:, c, cols], h_hi[:, c, cols], "h_lo")
            for t in range(NT):
                nc.gpsimd.tensor_tensor(x[:, t, :], x[:, t, :], xn[:, t, :], ALU.add).then_inc(x_sum, 1)
            pool.sem_inc(m5["a_lo"], 2)

            def pool_experts(pair, final):
                for i in range(2 * B):
                    for hc in range(2):
                        pool.wait_ge(m5["a_hi"], pair * 4 * B + 2 * i + hc + 1)
                        rest(a_lo[:, i % 2, hc, :], glu[:, hc, :], a_hi[:, i % 2, hc, :], "a_lo")
                    if i % B == 1 and not (final and i > B):
                        weights_rest(pair * 2 + i // B + 1, (i // B + 1) % 2)

            with pool.Fori(0, E // 2 - 1) as pair:
                pool_experts(pair, False)
            pool_experts(E // 2 - 1, True)

        vch = Count(v_chain)

        def dve_norm(v, phase, eps, src=x, dst=xn, rms=False):
            for t in range(NT):
                if phase == 0 and t % TB == 0:
                    v.wait_ge(ld_x[t // TB], 16)
                vch.inc(nc.vector.bn_stats(st[:, t, :], src[:, t, :]))
            vch.wait(v)
            for t in range(NT):
                vch.inc(nc.vector.bn_aggr(mv[:, t, :], st[:, t, :]))
            vch.wait(v)
            if rms:
                vch.inc(nc.vector.tensor_tensor(std[:], mv[:, :, 0], mv[:, :, 0], ALU.mult))
                vch.wait(v)
                vch.inc(nc.vector.tensor_tensor(var[:], mv[:, :, 1], std[:], ALU.add))
                vch.wait(v)
                nc.vector.tensor_scalar(var[:], var[:], eps, None, ALU.add).then_inc(ln_var, 1)
            else:
                nc.vector.tensor_scalar(var[:], mv[:, :, 1], eps, None, ALU.add).then_inc(ln_var, 1)
            v.wait_ge(ln_std, phase + 1)
            vch.inc(nc.vector.reciprocal(rstd[:], std[:]))
            vch.wait(v)
            for t in range(NT):
                if rms:
                    nc.vector.tensor_scalar(dst[:, t, :], src[:, t, :], rstd[:, t:t + 1], None, ALU.mult).then_inc(xn_all, 1)
                else:
                    nc.vector.tensor_scalar(dst[:, t, :], src[:, t, :], mv[:, t, 0:1], rstd[:, t:t + 1],
                                            ALU.subtract, ALU.mult).then_inc(xn_all, 1)
            v.wait_ge(xn_all, NT * (phase + 1))

        @block.vector
        def _(v):
            dve_norm(v, 0, 1e-5)
            v.wait_ge(ld_s, 16 * 17)
            v.wait_ge(ld_c, 16)
            nc.vector.tensor_scalar(nslope_b[:], slope_b[:], -1.0, None, ALU.mult).then_inc(slopes, 1)
            nc.vector.tensor_scalar(nslope_p[:], slope_p[:], -1.0, None, ALU.mult).then_inc(slopes, 1)
            v.wait_ge(ld_w, 16 * 6)
            vch.inc(nc.vector.memset(wo_nat, 0.0))
            vch.wait(v)
            for blk in range(DC):
                ins = nc.vector.tensor_copy(
                    wo_nat[:, 4 * blk:4 * blk + 4, :].rearrange("p i (g d) -> p i g d", d=32)[:, :, :, 0:HD16],
                    wnat[:, 13 + blk, :].rearrange("p (g i d) -> p i g d", g=KV16, d=HD16))
            ins.then_inc(wo_spread, 1)
            for n, (_src, c, blocks, dst) in enumerate(START):
                if n % 2 == 0:
                    v.wait_ge(wt_ps, n + 1)
                    nc.vector.tensor_copy(dst, bank[n % 8][:, 0:P * len(blocks)]).then_inc(wt_sb[0], 1)
            v.wait_ge(dec_exp, H16 + 2 * DC + 1)
            a, _b = mid("ge")
            vch.inc(nc.vector.tensor_tensor(DT, DT, con[:, None, a:_b].to_broadcast([P, H16, P]), ALU.mult))
            vch.wait(v)

            v.wait_ge(wt_ps, len(START))
            ch = Count(l0["chain"], 2)
            with v.Fori(0, B) as b:
                ch.n = 0
                v.wait_ge(l0["xT_ps"], b * DC + 1)
                nc.vector.tensor_copy(xn_st[:], xn[:, bass.ts(b, TB), :]).then_inc(l0["stage"], 1)
                v.wait_ge(l0["q_sb"], b * 4 + 2)
                nc.vector.tensor_tensor(qdT.rearrange("p c (t i) -> p c t i", t=TB),
                                        qT.rearrange("p c (t i) -> p c t i", t=TB),
                                        QD.unsqueeze(2).to_broadcast([P, DC, TB, P]), ALU.mult).then_inc(l0["qd"], 1)
                v.wait_ge(l0["q_sb"], b * 4 + 4)
                par = const("parity")
                for e in range(2):
                    nc.vector.tensor_scalar(kTm[:, e, :, :], kT, par[:, e:e + 1], None, ALU.mult).then_inc(l0["kTm"], 1)
                for t in range(TB):
                    v.wait_ge(l0["u_ps"], b * TB + t + 1)
                    nc.vector.tensor_copy(u0[:, t, :], bank[(7, 1)[t % 2]][:, 0:D]).then_inc(l0["u_sb"], 1)
                    v.wait_ge(l0["k_sb"], b * TB + t + 1)
                    nc.vector.tensor_tensor(kd[:, t, :].rearrange("p (h d) -> p h d", h=H16),
                                            ks[:, t % 2, :].rearrange("p (h d) -> p h d", h=H16),
                                            KD.unsqueeze(2).to_broadcast([P, H16, HD16]),
                                            ALU.mult).then_inc(l0["kd"], 1)

                def decay(t):
                    for g in range(4):
                        v.wait_ge(l0["s_ps"], b * 16 + 4 * t + g + 1)
                        if g == 0 and t >= 2:
                            v.wait_ge(l0["o_ps"], b * TB + t - 1)
                        nc.vector.tensor_tensor(PT0[:, t % 2, 4 * g:4 * g + 4, :],
                                                bank[g][:].rearrange("p (h i) -> p h i", h=4),
                                                DT[:, 4 * g:4 * g + 4, :], ALU.mult).then_inc(l0["pt"], 1)

                decay(0)
                for t in range(TB):
                    if t + 1 < TB:
                        decay(t + 1)
                    v.wait_ge(l0["o_ps"], b * TB + t + 1)
                    nc.vector.tensor_tensor(ou[:, t, :], bank[4 + t % 2][:, 0:D], u0[:, t, :],
                                            ALU.mult).then_inc(l0["ou"], 1)
                    if t < TB - 1:
                        v.wait_ge(l0["st_ps"], b * 3 + t + 1)
                        into = kvs if t == 0 else kvt
                        a, _b = mid("block")
                        kv_ins = nc.vector.tensor_tensor(into[:], bank[6][:, 0:D].rearrange("p (c e) -> p c e", c=DC),
                                                         con[:, None, a:_b].to_broadcast([P, DC, P]), ALU.mult)
                        if t == 0:
                            kv_ins.then_inc(l0["st"], 1)
                        else:
                            ch.inc(kv_ins)
                            ch.wait(v, b)
                            v.wait_ge(l0["st"], b * 5 + 2 * t - 1)
                            for c in range(DC):
                                nc.vector.scalar_tensor_tensor(kvs[:, c, :], kvs[:, c, :], BD[:, c:c + 1], kvt[:, c, :],
                                                               ALU.mult, ALU.add).then_inc(l0["st"], 1)
            l0_chain_check = ch.n
            assert l0_chain_check == 2

            v.wait_ge(l0["sq"], NT + 1)
            v.wait_ge(l0["y_sb"], 2 * B + 1)
            nc.vector.tensor_scalar(ss[:], ss[:], 1.0 / D, 1e-6, ALU.mult, ALU.add).then_inc(rms_in, 1)
            v.wait_ge(rms_std, 1)
            vch.inc(nc.vector.reciprocal(rstd[:], std[:]))
            vch.wait(v)
            for t in range(NT):
                vch.inc(nc.vector.scalar_tensor_tensor(x[:, t, :], y0[:, t, :], rstd[:, t:t + 1], x[:, t, :],
                                                       ALU.mult, ALU.add))
            vch.wait(v)
            for n, (_src, c, blocks, dst, sign) in enumerate(FFN):
                if n % 2 == 0:
                    v.wait_ge(wt_ps, len(START) + n + 1)
                    nc.vector.tensor_scalar(dst, bank[n % 8][:, 0:P * len(blocks)], sign, None, ALU.mult).then_inc(wt_sb[0], 1)
            dve_norm(v, 1, 1e-5)
            v.sem_inc(f0["y"], 1)
            with v.Fori(0, B) as b:
                v.wait_ge(f0["xT_ps"], b * DC + 1)
                nc.vector.tensor_copy(xn_st[:], xn[:, bass.ts(b, TB), :]).then_inc(f0["stage"], 1)
                for k in range(IC):
                    v.wait_ge(f0["silu"], b * IC + k + 1)
                    nc.vector.tensor_tensor(aT[:, k, :], bank[2 + 2 * (k % 2)][:], gsil[:, k % 2, :],
                                            ALU.mult).then_inc(f0["glu"], 1)
                for i in range(2):
                    v.wait_ge(f0["y_ps"], b * 2 + i + 1)
                    rows = x[:, bass.ds(b * TB + 2 * i, 2), :]
                    nc.vector.tensor_tensor(rows, rows, bank[6 + i][:].rearrange("p (t d) -> p t d", t=2),
                                            ALU.add).then_inc(f0["y"], 1)
            v.wait_ge(f0["y"], 2 * B + 1)
            def turned_x(at, all_xT, scale=None):
                for b in range(B):
                    v.wait_ge(at.sem["xT_ps"], b * DC + 1)
                    dst = all_xT[:, 0, S * b:S * b + S]
                    if scale is None:
                        ins = nc.vector.tensor_copy(dst, bank[b * DC][:])
                    else:
                        ins = nc.vector.tensor_scalar(dst, bank[b * DC][:], scale[:, 0:1], None, ALU.mult)
                    ins.then_inc(at.sem["xT_dve"], 1)

            def rope(at, n, t, v_dst):
                v.wait_ge(at.sem["qkv_ps"], n * TB + t + 1)
                hd, h = at.hd, t % 2
                src = bank[YBANK][:, 0:320].rearrange("p (h d) -> p h d", d=hd)
                tab = lambda name, lo, hi: con[:, None, mid(name)[0] + t * hd + lo:mid(name)[0] + t * hd + hi].to_broadcast(
                    [P, 320 // hd, hi - lo])
                u1, u2 = (a[:, h, :].rearrange("p (h d) -> p h d", d=hd) for a in (at.t1, at.t2))
                name, half = str(hd), hd // 2
                nc.vector.tensor_tensor(u1, src, tab("cos" + name, 0, hd), ALU.mult)
                nc.vector.tensor_tensor(u2[:, :, 0:half], src[:, :, half:hd], tab("sin" + name, 0, half), ALU.mult)
                nc.vector.tensor_tensor(u2[:, :, half:hd], src[:, :, 0:half], tab("sin" + name, half, hd),
                                        ALU.mult).then_inc(at.sem["rope"], 1)
                vp = bank[YBANK][:, 320:384]
                if at is a2 and t == 0 and reached(n - 1):
                    v.wait_ge(at.sem["pv"], (n - 1) * len(at.steps))
                nc.vector.tensor_copy(v_dst, vp.rearrange("p (g d) -> p g d", g=KV16) if at is a1 else vp).then_inc(at.sem["yb"], 1)

            def dve_work(at, ops, it, par, b, res):

                def invert(rnd, m):
                    v.wait_ge(at.sem["exp"], rnd * at.units + m + 1)
                    nc.vector.reciprocal(rinv[:, m:m + 1], rowsum[:, m:m + 1]).then_inc(at.sem["inv"], 1)

                if ops is at.windows["drain"]:
                    for m in range(at.units - at.behind, at.units):
                        invert(it - 1, m)
                for kind, d, a in ops:
                    n = it + d
                    n0 = n * len(at.steps)
                    if kind == "scores":
                        v.wait_ge(at.sem["s_ps"], n * at.units + a + 1)
                        nc.vector.tensor_reduce(negmax[:, a:a + 1],
                                                bank[at.sbank(a)][:, 0:P * at.keys(at.row_of(a))],
                                                AX, ALU.max, negate=True).then_inc(at.sem["max"], 1)
                        if a >= at.behind:
                            invert(n, a - at.behind)
                        elif reached(n):
                            invert(n - 1, at.units + a - at.behind)
                    elif kind == "turn" and a % 2 == 0:
                        v.wait_ge(at.sem["t_ps"], n0 + a + 1)
                        if reached(n0 + a + 1 - at.n_turned):
                            v.wait_ge(at.sem["pv"], n0 + a + 1 - at.n_turned)
                        nc.vector.tensor_copy(at.probsT[:, a % at.n_turned, :], bank[PTBANK[0]][:]).then_inc(at.sem["pt_dve"], 1)
                    elif kind == "fresh_v":
                        if reached(n0):
                            v.wait_ge(at.sem["pv"], n0)
                        nc.vector.tensor_copy(narrow_v[:, :, :, 0:HD16], v_next).then_inc(at.sem["v"], 1)
                    elif kind == "project":
                        r = at.quads[a * at.per_row][0]
                        v.wait_ge(at.sem["y_ps"], n * TB + a + 1)
                        rows = res[:, bass.ds(b(n) * TB + r, 1), :]
                        nc.vector.tensor_tensor(rows, rows, bank[YBANK][:, None, 0:D], ALU.add).then_inc(at.sem["yb"], 1)
                    elif kind == "qkv":
                        rope(at, n, a, v_next[:, a, :, :] if at is a1 else wide_v[:, (par + d) % 2, a, :])
                    elif kind == "split":
                        v.wait_ge(at.sem["hi"], n * TB + a + 1)
                        for dst, high, whole in parts(at, a):
                            ins = nc.vector.tensor_tensor(dst(1), whole, high, ALU.subtract)
                        ins.then_inc(at.sem["qk"], 1)

            def narrow(ops, it):
                dve_work(a1, ops, it, None, lambda n: n, x)

            def wide(ops, it, par):
                dve_work(a2, ops, it, par, sequence_of, xn)

            vch.inc(nc.vector.tensor_copy(causal[:], const("causal")))
            vch.inc(nc.vector.tensor_copy(ident_h[:], ident))
            vch.inc(nc.vector.tensor_copy(ident_r[:], ident))
            for half in range(2):
                vch.inc(nc.vector.tensor_scalar(narrow_x[:, half, :], con[:, 0:1].to_broadcast([P, (H16 + KV16) * P]), 0.0, None,
                                                ALU.mult))
            vch.inc(nc.vector.memset(narrow_v, 0.0))
            dve_norm(v, 2, 1e-5)
            turned_x(a1, narrow_xT)
            narrow(prologue(5), 0)
            narrow(a1.windows["first"], 0)
            with v.Fori(1, B - 1) as b:
                narrow(a1.windows["steady"], b)
            narrow(a1.windows["last"], B - 1)
            narrow(a1.windows["drain"], B)
            v.wait_ge(a1.sem["yb"], 2 * TB * B)
            dve_norm(v, 3, 1e-5)
            dve_norm(v, 4, 1e-5, xn, hn, rms=True)
            v.wait_ge(ld_l1, 16 * 10)
            turned_x(a2, wide_xT, lnw)
            wide(prologue(2), 0, 0)
            wide(a2.windows["first"], 0, 0)
            with v.Fori(0, ROUNDS // 2 - 1) as pair:
                for i in (1, 2):
                    wide(a2.windows["steady"], pair * 2 + i, i % 2)
            wide(a2.windows["last"], ROUNDS - 1, 1)
            wide(a2.windows["drain"], ROUNDS, 0)
            v.wait_ge(a2.sem["yb"], 2 * TB * ROUNDS)
            dve_norm(v, 5, 1e-5, xn, hn, rms=True)

            def step(ins):
                vch.inc(ins)
                vch.wait(v)

            v.wait_ge(m5["lg_ps"], 1)
            step(nc.vector.tensor_copy(logits, bank[4][:, 0:NT * E].rearrange("p (t e) -> p t e", e=E)))
            for t in range(NT):
                vch.inc(nc.vector.max(best[:, t, :], logits[:, t, :]))
            vch.wait(v)
            wide = lambda col: col.to_broadcast([P, NT, E])
            least = wide(best[:, :, TOPK - 1:TOPK])
            vch.inc(nc.vector.tensor_tensor(above, logits, least, ALU.is_gt))
            vch.inc(nc.vector.tensor_tensor(ties, logits, least, ALU.is_equal))
            step(nc.vector.tensor_tensor(gate, logits, wide(best[:, :, 0:1]), ALU.subtract))
            nc.vector.tensor_reduce(room[:], above, AX, ALU.add).then_inc(m5["shift"], 1)
            v.wait_ge(m5["shift"], 1)
            step(nc.vector.tensor_scalar(room[:], room[:], -1.0, float(TOPK), ALU.mult, ALU.add))
            src, dst = ties, run_a
            for sh in (1, 2, 4, 8):
                vch.inc(nc.vector.tensor_copy(dst[:, :, 0:sh], src[:, :, 0:sh]))
                step(nc.vector.tensor_tensor(dst[:, :, sh:E], src[:, :, sh:E], src[:, :, 0:E - sh], ALU.add))
                src, dst = dst, (run_b if dst is run_a else run_a)
            step(nc.vector.tensor_tensor(dst, src, wide(room[:].unsqueeze(2)), ALU.is_le))
            step(nc.vector.tensor_tensor(dst, dst, ties, ALU.mult))
            step(nc.vector.tensor_tensor(above, above, dst, ALU.add))
            v.wait_ge(m5["exp"], 1)
            step(nc.vector.tensor_tensor(gate, gate, above, ALU.mult))
            step(nc.vector.tensor_reduce(room[:], gate, AX, ALU.add))
            step(nc.vector.reciprocal(room[:], room[:]))
            step(nc.vector.tensor_tensor(gate, gate, wide(room[:].unsqueeze(2)), ALU.mult))

            v.wait_ge(x_sum, NT)
            v.sem_inc(m5["acc"], 17)
            with v.Fori(0, E // 2) as pair:
                for i in range(2 * B + 1):
                    if i < 2 * B:
                        for hc in range(2):
                            v.wait_ge(m5["silu"], pair * 4 * B + 2 * i + hc + 1)
                            v.wait_ge(m5["a_lo"], pair * 4 * B + 2 * i + hc + 1)
                            nc.vector.tensor_tensor(glu[:, hc, :], bank[2 * hc + 1][:], gs5[:, hc, :],
                                                    ALU.mult).then_inc(m5["glu"], 1)
                    i -= 1
                    if i >= 0:
                        par, b = i // B, i % B
                        if b == 0:
                            nc.vector.tensor_copy(gcol[:, par, :], gate[:, :, bass.ds(pair * 2 + par, 1)].rearrange(
                                "p t e -> p (t e)")).then_inc(m5["gcol"], 1)
                            v.wait_ge(m5["gcol"], pair * 2 + par + 1)
                        v.wait_ge(m5["acc"], pair * 8 * B + TB * i + 1)
                        for t in range(TB):
                            if t % 2 == 0:
                                v.wait_ge(m5["y_ps"], pair * 4 * B + 2 * i + t // 2 + 2)
                            n = TB * b + t
                            nc.vector.scalar_tensor_tensor(
                                x[:, n, :], bank[4 + 2 * (i % 2) + t // 2][:, D * (t % 2):D * (t % 2) + D],
                                gcol[:, par, n:n + 1], x[:, n, :], ALU.mult, ALU.add).then_inc(m5["acc"], 1)
            v.wait_ge(m5["acc"], 17 + NT * E)
            v.drain().then_inc(stored, 1)

        @block.scalar
        def _(act):
            act.wait_ge(ld_c, 16)
            act.wait_ge(ln_var, 1)
            nc.scalar.activation(std[:], var[:], ACT.Sqrt).then_inc(ln_std, 1)

            def start_weights(turns):
                for n in turns:
                    _src, _c, blocks, dst = START[n]
                    act.wait_ge(wt_ps, n + 1)
                    nc.scalar.activation(dst, bank[n % 8][:, 0:P * len(blocks)], ACT.Copy).then_inc(wt_sb[1], 1)

            start_weights(range(1, 9, 2))
            act.wait_ge(slopes, 2)
            for slot in range(H16):
                h = head_of(slot)
                nc.scalar.activation(DT[:, slot, :], const("lag"), ACT.Exp,
                                     scale=nslope_b[:, h:h + 1]).then_inc(dec_exp, 1)
            for c in range(DC):
                nc.scalar.activation(QD[:, c, :], const("ramp"), ACT.Exp, scale=nslope_p[:, c:c + 1]).then_inc(dec_exp, 1)
                nc.scalar.activation(BD[:, c:c + 1], nslope_p[:, c:c + 1], ACT.Exp, scale=float(P)).then_inc(dec_exp, 1)
            nc.scalar.activation(KD, nslope_b[:], ACT.Exp, scale=const("left")).then_inc(dec_exp, 1)
            start_weights(range(9, len(START), 2))

            def turn_evac(sems, b, scale=None):
                for c in range(DC):
                    act.wait_ge(sems["xT_ps"], b * DC + c + 2)
                    if scale is None:
                        ins = nc.scalar.activation(xnT[:, c, :], bank[c][:], ACT.Copy)
                    else:
                        ins = nc.scalar.activation(xnT[:, c, :], bank[c][:], ACT.Identity, scale=scale[:, c:c + 1])
                    ins.then_inc(sems["xT_sb"], 1)

            act.sem_inc(l0["y_sb"], 1)
            act.sem_inc(l0["sq"], 1)
            with act.Fori(0, B) as b:
                turn_evac(l0, b)
                for m in range(4):
                    act.wait_ge(l0["qk_ps"], b * 4 + m + 1)
                    nc.scalar.activation((qT, kT)[m // 2][:, m % 2, :], bank[2 + m][:], ACT.Silu).then_inc(l0["q_sb"], 1)
                for t in range(TB):
                    act.wait_ge(l0["kv_ps"], b * TB + t + 1)
                    if t >= 2:
                        act.wait_ge(l0["kd"], b * TB + t - 1)
                    kvb = bank[(6, 0)[t % 2]]
                    nc.scalar.activation(ks[:, t % 2, :], kvb[:, 0:D], ACT.Silu).then_inc(l0["k_sb"], 1)
                    nc.scalar.activation(v0[:, t, :], kvb[:, D:2 * D], ACT.Copy).then_inc(l0["v_sb"], 1)
                for t in range(TB):
                    act.wait_ge(l0["ou"], b * TB + t + 1)
                    act.wait_ge(l0["sq"], b * TB + t + 1)
                    nc.scalar.activation(osq, bank[4 + t % 2][:, 0:D], ACT.Square,
                                         accum_out=ss[:, bass.ds(b * TB + t, 1)]).then_inc(l0["sq"], 1)
                for c in range(DC):
                    act.wait_ge(l0["ouT_ps"], b * DC + c + 1)
                    nc.scalar.activation(ouT[:, c, :], bank[6 + c][:], ACT.Copy).then_inc(l0["ouT_sb"], 1)
                for i in range(2):
                    act.wait_ge(l0["y_ps"], b * 2 + i + 1)
                    nc.scalar.activation(y0[:, bass.ds(b * TB + 2 * i, 2), :],
                                         bank[i][:].rearrange("p (t d) -> p t d", t=2), ACT.Copy).then_inc(l0["y_sb"], 1)
            act.wait_ge(rms_in, 1)
            nc.scalar.activation(std[:], ss[:], ACT.Sqrt).then_inc(rms_std, 1)
            for n, (_src, c, blocks, dst, sign) in enumerate(FFN):
                if n % 2 == 1:
                    act.wait_ge(wt_ps, len(START) + n + 1)
                    nc.scalar.activation(dst, bank[n % 8][:, 0:P * len(blocks)], ACT.Identity, scale=sign).then_inc(wt_sb[1], 1)
            act.wait_ge(ln_var, 2)
            nc.scalar.activation(std[:], var[:], ACT.Sqrt).then_inc(ln_std, 1)
            with act.Fori(0, B) as b:
                turn_evac(f0, b)
                for k in range(IC):
                    act.wait_ge(f0["up"], b * IC + k + 1)
                    if k >= 2:
                        act.wait_ge(f0["glu"], b * IC + k - 1)
                    nc.scalar.activation(gsil[:, k % 2, :], bank[3 + 2 * (k % 2)][:], ACT.Silu).then_inc(f0["silu"], 1)
            def turned_x(at, all_xT, scale=None):
                for b in range(B):
                    act.wait_ge(at.sem["xT_ps"], b * DC + 2)
                    dst = all_xT[:, 1, S * b:S * b + S]
                    if scale is None:
                        ins = nc.scalar.activation(dst, bank[b * DC + 1][:], ACT.Copy)
                    else:
                        ins = nc.scalar.activation(dst, bank[b * DC + 1][:], ACT.Identity, scale=scale[:, 1:2])
                    ins.then_inc(at.sem["xT_act"], 1)

            def turned_qk(at, n, par, a):
                act.wait_ge(at.sem["m_ps"], n * at.turns + a + 1)
                t, i = a // at.pieces, a % at.pieces
                cols = slice(P * t, P * t + P)
                if at is a1:
                    dst = narrow_q[:, 4 * (i - 1):4 * i, cols] if i else narrow_k[:, bass.ds((n & 1) * KV16, KV16), cols]
                    heads, is_q = 4, i > 0
                else:
                    dst = wide_k[:, par, :, cols] if i else wide_q[:, par, :, cols]
                    heads, is_q = (2 if i else R64), i == 0
                src = bank[MBANK][:, 0:heads * P].rearrange("p (h n) -> p h n", h=heads)
                nc.scalar.activation(dst, src, ACT.Copy, scale=at.hd ** -0.5 if is_q else 1.0).then_inc(at.sem["m_sb"], 1)

            def act_work(at, ops, it, par, all_xT, b):

                def exponentials(rnd, m):
                    n = P * at.keys(at.row_of(m))
                    act.wait_ge(at.sem["max"], rnd * at.units + m + 1)
                    before = m // 4 - RING // 4
                    if before >= 0:
                        act.wait_ge(at.sem["t_ps"], rnd * len(at.steps) + at.last_step(before) + 1)
                    elif reached(rnd):
                        act.wait_ge(at.sem["t_ps"], (rnd - 1) * len(at.steps) + at.last_step(before + len(at.quads)) + 1)
                    nc.scalar.activation(at.prob(m)[:, 0:n], bank[at.sbank(m)][:, 0:n], ACT.Exp, bias=negmax[:, m:m + 1],
                                         accum_out=rowsum[:, m:m + 1]).then_inc(at.sem["exp"], 1)

                held = None
                for kind, d, a in ops:
                    n = it + d
                    n0 = n * len(at.steps)
                    if kind == "scores":
                        if held is not None:
                            exponentials(*held)
                        held = n, a
                    elif kind == "turn" and a % 2 == 1:
                        act.wait_ge(at.sem["t_ps"], n0 + a + 1)
                        if reached(n0 + a + 1 - at.n_turned):
                            act.wait_ge(at.sem["pv"], n0 + a + 1 - at.n_turned)
                        nc.scalar.activation(at.probsT[:, a % at.n_turned, :], bank[PTBANK[1]][:],
                                             ACT.Copy).then_inc(at.sem["pt_act"], 1)
                    if kind in ("turn", "values") and held is not None:
                        exponentials(*held)
                        held = None
                    if kind == "values":
                        q = at.steps[a][0]
                        if a == at.last_step(q) and (q + 1) % at.per_row == 0:
                            i, ring = q // at.per_row, at.onT.shape[1]
                            act.wait_ge(at.sem["pv"], n0 + a + 1)
                            if reached(n * TB + i + 1 - ring):
                                act.wait_ge(at.sem["y_ps"], n * TB + i + 1 - ring)
                            w = S // ring
                            nc.scalar.activation(at.onT[:, i % ring, :], bank[OBANK][:, 0:w], ACT.Copy).then_inc(at.sem["o_sb"], 1)
                    elif kind == "stage":
                        if reached(n):
                            act.wait_ge(at.sem["qkv_ps"], n * TB)
                        nc.scalar.activation(xnT[:], all_xT[:, :, bass.ds(b(n) * S, S)], ACT.Copy).then_inc(at.sem["stage"], 1)
                    elif kind == "split":
                        act.wait_ge(at.sem["sum"], n * TB + a + 1)
                        for dst, _high, whole in parts(at, a):
                            ins = nc.scalar.activation(dst(0), whole, ACT.Copy)
                        ins.then_inc(at.sem["hi"], 1)
                    elif kind == "turn_qk":
                        turned_qk(at, n, (par + d) % 2 if at is a2 else None, a)
                if held is not None:
                    exponentials(*held)

            def narrow(ops, it):
                act_work(a1, ops, it, None, narrow_xT, lambda n: n)

            def wide(ops, it, par):
                act_work(a2, ops, it, par, wide_xT, sequence_of)

            act.wait_ge(ln_var, 3)
            nc.scalar.activation(std[:], var[:], ACT.Sqrt).then_inc(ln_std, 1)
            turned_x(a1, narrow_xT)
            for half in ("xT_dve", "xT_act"):
                act.wait_ge(a1.sem[half], B)
            narrow(prologue(5), 0)
            narrow(a1.windows["first"], 0)
            with act.Fori(1, B - 1) as b:
                narrow(a1.windows["steady"], b)
            narrow(a1.windows["last"], B - 1)
            narrow(a1.windows["drain"], B)
            for n in (4, 5):
                act.wait_ge(ln_var, n)
                nc.scalar.activation(std[:], var[:], ACT.Sqrt).then_inc(ln_std, 1)
            act.wait_ge(ld_l1, 16 * 10)
            turned_x(a2, wide_xT, lnw)
            for half in ("xT_dve", "xT_act"):
                act.wait_ge(a2.sem[half], B)
            wide(prologue(2), 0, 0)
            wide(a2.windows["first"], 0, 0)
            with act.Fori(0, ROUNDS // 2 - 1) as pair:
                for i in (1, 2):
                    wide(a2.windows["steady"], pair * 2 + i, i % 2)
            wide(a2.windows["last"], ROUNDS - 1, 1)
            wide(a2.windows["drain"], ROUNDS, 0)
            act.wait_ge(ln_var, 6)
            nc.scalar.activation(std[:], var[:], ACT.Sqrt).then_inc(ln_std, 1)
            for b in range(B):
                for c in range(DC):
                    act.wait_ge(m5["hT_ps"], DC * b + c + 1)
                    nc.scalar.activation(hT5[:, c, S * b:S * b + S], bank[2 * (b % 2) + c][:], ACT.Identity,
                                         scale=fflnw[:, c:c + 1]).then_inc(m5["hT_sb"], 1)

            def weights_rounded(e, half):
                act.wait_ge(ld_e[half], (e >> 1) * 48 + 48)
                nc.scalar.activation(w_hi[:, half], raw[:, half], ACT.Copy).then_inc(m5["w_hi"], 1)

            weights_rounded(0, 0)
            for b in range(B):
                for c in range(DC):
                    act.wait_ge(m5["hT_sb"], DC * b + c + 1)
                    cols = slice(S * b, S * b + S)
                    nc.scalar.activation(h_hi[:, c, cols], hT5[:, c, cols], ACT.Copy).then_inc(m5["h_hi"], 1)
            act.wait_ge(m5["shift"], 1)
            nc.scalar.activation(gate, gate, ACT.Exp).then_inc(m5["exp"], 1)

            def act_experts(pair, final):
                for i in range(2 * B):
                    for hc in range(2):
                        act.wait_ge(m5["up_ps"], pair * 4 * B + 2 * i + hc + 1)
                        if i >= 1:
                            act.wait_ge(m5["glu"], pair * 4 * B + 2 * i + hc - 1)
                        nc.scalar.activation(gs5[:, hc, :], bank[2 * hc][:], ACT.Silu).then_inc(m5["silu"], 1)
                    for hc in range(2):
                        act.wait_ge(m5["glu"], pair * 4 * B + 2 * i + hc + 1)
                        nc.scalar.activation(a_hi[:, i % 2, hc, :], glu[:, hc, :], ACT.Copy).then_inc(m5["a_hi"], 1)
                    if i % B == 1 and not (final and i > B):
                        e = pair * 2 + i // B
                        act.wait_ge(m5["y_ps"], e * 2 * B + 1)
                        weights_rounded(e + 1, (i // B + 1) % 2)

            with act.Fori(0, E // 2 - 1) as pair:
                act_experts(pair, False)
            act_experts(E // 2 - 1, True)

        @block.tensor
        def _(pe):
            pe.wait_ge(ld_c, 16)

            def turn_weights(turns, n0):
                for n, (src, c, blocks, *_rest) in enumerate(turns):
                    if n >= 8:
                        pe.wait_ge(wt_sb[n % 2], (n0 + n - 8) // 2 + 1)
                    if src is wo_nat:
                        pe.wait_ge(wo_spread, 1)
                    for i, blk in enumerate(blocks):
                        ins = nc.tensor.transpose(bank[n % 8][:, P * i:P * i + P], src[:, blk, P * c:P * c + P], ident)
                    ins.then_inc(wt_ps, 1)

            pe.wait_ge(ld_w, 16 * 6)
            turn_weights(START, 0)
            for half in wt_sb:
                pe.wait_ge(half, len(START) // 2)

            def turn_x(sems, b):
                pe.wait_ge(sems["stage"], b + 1)
                for c in range(DC):
                    for t in range(TB):
                        ins = nc.tensor.transpose(bank[c][:, P * t:P * t + P], xn_st[:, t, P * c:P * c + P], ident)
                    ins.then_inc(sems["xT_ps"], 1)
                pe.wait_ge(sems["xT_sb"], b * DC + DC)

            pe.sem_inc(l0["xT_ps"], 1)
            with pe.Fori(0, B) as b:
                pe.wait_ge(l0["y_sb"], b * 2 + 1)
                turn_x(l0, b)
                for m in range(4):
                    for c in range(DC):
                        ins = nc.tensor.matmul(bank[2 + m][:], wqkvuT[:, c, P * m:P * m + P], xnT[:, c, :],
                                               start=(c == 0), stop=(c == DC - 1))
                    ins.then_inc(l0["qk_ps"], 1)
                for t in range(TB):
                    if t >= 2:
                        pe.wait_ge(l0["v_sb"], b * TB + t - 1)
                        pe.wait_ge(l0["u_sb"], b * TB + t - 1)
                    for c in range(DC):
                        ins = nc.tensor.matmul(bank[(6, 0)[t % 2]][:], xnT[:, c, P * t:P * t + P],
                                               wqkvuT[:, c, D:3 * D], start=(c == 0), stop=(c == DC - 1))
                    ins.then_inc(l0["kv_ps"], 1)
                    for c in range(DC):
                        ins = nc.tensor.matmul(bank[(7, 1)[t % 2]][:, 0:D], xnT[:, c, P * t:P * t + P],
                                               wqkvuT[:, c, 3 * D:4 * D], start=(c == 0), stop=(c == DC - 1))
                    ins.then_inc(l0["u_ps"], 1)

                def scores(t):
                    for r in range(4):
                        for g in range(4):
                            if r == 0 and t >= 1:
                                pe.wait_ge(l0["pt"], b * 16 + 4 * (t - 1) + g + 1)
                            c, odd = r // 2, r % 2
                            rows = slice(32 * g, 32 * g + 32)
                            ins = nc.tensor.matmul(bank[g][:, P * r:P * r + P], kTm[rows, odd, c, P * t:P * t + P],
                                                   qT[rows, c, P * t:P * t + P], start=True, stop=True)
                            if r == 3:
                                ins.then_inc(l0["s_ps"], 1)

                pe.wait_ge(l0["kTm"], b * 2 + 2)
                pe.wait_ge(l0["v_sb"], b * TB + TB)
                pe.wait_ge(l0["u_sb"], b * TB + TB)
                scores(0)
                for t in range(TB):
                    if t < TB - 1:
                        pe.wait_ge(l0["kd"], b * TB + t + 1)
                        if t >= 1:
                            pe.wait_ge(l0["st"], b * 5 + 2 * t - 1)
                        for c in range(DC):
                            ins = nc.tensor.matmul(bank[6][:, P * c:P * c + P], kd[:, t, P * c:P * c + P],
                                                   v0[:, t, P * c:P * c + P], start=True, stop=True)
                        ins.then_inc(l0["st_ps"], 1)
                    if t + 1 < TB:
                        scores(t + 1)
                    pe.wait_ge(l0["pt"], b * 16 + 4 * t + 4)
                    if t >= 2:
                        pe.wait_ge(l0["sq"], b * TB + t)
                    o = bank[4 + t % 2]
                    for slot in range(H16):
                        h = head_of(slot)
                        cols = slice(HD16 * h, HD16 * h + HD16)
                        ins = nc.tensor.matmul(o[:, cols], PT0[:, t % 2, slot, :], v0[:, t, cols], start=(slot == 0),
                                               stop=(t == 0 and slot == H16 - 1), skip_group_check=True)
                    if t >= 1:
                        pe.wait_ge(l0["st"], b * 5 + 2 * t - 1)
                        pe.wait_ge(l0["qd"], b + 1)
                        for c in range(DC):
                            ins = nc.tensor.matmul(o[:, P * c:P * c + P], qdT[:, c, P * t:P * t + P], kvs[:, c, :],
                                                   start=False, stop=(c == DC - 1), skip_group_check=True)
                    ins.then_inc(l0["o_ps"], 1)
                pe.wait_ge(l0["ou"], b * TB + TB)
                for c in range(DC):
                    for t in range(TB):
                        ins = nc.tensor.transpose(bank[6 + c][:, P * t:P * t + P], ou[:, t, P * c:P * c + P], ident)
                    ins.then_inc(l0["ouT_ps"], 1)
                pe.wait_ge(l0["ouT_sb"], b * DC + DC)
                for t in range(TB):
                    for c in range(DC):
                        ins = nc.tensor.matmul(bank[t // 2][:, D * (t % 2):D * (t % 2) + D], ouT[:, c, P * t:P * t + P],
                                               wout0T[:, c, :], start=(c == 0), stop=(c == DC - 1))
                    if t % 2:
                        ins.then_inc(l0["y_ps"], 1)
            pe.wait_ge(l0["y_sb"], 2 * B + 1)
            pe.wait_ge(l0["sq"], NT + 1)
            pe.wait_ge(fw_done, 1)
            turn_weights(FFN, len(START))
            for half in wt_sb:
                pe.wait_ge(half, (len(START) + len(FFN)) // 2)
            pe.sem_inc(f0["xT_ps"], 1)
            with pe.Fori(0, B) as b:
                turn_x(f0, b)
                for k in range(IC):
                    if k >= 2:
                        pe.wait_ge(f0["glu"], b * IC + k - 1)
                    for j in range(2):
                        for c in range(DC):
                            ins = nc.tensor.matmul(bank[2 + 2 * (k % 2) + j][:],
                                                   wugT[:, c, INTER * j + P * k:INTER * j + P * k + P], xnT[:, c, :],
                                                   start=(c == 0), stop=(c == DC - 1))
                    ins.then_inc(f0["up"], 1)
                pe.wait_ge(f0["glu"], b * IC + IC)
                pe.wait_ge(f0["y"], b * 2 + 1)
                for t in range(TB):
                    for k in range(IC):
                        ins = nc.tensor.matmul(bank[6 + t // 2][:, D * (t % 2):D * (t % 2) + D], aT[:, k, P * t:P * t + P],
                                               wdT[:, k, :], start=(k == 0), stop=(k == IC - 1))
                    if t % 2:
                        ins.then_inc(f0["y_ps"], 1)
            def turn_all_x(at, phase, rows):
                for b in range(B):
                    pe.wait_ge(xn_all, phase * NT + TB * b + TB)
                    for c in range(DC):
                        for t in range(TB):
                            ins = nc.tensor.transpose(bank[b * DC + c][:, P * t:P * t + P],
                                                      rows[:, TB * b + t, P * c:P * c + P], ident)
                        ins.then_inc(at.sem["xT_ps"], 1)
                for half in ("xT_dve", "xT_act"):
                    pe.wait_ge(at.sem[half], B)

            def pe_work(at, ops, it, par, n_y, w_qkv, w_out):
                for kind, d, a in ops:
                    n = it + d
                    n0 = n * len(at.steps)
                    side = (par + d) % 2 if at is a2 else None
                    if kind == "scores":
                        q, i, sbank = a // 4, a % 4, bank[at.sbank(a)]
                        r, g = at.quads[q]
                        keys = P * at.keys(r)
                        qcols = slice(P * r, P * r + P)
                        if i == 0 and (at is a1 or q == 0):
                            pe.wait_ge(at.sem["m_sb"], n * at.turns + (at.pieces * max(r + 1, TB - 1) + (r < TB - 1)
                                                                       if at is a1 else at.turns))
                        if reached(n * at.units + a - at.units_in_use(a)):
                            pe.wait_ge(at.sem["exp"], n * at.units + a - at.units_in_use(a))
                        if at is a1:
                            keys_at = narrow_k[:, bass.ds((n & 1) * KV16 + g, 1), :].rearrange("p a n -> p (a n)")
                            ins = nc.tensor.matmul(sbank[:], narrow_q[:, 4 * g + i, qcols], keys_at, start=True, stop=True)
                        else:
                            for w in range(2):
                                nc.tensor.matmul(sbank[:, 0:keys], wide_q[:, side, i, qcols], wide_k[:, side, w, 0:keys],
                                                 start=(w == 0), stop=False)
                            ins = nc.tensor.matmul(sbank[:, keys - P:keys], ident_h[:], causal[:], start=False, stop=True)
                        ins.then_inc(at.sem["s_ps"], 1)
                    elif kind == "turn":
                        q, k = at.steps[a]
                        pe.wait_ge(at.sem["norm"], n * at.units + 4 * q + 4)
                        evac = at.sem[("pt_dve", "pt_act")[a % 2]]
                        if reached(n * (len(at.steps) // 2) + a // 2):
                            pe.wait_ge(evac, n * (len(at.steps) // 2) + a // 2)
                        for i in range(4):
                            ins = nc.tensor.transpose(bank[PTBANK[a % 2]][:, P * i:P * i + P],
                                                      at.prob(4 * q + i)[:, P * k:P * k + P], ident)
                        ins.then_inc(at.sem["t_ps"], 1)
                    elif kind == "values":
                        q, k = at.steps[a]
                        r, g = at.quads[q]
                        if at is a1 and a == 0:
                            pe.wait_ge(at.sem["v"], n + 1)
                        pe.wait_ge(at.sem[("pt_dve", "pt_act")[a % 2]], n * (len(at.steps) // 2) + a // 2 + 1)
                        if q % at.per_row == 0 and k == 0 and reached(n * TB + q // at.per_row):
                            pe.wait_ge(at.sem["o_sb"], n * TB + q // at.per_row)
                        flags = dict(start=(k == 0), stop=(k == at.keys(r) - 1))
                        pT = at.probsT[:, a % at.n_turned, :]
                        if at is a1:
                            ins = nc.tensor.matmul(bank[OBANK][32 * g:32 * g + 32, :], narrow_v[:, k, g, :], pT, **flags)
                        else:
                            for e in range(2):
                                ins = nc.tensor.matmul(bank[OBANK][HD64 * e:HD64 * e + HD64, 0:D], wide_v[:, side, k, :],
                                                       pT.rearrange("p (c e n) -> p e c n", e=2, n=P)[:, e], **flags)
                        ins.then_inc(at.sem["pv"], 1)
                    elif kind == "project":
                        pe.wait_ge(at.sem["o_sb"], n * TB + a + 1)
                        pe.wait_ge(at.sem["yb"], n_y)
                        ring = at.onT.shape[1]
                        chunks = S // ring // P
                        for c in range(chunks):
                            ins = nc.tensor.matmul(bank[YBANK][:, 0:D], at.onT[:, a % ring, P * c:P * c + P], w_out(n, c),
                                                   start=(c == 0), stop=(c == chunks - 1))
                        ins.then_inc(at.sem["y_ps"], 1)
                        n_y = n_y + 1
                    elif kind == "qkv":
                        if a == 0:
                            pe.wait_ge(at.sem["stage"], n + 1)
                        if reached(n_y):
                            pe.wait_ge(at.sem["yb"], n_y)
                        for c in range(DC):
                            ins = nc.tensor.matmul(bank[YBANK][:, 0:QKV], xnT[:, c, P * a:P * a + P], w_qkv(n, c),
                                                   start=(c == 0), stop=(c == DC - 1))
                        ins.then_inc(at.sem["qkv_ps"], 1)
                        n_y = n_y + 1
                    elif kind == "turn_qk":
                        t, i = a // at.pieces, a % at.pieces
                        if i == 0:
                            pe.wait_ge(at.sem["qk"], n * TB + t + 1)
                        if reached(n * at.turns + a):
                            pe.wait_ge(at.sem["m_sb"], n * at.turns + a)
                        if at is a1:
                            src, z, heads = narrow_x, P * (4 * (i - 1) if i else H16), 4
                        else:
                            src, z, heads = wide_x, P * (R64 if i else 0), (2 if i else R64)
                        for h in range(heads):
                            ins = nc.tensor.transpose(bank[MBANK][:, P * h:P * h + P].bitcast(F32R),
                                                      src[:, t % 2, z + P * h:z + P * h + P], ident_r[:])
                        ins.then_inc(at.sem["m_ps"], 1)

            def narrow(window, it, n_y=None):
                ops = prologue(5) if window == "prologue" else a1.windows[window]
                pe_work(a1, ops, it, None, a1.y_before(window, it) if n_y is None else n_y,
                        lambda n, c: wqkv1T[:, c, :], lambda n, c: wo1p[:, c, :])

            def wide(window, it, par, n_y=None):
                ops = prologue(2) if window == "prologue" else a2.windows[window]
                flat = lambda a: a.rearrange("p a n -> p (a n)")
                pe_work(a2, ops, it, par, a2.y_before(window, it) if n_y is None else n_y,
                        lambda n, c: flat(wgrp[:, c, bass.ds(group_of(n), 1), :]),
                        lambda n, c: flat(wo_sb[:, bass.ds(group_of(n) * 2 + c, 1), :]))

            pe.wait_ge(f0["y"], 2 * B + 1)
            turn_all_x(a1, 2, xn)
            narrow("prologue", 0, 0)
            narrow("first", 0)
            with pe.Fori(1, B - 1) as b:
                narrow("steady", b)
            narrow("last", B - 1)
            narrow("drain", B, 2 * TB * B - sum(op[0] == "project" for op in a1.windows["drain"]))
            pe.wait_ge(ld_l1, 16 * 10)
            turn_all_x(a2, 4, hn)
            wide("prologue", 0, 0, 0)
            wide("first", 0, 0)
            with pe.Fori(0, ROUNDS // 2 - 1) as pair:
                for i in (1, 2):
                    wide("steady", pair * 2 + i, i % 2)
            wide("last", ROUNDS - 1, 1)
            wide("drain", ROUNDS, 0, 2 * TB * ROUNDS - sum(op[0] == "project" for op in a2.windows["drain"]))
            for b in range(B):
                pe.wait_ge(xn_all, 5 * NT + TB * b + TB)
                if b >= 2:
                    pe.wait_ge(m5["hT_sb"], DC * (b - 1))
                for c in range(DC):
                    for t in range(TB):
                        ins = nc.tensor.transpose(bank[2 * (b % 2) + c][:, P * t:P * t + P],
                                                  hn[:, TB * b + t, P * c:P * c + P], ident)
                    ins.then_inc(m5["hT_ps"], 1)
            pe.wait_ge(m5["hT_sb"], DC * B)
            for t in range(NT):
                for c in range(DC):
                    ins = nc.tensor.matmul(bank[4][:, E * t:E * t + E], hT5[:, c, P * t:P * t + P], wg_sb[:, c, :],
                                           start=(c == 0), stop=(c == DC - 1))
            ins.then_inc(m5["lg_ps"], 1)
            pe.wait_ge(m5["exp"], 1)
            pe.wait_ge(m5["h_lo"], DC * B)
            pe.sem_inc(m5["y_ps"], 1)

            def product(out, w, h, start, stop):
                for n, (wp, hp) in enumerate(((w[0], h[0]), (w[0], h[1]), (w[1], h[0]))):
                    ins = nc.tensor.matmul(out, wp, hp, start=start and n == 0, stop=stop and n == 2)
                return ins

            with pe.Fori(0, E // 2) as pair:
                for i in range(2 * B + 1):
                    if i < 2 * B:
                        par, b = i // B, i % B
                        if b == 0:
                            pe.wait_ge(m5["w_lo"], pair * 2 + par + 1)
                        for hc in range(2):
                            if i >= 1:
                                pe.wait_ge(m5["glu"], pair * 4 * B + 2 * i + hc - 1)
                            for j in range(2):
                                for c in range(DC):
                                    ins = product(bank[2 * hc + j][:],
                                                  [w[:, par, DC * j + c, P * hc:P * hc + P] for w in (w_hi, w_lo)],
                                                  [h[:, c, S * b:S * b + S] for h in (h_hi, h_lo)], c == 0, c == DC - 1)
                            ins.then_inc(m5["up_ps"], 1)
                    i -= 1
                    if i >= 0:
                        par = i // B
                        pe.wait_ge(m5["a_lo"], pair * 4 * B + 2 * i + 4)
                        pe.wait_ge(m5["acc"], pair * 8 * B + TB * i + 17 - 2 * TB)
                        for t in range(TB):
                            for hc in range(2):
                                ins = product(bank[4 + 2 * (i % 2) + t // 2][:, D * (t % 2):D * (t % 2) + D],
                                              [a[:, i % 2, hc, P * t:P * t + P] for a in (a_hi, a_lo)],
                                              [w[:, par, 2 * DC + hc, :] for w in (w_hi, w_lo)], hc == 0, hc == 1)
                            if t % 2:
                                ins.then_inc(m5["y_ps"], 1)

_INS = ["L0_attn_x", "L0_attn_slope_rate", "L0_attn_W_qkvu", "L0_attn_W_out", "L0_ffn_SU_ug", "L0_ffn_SU_dp",
        "L0_ffn_Wscale_ug", "L0_ffn_Wscale_dp", "L0_ffn_W_up", "L0_ffn_W_gate", "L0_ffn_W_down", "L1_attn_Wq",
        "L1_attn_Wk", "L1_attn_Wv", "L1_attn_Wo", "L1_ffn_ln_w", "L1_ffn_ff_ln_w", "L1_ffn_wq", "L1_ffn_wk",
        "L1_ffn_wv", "L1_ffn_wo", "L1_ffn_wg", "L1_ffn_w1", "L1_ffn_w3", "L1_ffn_w2"]
_OUTS = [((B, S, D), "float32")]


def shape_constants(np):
    f = np.float32
    c = np.zeros((P, NCONST), f)

    def put(name, a):
        lo, hi = CONST_COLS[name]
        c[:, lo:hi] = np.asarray(a, f).reshape(P, hi - lo)

    p, i = np.arange(P)[:, None], np.arange(P)[None, :]
    put("ident", p == i)
    put("lag", np.maximum(i - p, 0))
    put("ge", i >= p)
    put("causal", np.where(i <= p, 0.0, -1e30))
    put("block", p // HD16 == i // HD16)
    put("ramp", np.broadcast_to(i + 1, (P, P)))
    put("left", P - 1 - np.arange(P))
    put("parity", np.stack([(p[:, 0] // HD16) % 2 == 0, (p[:, 0] // HD16) % 2 == 1], 1))
    for name, hd, inv in (
            ("16", HD16, f(1.0) / f(10000.0) ** (np.arange(0, HD16, 2, dtype=f) / f(HD16))),
            ("64", HD64, f(1.0) / f(150000.0) ** (np.arange(HD64 // 2, dtype=f) / f(HD64 // 2)))):
        ang = (np.arange(S, dtype=f)[:, None] * inv.astype(f)[None, :]).astype(f)
        tiles = lambda a: a.reshape(TB, P, hd).transpose(1, 0, 2)
        put("cos" + name, tiles(np.concatenate([np.cos(ang), np.cos(ang)], 1)))
        put("sin" + name, tiles(np.concatenate([-np.sin(ang), np.sin(ang)], 1)))
    return c


def kernel(**inputs):
    import numpy as _np
    import concourse.bacc as _bacc
    from concourse import mybir as _mybir
    from concourse.bass_utils import run_bass_kernel_spmd as _run

    nc = _bacc.Bacc("TRN2", target_bir_lowering=False, num_devices=1)
    arrays, args = {}, []
    for name in _INS + ["consts"]:
        a = _np.ascontiguousarray(shape_constants(_np) if name == "consts" else inputs[name])
        arrays[f"in_{name}_dram"] = a
        args.append(nc.dram_tensor(f"in_{name}_dram", a.shape, _mybir.dt.from_np(a.dtype), kind="ExternalInput").ap())
    for i, (shape, dtype) in enumerate(_OUTS):
        dt = _mybir.dt.from_np(_np.dtype(dtype))
        args.append(nc.dram_tensor(f"out_{i}_dram", shape, dt, kind="ExternalOutput").ap())
    two_layers(nc, *args)
    r = _run(nc, [arrays], core_ids=[0])
    return r.results[0]["out_0_dram"]
```
